# Optimizing a Trainium2 kernel written in Bass

```python
import numpy as np
import jax
import jax.numpy as jnp

def _softmax(x, axis=-1):
    return jax.nn.softmax(x, axis=axis)

def _gelu(x):
    return jax.nn.gelu(x, approximate=True)

def _silu(x):
    return jax.nn.silu(x)

def _sigmoid(x):
    return jax.nn.sigmoid(x)

def _layernorm(x, axis=-1, eps=1e-05):
    m = jnp.mean(x, axis=axis, keepdims=True)
    v = jnp.var(x, axis=axis, keepdims=True)
    return (x - m) / jnp.sqrt(v + eps)

def _scatter_add(tgt, idx, src, axis=0):
    return tgt.at[idx].add(src)

def _segment_sum(src, seg, n):
    return jax.ops.segment_sum(src, seg, n)
kernel_name = 'mk_adaln_ffn_d4_seqx_r8_0c1dc2'

def setup_inputs(seed: int=0):
    np.random.seed(seed)
    _w = jnp.asarray

    def _rec_inputs():
        import jax
        import jax.numpy as jnp
        _rk = jax.random.key(seed)
        x = -0.0003929 + 0.9999 * jax.random.normal(jax.random.fold_in(_rk, 1), (32, 32, 512), jnp.float32)
        _lenS = 32 - jax.random.randint(jax.random.fold_in(_rk, 7), (32,), 0, max(1, 32 // 4) + 1, jnp.int32)
        _lenS2 = 32 - jax.random.randint(jax.random.fold_in(_rk, 8), (32,), 0, max(1, 32 // 4) + 1, jnp.int32)
        itok_B_78_3631 = jax.random.randint(jax.random.fold_in(_rk, 11), (32,), 78, 454, jnp.int32)
        itok_Bx16_0_63 = jax.random.randint(jax.random.fold_in(_rk, 12), (32, 16), 0, 64, jnp.int32)
        itok_B_207_1644 = jax.random.randint(jax.random.fold_in(_rk, 13), (32,), 207, 1645, jnp.int32)
        itok_B_3_7 = jax.random.randint(jax.random.fold_in(_rk, 14), (32,), 3, 8, jnp.int32)
        itok_B_0_4 = jax.random.randint(jax.random.fold_in(_rk, 15), (32,), 0, 5, jnp.int32)
        return (x, itok_B_78_3631, itok_Bx16_0_63, itok_B_207_1644, itok_B_3_7, itok_B_0_4)
    x, itok_B_78_3631, itok_Bx16_0_63, itok_B_207_1644, itok_B_3_7, itok_B_0_4 = _rec_inputs()

    def _L0_cond_setup():
        import math
        import jax, jax.numpy as jnp
        import numpy as np
        B, H, N, L = (16, 32, 64, 512)
        DT_MIN, DT_MAX = (0.001, 0.1)

        def _get_kernel(log_dt, C, log_A_real, A_imag, length):
            dt = jnp.exp(log_dt)
            Cc = C[..., 0] + 1j * C[..., 1]
            A = -jnp.exp(log_A_real) + 1j * A_imag
            dtA = A * dt[:, None]
            Ct = Cc * (jnp.exp(dtA) - 1.0) / A
            P = dtA[:, :, None] * jnp.arange(length, dtype=jnp.float32)
            K = 2.0 * jnp.einsum('hn,hnl->hl', Ct, jnp.exp(P)).real
            return K
        key = jax.random.key(seed)
        ks = jax.random.split(key, 5)
        u = jax.random.normal(ks[0], (B, H, L), dtype=jnp.float32)
        log_dt = jax.random.uniform(ks[1], (H,), dtype=jnp.float32) * (math.log(DT_MAX) - math.log(DT_MIN)) + math.log(DT_MIN)
        C = jax.random.normal(ks[2], (H, N, 2), dtype=jnp.float32)
        log_A_real = jnp.log(0.5 * jnp.ones((H, N), dtype=jnp.float32))
        A_imag = math.pi * jnp.broadcast_to(jnp.arange(N, dtype=jnp.float32), (H, N))
        D = jax.random.normal(ks[3], (H,), dtype=jnp.float32)
        length = jax.random.randint(ks[4], (B,), 1, L + 1, dtype=jnp.int32)
        return {'u': u, 'log_dt': log_dt, 'C': C, 'log_A_real': log_A_real, 'A_imag': A_imag, 'D': D, 'length': length}
    _L0_cond_all = _L0_cond_setup()
    _L0_cond_in = {k: v for k, v in _L0_cond_all.items() if k in ('log_dt', 'C', 'log_A_real', 'A_imag', 'D')}
    del _L0_cond_all

    def _L0_ffn_setup():
        import jax, jax.numpy as jnp
        import numpy as np
        HIDDEN = 512
        INTER = 1376
        SPARSITY = 0.5

        def _ternary_weight(key, out_dim, in_dim, sparsity):
            k_mask, k_sign = jax.random.split(key)
            nonzero = jax.random.bernoulli(k_mask, 1.0 - sparsity, (out_dim, in_dim))
            sign = jnp.where(jax.random.bernoulli(k_sign, 0.5, (out_dim, in_dim)), 1.0, -1.0)
            return (nonzero * sign).astype(jnp.float32)
        key = jax.random.key(seed)
        kx, kg, ku, kd, ksg, ksu, ksd = jax.random.split(key, 7)
        x = jax.random.normal(kx, (4, 256, HIDDEN), dtype=jnp.float32)
        Wg = _ternary_weight(kg, INTER, HIDDEN, SPARSITY)
        Wu = _ternary_weight(ku, INTER, HIDDEN, SPARSITY)
        Wd = _ternary_weight(kd, HIDDEN, INTER, SPARSITY)
        ag = jax.random.uniform(ksg, (INTER,), dtype=jnp.float32, minval=0.5, maxval=1.5) / np.sqrt(HIDDEN)
        au = jax.random.uniform(ksu, (INTER,), dtype=jnp.float32, minval=0.5, maxval=1.5) / np.sqrt(HIDDEN)
        ad = jax.random.uniform(ksd, (HIDDEN,), dtype=jnp.float32, minval=0.5, maxval=1.5) / np.sqrt(INTER)
        return {'x': x, 'Wg': Wg, 'Wu': Wu, 'Wd': Wd, 'ag': ag, 'au': au, 'ad': ad}
    _L0_ffn_all = _L0_ffn_setup()
    _L0_ffn_in = {k: v for k, v in _L0_ffn_all.items() if k in ('Wg', 'Wu', 'Wd', 'ag', 'au', 'ad')}
    del _L0_ffn_all

    def _L1_cond_setup():
        import jax, jax.numpy as jnp
        import numpy as np
        B, S, HID = (4, 128, 512)
        D, HQ, HK = (128, 32, 8)
        PAGES, PSIZE, NPP = (64, 32, 16)
        THETA = 10000.0
        EPS = 1e-06
        SCALE = 1.0 / float(np.sqrt(D))

        def _rmsnorm(t, w):
            var = jnp.mean(t * t, axis=-1, keepdims=True)
            return t * jax.lax.rsqrt(var + EPS) * w

        def _rope(t, pos):
            inv_freq = 1.0 / THETA ** (jnp.arange(0, D, 2, dtype=jnp.float32) / D)
            freqs = pos[..., None].astype(jnp.float32) * inv_freq
            cos = jnp.cos(freqs)[:, :, None, :]
            sin = jnp.sin(freqs)[:, :, None, :]
            t1, t2 = (t[..., :D // 2], t[..., D // 2:])
            return jnp.concatenate([t1 * cos - t2 * sin, t2 * cos + t1 * sin], axis=-1)
        key = jax.random.key(seed)
        ks = jax.random.split(key, 10)
        x = jax.random.normal(ks[0], (B, S, HID), jnp.float32)
        Wq = jax.random.normal(ks[1], (HQ * D, HID), jnp.float32) * 0.02
        Wk = jax.random.normal(ks[2], (HK * D, HID), jnp.float32) * 0.02
        Wv = jax.random.normal(ks[3], (HK * D, HID), jnp.float32) * 0.02
        Wo = jax.random.normal(ks[4], (HID, HQ * D), jnp.float32) * 0.02
        q_norm_w = jax.random.uniform(ks[5], (D,), jnp.float32)
        k_norm_w = jax.random.uniform(ks[6], (D,), jnp.float32)
        k_cache = jax.random.normal(ks[7], (PAGES, PSIZE, HK, D), jnp.float32)
        v_cache = jax.random.normal(ks[8], (PAGES, PSIZE, HK, D), jnp.float32)
        block_table = jnp.arange(B * NPP, dtype=jnp.int32).reshape(B, NPP)
        cache_seqlens = jax.random.randint(ks[9], (B,), 0, 475).astype(jnp.int32)
        return dict(x=x, Wq=Wq, Wk=Wk, Wv=Wv, Wo=Wo, q_norm_w=q_norm_w, k_norm_w=k_norm_w, k_cache=k_cache, v_cache=v_cache, block_table=block_table, cache_seqlens=cache_seqlens)
    _L1_cond_all = _L1_cond_setup()
    _L1_cond_in = {k: v for k, v in _L1_cond_all.items() if k in ('Wq', 'Wk', 'Wv', 'Wo', 'q_norm_w', 'k_norm_w', 'k_cache', 'v_cache')}
    del _L1_cond_all

    def _L1_ffn_setup():
        import jax, jax.numpy as jnp
        import numpy as np
        NUM_EXPERTS = 8
        D_IN = 512
        D_OUT = 512
        key = jax.random.key(seed)
        k_x, k_gw, k_gb, k_ew, k_eb = jax.random.split(key, 5)
        x = jax.random.normal(k_x, (4, 256, D_IN), dtype=jnp.float32)
        gate_w = jax.random.normal(k_gw, (NUM_EXPERTS, D_IN), dtype=jnp.float32) * 0.02
        gate_b = jax.random.normal(k_gb, (NUM_EXPERTS,), dtype=jnp.float32) * 0.02
        expert_w = jax.random.normal(k_ew, (NUM_EXPERTS, D_OUT, D_IN), dtype=jnp.float32) * 0.02
        expert_b = jax.random.normal(k_eb, (NUM_EXPERTS, D_OUT), dtype=jnp.float32) * 0.02
        return {'x': x, 'gate_w': gate_w, 'gate_b': gate_b, 'expert_w': expert_w, 'expert_b': expert_b}
    _L1_ffn_all = _L1_ffn_setup()
    _L1_ffn_in = {k: v for k, v in _L1_ffn_all.items() if k in ('gate_w', 'gate_b', 'expert_w', 'expert_b')}
    del _L1_ffn_all

    def _L2_cond_setup():
        import jax, jax.numpy as jnp
        import numpy as np
        RANK = 16
        ALPHA = 16.0
        SCALING = ALPHA / RANK
        N_ADAPTERS = 8
        IN_F = 512
        OUT_F = 512
        BATCH = 4
        SEQ = 256
        key = jax.random.key(seed)
        kx, ka, kb, ki = jax.random.split(key, 4)
        x = jax.random.normal(kx, (BATCH, SEQ, IN_F), dtype=jnp.float32)
        A = jax.random.normal(ka, (N_ADAPTERS, OUT_F, RANK), dtype=jnp.float32) * 0.02
        B = jax.random.normal(kb, (N_ADAPTERS, RANK, IN_F), dtype=jnp.float32) * 0.02
        adapter_ids = jax.random.randint(ki, (BATCH,), 0, N_ADAPTERS, dtype=jnp.int32)
        return {'x': x, 'A': A, 'B': B, 'adapter_ids': adapter_ids}
    _L2_cond_all = _L2_cond_setup()
    _L2_cond_in = {k: v for k, v in _L2_cond_all.items() if k in ('A', 'B')}
    del _L2_cond_all

    def _L2_ffn_setup():
        import jax, jax.numpy as jnp
        import numpy as np
        B_SZ, S, D_IN, D_OUT = (4, 512, 512, 512)
        E, R = (16, 16)
        key = jax.random.key(seed)
        ks = jax.random.split(key, 6)
        x = jax.random.normal(ks[0], (B_SZ, S, D_IN), dtype=jnp.float32)
        W = jax.random.normal(ks[1], (D_OUT, D_IN), dtype=jnp.float32) * (1.0 / np.sqrt(D_IN))
        b = jax.random.normal(ks[2], (D_OUT,), dtype=jnp.float32) * 0.01
        A = jax.random.normal(ks[3], (E, R, D_IN), dtype=jnp.float32) * (1.0 / np.sqrt(D_IN))
        Bw = jax.random.normal(ks[4], (E, D_OUT, R), dtype=jnp.float32) * (1.0 / np.sqrt(R))
        probs = jax.random.uniform(ks[5], (E,), dtype=jnp.float32)
        probs = probs / jnp.sum(probs)
        return {'x': x, 'W': W, 'b': b, 'A': A, 'B': Bw, 'probs': probs}
    _L2_ffn_all = _L2_ffn_setup()
    _L2_ffn_in = {k: v for k, v in _L2_ffn_all.items() if k in ('W', 'b', 'A', 'B', 'probs')}
    del _L2_ffn_all

    def _L3_cond_setup():
        import jax, jax.numpy as jnp
        import numpy as np
        LORA_SCALING = 16.0 / 32.0
        key = jax.random.key(seed)
        k1, k2, k3, k4, k5 = jax.random.split(key, 5)
        B, S, D, R, L = (4, 256, 512, 32, 5)
        x = jax.random.normal(k1, (B, S, D), dtype=jnp.float32)
        weight = jax.random.normal(k2, (D, D), dtype=jnp.float32) * 0.02
        lora_A = jax.random.normal(k3, (L, D, R), dtype=jnp.float32) * 0.02
        lora_B_w = jax.random.normal(k4, (D, R), dtype=jnp.float32) * 0.02
        labeler_index = jax.random.randint(k5, (B,), 0, L, dtype=jnp.int32)
        return {'x': x, 'weight': weight, 'lora_A': lora_A, 'lora_B_w': lora_B_w, 'labeler_index': labeler_index}
    _L3_cond_all = _L3_cond_setup()
    _L3_cond_in = {k: v for k, v in _L3_cond_all.items() if k in ('weight', 'lora_A', 'lora_B_w')}
    del _L3_cond_all

    def _L3_ffn_setup():
        import jax, jax.numpy as jnp
        import numpy as np
        EPS = 1e-05

        def _bitlinear(x, w):
            scale = jnp.mean(jnp.abs(w))
            q = jnp.round(jnp.clip(w / (scale + EPS), -1.0, 1.0))
            deq = q * scale
            return x @ deq.T
        key = jax.random.key(seed)
        k1, k2, k3, k4 = jax.random.split(key, 4)
        B, S, H, I = (4, 256, 512, 1376)
        return {'hidden_states': jax.random.normal(k1, (B, S, H), dtype=jnp.float32), 'w_gate': jax.random.normal(k2, (I, H), dtype=jnp.float32) * 0.02, 'w_up': jax.random.normal(k3, (I, H), dtype=jnp.float32) * 0.02, 'w_down': jax.random.normal(k4, (H, I), dtype=jnp.float32) * 0.02}
    _L3_ffn_all = _L3_ffn_setup()
    _L3_ffn_in = {k: v for k, v in _L3_ffn_all.items() if k in ('w_gate', 'w_up', 'w_down')}
    del _L3_ffn_all
    return {'x': x, 'itok_B_78_3631': itok_B_78_3631, 'itok_Bx16_0_63': itok_Bx16_0_63, 'itok_B_207_1644': itok_B_207_1644, 'itok_B_3_7': itok_B_3_7, 'itok_B_0_4': itok_B_0_4, 'L0_cond_log_dt': _L0_cond_in['log_dt'], 'L0_cond_C': _L0_cond_in['C'], 'L0_cond_log_A_real': _L0_cond_in['log_A_real'], 'L0_cond_A_imag': _L0_cond_in['A_imag'], 'L0_cond_D': _L0_cond_in['D'], 'L0_ffn_Wg': _L0_ffn_in['Wg'], 'L0_ffn_Wu': _L0_ffn_in['Wu'], 'L0_ffn_Wd': _L0_ffn_in['Wd'], 'L0_ffn_ag': _L0_ffn_in['ag'], 'L0_ffn_au': _L0_ffn_in['au'], 'L0_ffn_ad': _L0_ffn_in['ad'], 'L1_cond_Wq': _L1_cond_in['Wq'], 'L1_cond_Wk': _L1_cond_in['Wk'], 'L1_cond_Wv': _L1_cond_in['Wv'], 'L1_cond_Wo': _L1_cond_in['Wo'], 'L1_cond_q_norm_w': _L1_cond_in['q_norm_w'], 'L1_cond_k_norm_w': _L1_cond_in['k_norm_w'], 'L1_cond_k_cache': _L1_cond_in['k_cache'], 'L1_cond_v_cache': _L1_cond_in['v_cache'], 'L1_ffn_gate_w': _L1_ffn_in['gate_w'], 'L1_ffn_gate_b': _L1_ffn_in['gate_b'], 'L1_ffn_expert_w': _L1_ffn_in['expert_w'], 'L1_ffn_expert_b': _L1_ffn_in['expert_b'], 'L2_cond_A': _L2_cond_in['A'], 'L2_cond_B': _L2_cond_in['B'], 'L2_ffn_W': _L2_ffn_in['W'], 'L2_ffn_b': _L2_ffn_in['b'], 'L2_ffn_A': _L2_ffn_in['A'], 'L2_ffn_B': _L2_ffn_in['B'], 'L2_ffn_probs': _L2_ffn_in['probs'], 'L3_cond_weight': _L3_cond_in['weight'], 'L3_cond_lora_A': _L3_cond_in['lora_A'], 'L3_cond_lora_B_w': _L3_cond_in['lora_B_w'], 'L3_ffn_w_gate': _L3_ffn_in['w_gate'], 'L3_ffn_w_up': _L3_ffn_in['w_up'], 'L3_ffn_w_down': _L3_ffn_in['w_down']}

def reference(x, itok_B_78_3631, itok_Bx16_0_63, itok_B_207_1644, itok_B_3_7, itok_B_0_4, L0_cond_log_dt, L0_cond_C, L0_cond_log_A_real, L0_cond_A_imag, L0_cond_D, L0_ffn_Wg, L0_ffn_Wu, L0_ffn_Wd, L0_ffn_ag, L0_ffn_au, L0_ffn_ad, L1_cond_Wq, L1_cond_Wk, L1_cond_Wv, L1_cond_Wo, L1_cond_q_norm_w, L1_cond_k_norm_w, L1_cond_k_cache, L1_cond_v_cache, L1_ffn_gate_w, L1_ffn_gate_b, L1_ffn_expert_w, L1_ffn_expert_b, L2_cond_A, L2_cond_B, L2_ffn_W, L2_ffn_b, L2_ffn_A, L2_ffn_B, L2_ffn_probs, L3_cond_weight, L3_cond_lora_A, L3_cond_lora_B_w, L3_ffn_w_gate, L3_ffn_w_up, L3_ffn_w_down):
    import jax
    import jax.numpy as jnp

    def _L0_cond_ref(u, log_dt, C, log_A_real, A_imag, D, length):
        import math
        import jax, jax.numpy as jnp
        import numpy as np
        B, H, N, L = (16, 32, 64, 512)
        DT_MIN, DT_MAX = (0.001, 0.1)

        def _get_kernel(log_dt, C, log_A_real, A_imag, length):
            dt = jnp.exp(log_dt)
            Cc = C[..., 0] + 1j * C[..., 1]
            A = -jnp.exp(log_A_real) + 1j * A_imag
            dtA = A * dt[:, None]
            Ct = Cc * (jnp.exp(dtA) - 1.0) / A
            P = dtA[:, :, None] * jnp.arange(length, dtype=jnp.float32)
            K = 2.0 * jnp.einsum('hn,hnl->hl', Ct, jnp.exp(P)).real
            return K
        Bq, Hq, Lq = u.shape
        K = _get_kernel(log_dt, C, log_A_real, A_imag, Lq)
        n = 2 * Lq
        kf = jnp.fft.rfft(K, n=n)
        uf = jnp.fft.rfft(u, n=n)
        y = jnp.fft.irfft(uf * kf[None], n=n)[..., :Lq]
        y = y + u * D[:, None]
        mask = (jnp.arange(Lq)[None, :] < length[:, None]).astype(u.dtype)
        return y * mask[:, None, :]

    def _L0_ffn_ref(x, Wg, Wu, Wd, ag, au, ad):
        import jax, jax.numpy as jnp
        import numpy as np
        HIDDEN = 512
        INTER = 1376
        SPARSITY = 0.5

        def _ternary_weight(key, out_dim, in_dim, sparsity):
            k_mask, k_sign = jax.random.split(key)
            nonzero = jax.random.bernoulli(k_mask, 1.0 - sparsity, (out_dim, in_dim))
            sign = jnp.where(jax.random.bernoulli(k_sign, 0.5, (out_dim, in_dim)), 1.0, -1.0)
            return (nonzero * sign).astype(jnp.float32)
        gate = jnp.einsum('bsh,ih->bsi', x, Wg) * ag
        up = jnp.einsum('bsh,ih->bsi', x, Wu) * au
        h = jax.nn.silu(gate) * up
        out = jnp.einsum('bsi,hi->bsh', h, Wd) * ad
        return out

    def _L1_cond_ref(x, Wq, Wk, Wv, Wo, q_norm_w, k_norm_w, k_cache, v_cache, block_table, cache_seqlens):
        import jax, jax.numpy as jnp
        import numpy as np
        B, S, HID = (4, 128, 512)
        D, HQ, HK = (128, 32, 8)
        PAGES, PSIZE, NPP = (64, 32, 16)
        THETA = 10000.0
        EPS = 1e-06
        SCALE = 1.0 / float(np.sqrt(D))

        def _rmsnorm(t, w):
            var = jnp.mean(t * t, axis=-1, keepdims=True)
            return t * jax.lax.rsqrt(var + EPS) * w

        def _rope(t, pos):
            inv_freq = 1.0 / THETA ** (jnp.arange(0, D, 2, dtype=jnp.float32) / D)
            freqs = pos[..., None].astype(jnp.float32) * inv_freq
            cos = jnp.cos(freqs)[:, :, None, :]
            sin = jnp.sin(freqs)[:, :, None, :]
            t1, t2 = (t[..., :D // 2], t[..., D // 2:])
            return jnp.concatenate([t1 * cos - t2 * sin, t2 * cos + t1 * sin], axis=-1)
        bsz, seqlen, _ = x.shape
        q = jnp.einsum('bsd,ed->bse', x, Wq).reshape(bsz, seqlen, HQ, D)
        k = jnp.einsum('bsd,ed->bse', x, Wk).reshape(bsz, seqlen, HK, D)
        v = jnp.einsum('bsd,ed->bse', x, Wv).reshape(bsz, seqlen, HK, D)
        q = _rmsnorm(q, q_norm_w)
        k = _rmsnorm(k, k_norm_w)
        pos = cache_seqlens[:, None] + jnp.arange(seqlen)[None, :]
        q = _rope(q, pos)
        k = _rope(k, pos)
        L = NPP * PSIZE
        kc = k_cache[block_table].reshape(bsz, L, HK, D)
        vc = v_cache[block_table].reshape(bsz, L, HK, D)
        k_all = jnp.concatenate([kc, k], axis=1)
        v_all = jnp.concatenate([vc, v], axis=1)
        valid_c = jnp.arange(L)[None, :] < cache_seqlens[:, None]
        valid = jnp.concatenate([valid_c, jnp.ones((bsz, seqlen), dtype=bool)], axis=1)
        rep = HQ // HK
        k_all = jnp.repeat(k_all, rep, axis=2)
        v_all = jnp.repeat(v_all, rep, axis=2)
        scores = jnp.einsum('bqhd,bkhd->bhqk', q, k_all) * SCALE
        scores = jnp.where(valid[:, None, None, :], scores, -1e+30)
        probs = jax.nn.softmax(scores, axis=-1)
        o = jnp.einsum('bhqk,bkhd->bqhd', probs, v_all)
        o = o.reshape(bsz, seqlen, HQ * D)
        return jnp.einsum('bse,de->bsd', o, Wo)

    def _L1_ffn_ref(x, gate_w, gate_b, expert_w, expert_b):
        import jax, jax.numpy as jnp
        import numpy as np
        NUM_EXPERTS = 8
        D_IN = 512
        D_OUT = 512
        orig_shape = x.shape
        xf = x.reshape(-1, x.shape[-1])
        gate_logits = xf @ gate_w.T + gate_b
        gates = jax.nn.softmax(gate_logits, axis=-1)
        selected = jnp.argmax(gates, axis=-1)
        out = jnp.zeros((xf.shape[0], expert_w.shape[1]), dtype=xf.dtype)
        for j in range(expert_w.shape[0]):
            yj = xf @ expert_w[j].T + expert_b[j]
            out = out + jnp.where((selected == j)[:, None], yj, 0.0)
        return out.reshape(*orig_shape[:-1], expert_w.shape[1])

    def _L2_cond_ref(x, A, B, adapter_ids):
        import jax, jax.numpy as jnp
        import numpy as np
        RANK = 16
        ALPHA = 16.0
        SCALING = ALPHA / RANK
        N_ADAPTERS = 8
        IN_F = 512
        OUT_F = 512
        BATCH = 4
        SEQ = 256
        B_sel = B[adapter_ids]
        A_sel = A[adapter_ids]
        Bx = jnp.einsum('bni,bri->bnr', x, B_sel)
        out = jnp.einsum('bnr,bor->bno', Bx, A_sel)
        return out * SCALING

    def _L2_ffn_ref(x, W, b, A, B, probs):
        import jax, jax.numpy as jnp
        import numpy as np
        B_SZ, S, D_IN, D_OUT = (4, 512, 512, 512)
        E, R = (16, 16)
        out = jnp.einsum('bsd,od->bso', x, W) + b
        h = jnp.einsum('bsd,erd->bser', x, A)
        contrib = jnp.einsum('bser,e,eor->bso', h, probs, B)
        return out + contrib

    def _L3_cond_ref(x, weight, lora_A, lora_B_w, labeler_index):
        import jax, jax.numpy as jnp
        import numpy as np
        LORA_SCALING = 16.0 / 32.0
        result = jnp.einsum('bsd,od->bso', x, weight)
        labelers_A = lora_A[labeler_index]
        low = jnp.einsum('bsd,bdr->bsr', x, labelers_A)
        result = result + jnp.einsum('bsr,or->bso', low, lora_B_w) * LORA_SCALING
        return result

    def _L3_ffn_ref(hidden_states, w_gate, w_up, w_down):
        import jax, jax.numpy as jnp
        import numpy as np
        EPS = 1e-05

        def _bitlinear(x, w):
            scale = jnp.mean(jnp.abs(w))
            q = jnp.round(jnp.clip(w / (scale + EPS), -1.0, 1.0))
            deq = q * scale
            return x @ deq.T
        gate = _bitlinear(hidden_states, w_gate)
        up = _bitlinear(hidden_states, w_up)
        inter = gate * up
        out = _bitlinear(inter, w_down)
        return out
    x = x + _L0_ffn_ref(_L0_cond_ref(x, L0_cond_log_dt, L0_cond_C, L0_cond_log_A_real, L0_cond_A_imag, L0_cond_D, itok_B_78_3631), L0_ffn_Wg, L0_ffn_Wu, L0_ffn_Wd, L0_ffn_ag, L0_ffn_au, L0_ffn_ad)
    x = x + _L1_ffn_ref(_L1_cond_ref(x, L1_cond_Wq, L1_cond_Wk, L1_cond_Wv, L1_cond_Wo, L1_cond_q_norm_w, L1_cond_k_norm_w, L1_cond_k_cache, L1_cond_v_cache, itok_Bx16_0_63, itok_B_207_1644), L1_ffn_gate_w, L1_ffn_gate_b, L1_ffn_expert_w, L1_ffn_expert_b)
    x = x + _L2_ffn_ref(_L2_cond_ref(x, L2_cond_A, L2_cond_B, itok_B_3_7), L2_ffn_W, L2_ffn_b, L2_ffn_A, L2_ffn_B, L2_ffn_probs)
    x = x + _L3_ffn_ref(_L3_cond_ref(x, L3_cond_weight, L3_cond_lora_A, L3_cond_lora_B_w, itok_B_0_4), L3_ffn_w_gate, L3_ffn_w_up, L3_ffn_w_down)
    return x

_drawn_inputs = setup_inputs


def setup_inputs(seed=0):
    import zlib

    import numpy as np

    out = dict(_drawn_inputs(seed))
    spreads = {'L0_cond_log_A_real': (-0.6931471824645996, 0.2)}
    factors = {'L1_cond_Wk': 8.0,
     'L1_cond_Wv': 4.905,
     'L1_cond_q_norm_w': 2.857,
     'L1_cond_k_norm_w': 8.0,
     'L1_ffn_expert_b': 3.241,
     'L2_ffn_b': 20.677,
     'L2_ffn_A': 5.781,
     'L2_ffn_B': 5.709,
     'L2_ffn_probs': 8.0,
     'L3_cond_weight': 4.131,
     'L3_cond_lora_A': 8.0,
     'L3_cond_lora_B_w': 8.0,
     'L3_ffn_w_gate': 3.591,
     'L3_ffn_w_up': 3.6,
     'L3_ffn_w_down': 3.608,
     'L2_ffn_W': 3.096}
    for name, (base, spread) in spreads.items():
        noise = np.random.default_rng([zlib.crc32(name.encode()), seed]).standard_normal(out[name].shape)
        drawn = base * np.exp(spread * noise) if base else spread * noise
        out[name] = jnp.asarray(drawn.astype(out[name].dtype))
    for name, factor in factors.items():
        out[name] = (out[name] * factor).astype(out[name].dtype)
    return out
```

```python
from contextlib import ExitStack

import numpy as np

import concourse.bass as bass
from concourse import mybir

F32 = mybir.dt.float32
F32R = mybir.dt.float32r
I32 = mybir.dt.int32
ALU = mybir.AluOpType
ACT = mybir.ActivationFunctionType
AX_X = mybir.AxisListType.X

P = 128
B, S, H = 32, 32, 512
TOK = B * S
HALF = TOK // 2
KT = H // P
INTER = 1376
IT = -(-INTER // P)
N_STATE = 64
LO_N, HI_N = 32, H // 32
D = 128
HQ, HK = 32, 8
REP = HQ // HK
PAGES, PSIZE, NPP = 64, 32, 16
CACHE = NPP * PSIZE
KEYS = CACHE + S
VCH = CACHE // P
GROUPS = (HQ + HK) // REP
TT = TOK // P
BPT = P // S
EXPERTS = 8
ADAPTERS, RANK2 = 8, 16
LABELS, RANK3 = 5, 32
LABEL_PAD = 8
THETA = 10000.0
RMS_EPS = 1e-6
BIT_EPS = 1e-5
ATT_SCALE = 1.0 / float(np.sqrt(D))
NEG = -1e30
KPAD = P + H

TWO_PI = 2.0 * np.pi
MAGIC = 1.5 * 2.0 ** 23
PI_1 = 6.28125
PI_2 = float(np.round((TWO_PI - PI_1) * 2.0 ** 20) / 2.0 ** 20)
PI_3 = float(TWO_PI - PI_1 - PI_2)
PI_SAFE = 3.1415925
LN2_1, LN2_2 = 0.693359375, -2.12194440e-4


def run_steps(eng, n, unroll, step):
    for u in range(min(unroll, n)):
        step(u, u, 0)
    whole = n // unroll
    if whole > 2:
        with eng.Fori(1, whole) as i:
            for u in range(unroll):
                step(i * unroll + u, u, i)
    else:
        for i in range(1, whole):
            for u in range(unroll):
                step(i * unroll + u, u, i)
    for t in range(max(whole, 1) * unroll, n):
        step(t, t % unroll, t // unroll)


def at(i, n=1):
    return bass.ds(i, n)


def f32(ap):
    return ap.bitcast(F32)


class Core:
    used = []

    def __init__(self, nc, ctx):
        self.nc, self.ctx = nc, ctx

    def sb(self, name, shape, dt=F32):
        return self.ctx.enter_context(self.nc.sbuf_tensor(name, shape, dt))

    def ps(self, name, shape):
        return self.ctx.enter_context(self.nc.psum_tensor(name, shape, F32))

    def sem(self, name):
        handle = self.ctx.enter_context(self.nc.semaphore(name))
        self.used.append(handle.num)
        return handle


def three_passes(nc, out, w_hi, w_lo, x_hi, x_lo, start, stop):
    nc.tensor.matmul(out, w_hi, x_hi, start=start, stop=False)
    nc.tensor.matmul(out, w_hi, x_lo, start=False, stop=False)
    return nc.tensor.matmul(out, w_lo, x_hi, start=False, stop=stop)


def setup_phase(nc, d, g):
    with ExitStack() as ctx:
        c = Core(nc, ctx)
        la2, ai2, ldt, cre, cim = (c.sb(f"s_{n}", [P, S]) for n in ("la", "ai", "ldt", "cre", "cim"))
        sgn = c.sb("s_sgn", [P, 4])
        bits = c.sb("s_bits", [P, S], I32)
        posn = c.sb("s_posn", [P, LO_N + HI_N])
        tmp = [c.sb(f"s_t{n}", [P, S]) for n in range(16)]
        LN = LO_N + HI_N
        mag = c.sb("s_mag", [P, S, LN])
        ang = c.sb("s_ang", [P, S, LN])
        angc = c.sb("s_angc", [P, S, LN])
        kk = c.sb("s_kk", [P, S, LN])
        kk2 = c.sb("s_kk2", [P, S, LN])
        low = c.sb("s_low", [P, S, LO_N])
        gco = c.sb("s_gco", [P, S, HI_N])
        gtm = c.sb("s_gtm", [P, S, HI_N])
        ks = c.sb("s_ks", [HI_N, S, LO_N])
        d16 = c.sb("s_d16", [1, S])
        zer = c.sb("s_zer", [S, P])
        wst = [c.sb(f"s_wst{n}", [P, 2 * KT * P]) for n in range(2)]
        wab = c.sb("s_wab", [P, 2 * KT * P])
        rows = c.sb("s_rows", [P, 3 * IT])
        tot = c.sb("s_tot", [P, 3])
        ones = c.sb("s_ones", [P, P])
        ints = c.sb("s_ints", [P, 4, B], I32)
        posi = c.sb("s_posi", [P, TT], I32)
        posf, spos = c.sb("s_posf", [P, TT]), c.sb("s_spos", [P, TT])
        invf = c.sb("s_invf", [P, D // 2])
        nw = c.sb("s_nw", [P, 2, D])
        fr = c.sb("s_fr", [P, 2, TT, D // 2])
        fk = c.sb("s_fk", [P, 2, TT, D // 2])
        fk2 = c.sb("s_fk2", [P, 2, TT, D // 2])
        pk = c.ps("s_pk", [HI_N, S, LO_N])
        pt = c.ps("s_pt", [P, 4])

        in_k, in_m, zero_in = c.sem("setup_kernel_in"), c.sem("setup_masks_in"), c.sem("setup_zeros")
        w_in = [c.sem(f"setup_w_in{n}") for n in range(2)]
        w_summed = c.sem("setup_w_summed")
        link, act_done, pe_done = c.sem("setup_dve_chain"), c.sem("setup_act_done"), c.sem("setup_pe_done")
        dve_ready, k_out, res_in = c.sem("setup_dve_ready"), c.sem("setup_k_out"), c.sem("setup_resid_in")

        with nc.Block() as block:
            @block.sync
            def _(sp):
                for dst, src in ((la2, "logA2"), (ai2, "Aim2"), (cre, "Cre2"), (cim, "Cim2")):
                    sp.dma_start(dst[:], d[src]).then_inc(in_k, 16)
                sp.dma_start(sgn[:], d["signs"]).then_inc(in_k, 16)
                sp.dma_start(posn[:], d["positions"]).then_inc(in_k, 16)
                sp.dma_start(ldt[:], d["L0_cond_log_dt"].rearrange("(a s) -> a s", a=1).to_broadcast([P, S])).then_inc(in_k, 16)
                sp.dma_start(d16[:], d["L0_cond_D"].rearrange("(a s) -> a s", a=1)).then_inc(in_k, 16)
                sp.dma_start(posi[:], d["posbase"]).then_inc(in_m, 16)
                sp.dma_start(spos[:], d["seqpos"]).then_inc(in_m, 16)
                sp.dma_start(invf[:], d["inv_freq"]).then_inc(in_m, 16)
                for n, src in enumerate(("itok_B_78_3631", "itok_B_207_1644", "itok_B_3_7", "itok_B_0_4")):
                    sp.dma_start(ints[:, n, :], d[src].rearrange("(a s) -> a s", a=1).to_broadcast([P, B])).then_inc(in_m, 16)
                for n, src in enumerate(("L1_cond_q_norm_w", "L1_cond_k_norm_w")):
                    sp.dma_start(nw[:, n, :], d[src].rearrange("(a s) -> a s", a=1).to_broadcast([P, D])).then_inc(in_m, 16)
                for dst, src in ((g["ident"], "ident"), (g["cols"], "cols"), (g["keyidx"], "keyidx")):
                    sp.dma_start(dst[:], d[src]).then_inc(in_m, 16)
                sp.dma_start(g["resid"][:], d["xT"]).then_inc(res_in, 16)
                for t in range(IT + IT // 2 + 1):
                    if t >= 2:
                        sp.wait_ge(w_summed, t - 1)
                    if t < IT:
                        src, n = d["w3_gu"][t], 2 * KT * P
                    elif t < IT + IT // 2:
                        u = 2 * (t - IT)
                        src, n = d["w3_d"][u:u + 2].rearrange("t p m -> p t m"), 2 * H
                    else:
                        src, n = d["w3_d"][IT - 1], H
                    dst = wst[t % 2][:, 0:n]
                    if t >= IT and n == 2 * H:
                        dst = dst.rearrange("p (t m) -> p t m", t=2)
                    sp.dma_start(dst, src).then_inc(w_in[t % 2], 16)
                sp.wait_ge(zero_in, 1)
                sp.dma_start(g["kpad"][:, 0:P], zer[:]).then_inc(k_out, 16)
                sp.wait_ge(dve_ready, 3)
                sp.dma_start(g["kpad"][:, P:KPAD].rearrange("s (a c) -> a s c", c=LO_N), ks[:]).then_inc(k_out, 16)
                sp.wait_ge(k_out, 32)
                sp.wait_ge(res_in, 16)

            @block.gpsimd
            def _(pool):
                nc.gpsimd.memset(zer[:], 0.0).then_inc(zero_in, 1)

            @block.scalar
            def _(act):
                act.wait_ge(dve_ready, 1)
                nc.scalar.activation(mag[:], mag[:], ACT.Exp).then_inc(act_done, 1)
                nc.scalar.activation(kk[:], ang[:], ACT.Sin)
                nc.scalar.activation(kk2[:], angc[:], ACT.Sin)
                nc.scalar.activation(tmp[7][:], tmp[5][:], ACT.Sin)
                nc.scalar.activation(tmp[8][:], tmp[6][:], ACT.Sin).then_inc(act_done, 1)
                act.wait_ge(dve_ready, 4)
                nc.scalar.activation(fk[:], fr[:], ACT.Sin).then_inc(act_done, 1)
                for t in range(IT + IT // 2 + 1):
                    act.wait_ge(w_in[t % 2], 16 * (t // 2 + 1))
                    if t >= 1:
                        act.wait_ge(w_summed, t)
                    if t < IT:
                        nc.scalar.activation(wab[:, 0:H], wst[t % 2][:, 0:H], ACT.Abs, accum_out=rows[:, t:t + 1])
                        last = nc.scalar.activation(wab[:, H:2 * H], wst[t % 2][:, H:2 * H], ACT.Abs, accum_out=rows[:, IT + t:IT + t + 1])
                    else:
                        n = 2 * H if t < IT + IT // 2 else H
                        last = nc.scalar.activation(wab[:, 0:n], wst[t % 2][:, 0:n], ACT.Abs, accum_out=rows[:, 2 * IT + t - IT:2 * IT + t - IT + 1])
                    last.then_inc(w_summed, 1)

            @block.vector
            def _(dve):
                count = [0]

                def chain(ins):
                    count[0] += 1
                    ins.then_inc(link, 1)
                    dve.wait_ge(link, count[0])

                def tt(out, a, b_, op):
                    chain(nc.vector.tensor_tensor(out, a, b_, op))

                def tsc(out, a, s1, s2, op0, op1):
                    chain(nc.vector.tensor_scalar(out, a, s1, s2, op0, op1))

                def reduce_angle(x, k):
                    tsc(k, x, 1.0 / TWO_PI, MAGIC, ALU.mult, ALU.add)
                    tsc(k, k, -MAGIC, 0.0, ALU.add, ALU.add)
                    for part in (PI_1, PI_2, PI_3):
                        chain(nc.vector.scalar_tensor_tensor(x, k, -part, x, ALU.mult, ALU.add))
                    tsc(x, x, PI_SAFE, -PI_SAFE, ALU.min, ALU.max)

                dt, nre, dre, dim = tmp[0], tmp[1], tmp[2], tmp[3]
                def exact_exp(out, x, k, r, bits):
                    tsc(r, x, -87.0, 88.0, ALU.max, ALU.min)
                    tsc(k, r, 1.0 / np.log(2.0), MAGIC, ALU.mult, ALU.add)
                    tsc(k, k, -MAGIC, 0.0, ALU.add, ALU.add)
                    for part in (LN2_1, LN2_2):
                        chain(nc.vector.scalar_tensor_tensor(r, k, -part, r, ALU.mult, ALU.add))
                    tsc(bits, k, 127.0, 2.0 ** 23, ALU.add, ALU.mult)
                    tsc(k, r, 1.0 / 5040, 1.0 / 720, ALU.mult, ALU.add)
                    for coef in (1.0 / 120, 1.0 / 24, 1.0 / 6, 0.5, 1.0, 1.0):
                        tt(k, k, r, ALU.mult)
                        tsc(k, k, coef, 0.0, ALU.add, ALU.add)
                    tt(out, k, bits.bitcast(F32), ALU.mult)

                dve.wait_ge(in_k, 16 * 8)
                exact_exp(dt[:], ldt[:], tmp[9][:], tmp[10][:], bits[:])
                exact_exp(nre[:], la2[:], tmp[9][:], tmp[10][:], bits[:])
                chain(nc.vector.scalar_tensor_tensor(dre[:], nre[:], -1.0, dt[:], ALU.mult, ALU.mult))
                tt(dim[:], ai2[:], dt[:], ALU.mult)
                exact_exp(tmp[4][:], dre[:], tmp[9][:], tmp[10][:], bits[:])
                chain(nc.vector.tensor_copy(tmp[5][:], dim[:]))
                tsc(tmp[6][:], dim[:], np.pi / 2, 0.0, ALU.add, ALU.add)
                reduce_angle(tmp[5][:], tmp[9][:])
                reduce_angle(tmp[6][:], tmp[9][:])
                pb = posn[:].rearrange("p (o n) -> p o n", o=1).to_broadcast([P, S, LN])
                tt(mag[:], dre[:].rearrange("p (s o) -> p s o", o=1).to_broadcast([P, S, LN]), pb, ALU.mult)
                tt(ang[:], dim[:].rearrange("p (s o) -> p s o", o=1).to_broadcast([P, S, LN]), pb, ALU.mult)
                reduce_angle(ang[:], kk[:])
                tsc(angc[:], ang[:], np.pi / 2, 0.0, ALU.add, ALU.add)
                reduce_angle(angc[:], kk[:])
                chain(nc.vector.memset(rows[:], 0.0))
                nc.vector.memset(ones[:], 1.0).then_inc(dve_ready, 1)
                dve.wait_ge(act_done, 2)
                sin_, cos_, e = tmp[7], tmp[8], tmp[4]
                nr, ni, q, den, cr, ci, al, be = (tmp[n] for n in (9, 10, 11, 12, 13, 14, 15, 5))
                tt(nr[:], e[:], cos_[:], ALU.mult)
                tsc(nr[:], nr[:], -1.0, 0.0, ALU.add, ALU.add)
                tt(ni[:], e[:], sin_[:], ALU.mult)
                tt(den[:], nre[:], nre[:], ALU.mult)
                tt(q[:], ai2[:], ai2[:], ALU.mult)
                tt(den[:], den[:], q[:], ALU.add)
                chain(nc.vector.reciprocal(den[:], den[:]))
                tt(cr[:], ni[:], ai2[:], ALU.mult)
                tt(q[:], nr[:], nre[:], ALU.mult)
                tt(cr[:], cr[:], q[:], ALU.subtract)
                tt(cr[:], cr[:], den[:], ALU.mult)
                tt(ci[:], ni[:], nre[:], ALU.mult)
                tt(q[:], nr[:], ai2[:], ALU.mult)
                tt(ci[:], ci[:], q[:], ALU.add)
                tt(ci[:], ci[:], den[:], ALU.mult)
                tsc(ci[:], ci[:], -1.0, 0.0, ALU.mult, ALU.add)
                tt(nr[:], cre[:], cr[:], ALU.mult)
                tt(q[:], cim[:], ci[:], ALU.mult)
                tt(nr[:], nr[:], q[:], ALU.subtract)
                tt(ni[:], cre[:], ci[:], ALU.mult)
                tt(q[:], cim[:], cr[:], ALU.mult)
                tt(ni[:], ni[:], q[:], ALU.add)
                tsc(al[:], nr[:], sgn[:, 0:1], None, ALU.mult, ALU.bypass)
                chain(nc.vector.scalar_tensor_tensor(al[:], ni[:], sgn[:, 1:2], al[:], ALU.mult, ALU.add))
                tsc(be[:], ni[:], sgn[:, 2:3], None, ALU.mult, ALU.bypass)
                chain(nc.vector.scalar_tensor_tensor(be[:], nr[:], sgn[:, 3:4], be[:], ALU.mult, ALU.add))
                hi_c, hi_s, hi_m = kk2[:, :, LO_N:], kk[:, :, LO_N:], mag[:, :, LO_N:]
                wide = [P, S, HI_N]
                tt(gco[:], hi_c, al[:].rearrange("p (s o) -> p s o", o=1).to_broadcast(wide), ALU.mult)
                tt(gtm[:], hi_s, be[:].rearrange("p (s o) -> p s o", o=1).to_broadcast(wide), ALU.mult)
                tt(gco[:], gco[:], gtm[:], ALU.add)
                tt(gco[:], gco[:], hi_m, ALU.mult)
                hp = P // 2
                tt(low[0:hp], kk2[0:hp, :, 0:LO_N], mag[0:hp, :, 0:LO_N], ALU.mult)
                chain(nc.vector.tensor_tensor(low[hp:P], kk[hp:P, :, 0:LO_N], mag[hp:P, :, 0:LO_N], ALU.mult))
                dve.sem_inc(dve_ready, 1)
                dve.wait_ge(pe_done, 1)
                chain(nc.vector.tensor_copy(ks[:], pk[:]))
                nc.vector.tensor_tensor(ks[0:1, :, 0], ks[0:1, :, 0], d16[:], ALU.add).then_inc(dve_ready, 1)
                dve.wait_ge(in_m, 16 * 12)
                chain(nc.vector.tensor_copy(posf[:], posi[:]))
                tt(posf[:], posf[:], spos[:], ALU.add)
                fw = [P, TT, D // 2]
                tt(fr[:, 0], posf[:].rearrange("p (t o) -> p t o", o=1).to_broadcast(fw),
                   invf[:].rearrange("p (o n) -> p o n", o=1).to_broadcast(fw), ALU.mult)
                reduce_angle(fr[:, 0], fk2[:, 0])
                tsc(fr[:, 1], fr[:, 0], np.pi / 2, 0.0, ALU.add, ALU.add)
                reduce_angle(fr[:, 1], fk2[:, 1])
                dve.sem_inc(dve_ready, 1)
                chain(nc.vector.tensor_copy(g["lens"][:], ints[:]))
                for m in range(KT):
                    tsc(g["lmask"][:, m, :], g["lens"][:, 0, :], g["cols"][:, m:m + 1], None, ALU.is_gt, ALU.bypass)
                tsc(g["amask"][:], g["lens"][:, 2, :], g["cols"][:, 4:5], None, ALU.is_equal, ALU.bypass)
                for m in range(2):
                    tsc(g["bmask"][:, m, :], g["lens"][:, 3, :], g["cols"][:, 5 + m:6 + m], 0.5, ALU.is_equal, ALU.mult)
                dve.wait_ge(act_done, 3)
                hd = D // 2
                for n in range(2):
                    for half in range(2):
                        w = nw[:, n, half * hd:(half + 1) * hd].rearrange("p (o n) -> p o n", o=1).to_broadcast(fw)
                        tt(g["rope_c"][:, n, :, half * hd:(half + 1) * hd], fk[:, 1], w, ALU.mult)
                        other = 1 - half
                        tt(g["rope_s"][:, n, :, other * hd:(other + 1) * hd], fk[:, 0], w, ALU.mult)
                    tsc(g["rope_s"][:, n, :, 0:hd], g["rope_s"][:, n, :, 0:hd], -1.0, 0.0, ALU.mult, ALU.add)
                dve.wait_ge(w_summed, IT + IT // 2 + 1)
                for n in range(3):
                    chain(nc.vector.reduce_sum(tot[:, n:n + 1], rows[:, n * IT:(n + 1) * IT], AX_X))
                dve.sem_inc(dve_ready, 1)
                dve.wait_ge(pe_done, 2)
                tsc(g["scale3"][:], pt[:, 0:3], 1.0 / (INTER * H), None, ALU.mult, ALU.bypass)
                tsc(g["thr3"][:, 0:3], g["scale3"][:], BIT_EPS, 0.5, ALU.add, ALU.mult)
                tsc(g["thr3"][:, 3:6], g["thr3"][:, 0:3], -1.0, 0.0, ALU.mult, ALU.add)

            @block.tensor
            def _(pe):
                pe.wait_ge(dve_ready, 2)
                for s in range(S):
                    last = nc.tensor.matmul(pk[:, s, :], gco[:, s, :], low[:, s, :], start=True, stop=True)
                last.then_inc(pe_done, 1)
                pe.wait_ge(dve_ready, 5)
                nc.tensor.matmul(pt[:, 0:3], ones[:], tot[:], start=True, stop=True).then_inc(pe_done, 1)


def conv_phase(nc, d, g):
    SG = 4
    steps = S // SG
    xh, xl = g["xh"], g["xl"]
    with ExitStack() as ctx:
        c = Core(nc, ctx)
        xr = c.sb("c_xr", [P, S, KT, B])
        rh, rl = c.sb("c_rh", [P, S, KT, B], F32R), c.sb("c_rl", [P, S, KT, B], F32R)
        tz = [c.sb(f"c_tz{n}", [P, SG, H]) for n in range(2)]
        th = [c.sb(f"c_th{n}", [P, SG, H], F32R) for n in range(2)]
        tl = [c.sb(f"c_tl{n}", [P, SG, H], F32R) for n in range(2)]
        y = [c.sb(f"c_y{n}", [P, SG, KT, B]) for n in range(2)]
        acc = [c.ps(f"c_acc{n}", [P, SG, KT, B]) for n in range(2)]
        x_in, x_hi, x_lo = c.sem("conv_x_in"), c.sem("conv_x_hi"), c.sem("conv_x_lo")
        t_in = [c.sem(f"conv_t_in{n}") for n in range(2)]
        t_hi, t_lo, done, masked, split = (c.sem(f"conv_{n}") for n in ("t_hi", "t_lo", "done", "masked", "split"))
        with nc.Block() as block:
            @block.sync
            def _(sp):
                sp.dma_start(xr[:], d["x_rev"]).then_inc(x_in, 16)
                for t in range(steps):
                    if t >= 2:
                        sp.wait_ge(t_lo, t - 1)
                        sp.wait_ge(split, t - 1)
                    win = bass.AP(tensor=g["kpad"].tensor, offset=g["kpad"].offset + t * SG * KPAD + 1,
                                  ap=[[1, P], [KPAD, SG], [1, H]])
                    sp.dma_start(tz[t % 2][:], win).then_inc(t_in[t % 2], 16)

            @block.scalar
            def _(act):
                act.wait_ge(x_in, 16)
                nc.scalar.activation(rh[:], xr[:], ACT.Copy).then_inc(x_hi, 1)
                for t in range(steps):
                    act.wait_ge(t_in[t % 2], 16 * (t // 2 + 1))
                    if t >= 2:
                        act.wait_ge(done, t - 1)
                    nc.scalar.activation(th[t % 2][:], tz[t % 2][:], ACT.Copy).then_inc(t_hi, 1)

            @block.gpsimd
            def _(pool):
                for t in range(steps):
                    pool.wait_ge(t_hi, t + 1)
                    nc.gpsimd.tensor_tensor(tl[t % 2][:, 0:2], tz[t % 2][:, 0:2], f32(th[t % 2][:, 0:2]), ALU.subtract).then_inc(t_lo, 1)

            @block.vector
            def _(dve):
                dve.wait_ge(x_hi, 1)
                nc.vector.tensor_tensor(rl[:], xr[:], f32(rh[:]), ALU.subtract).then_inc(x_lo, 1)
                mask = g["lmask"][:].rearrange("p (o m) b -> p o m b", o=1).to_broadcast([P, SG, KT, B])

                def low_half(t):
                    dve.wait_ge(t_hi, t + 1)
                    nc.vector.tensor_tensor(tl[t % 2][:, 2:4], tz[t % 2][:, 2:4], f32(th[t % 2][:, 2:4]), ALU.subtract).then_inc(split, 1)

                low_half(0)
                for t in range(steps):
                    if t + 1 < steps:
                        low_half(t + 1)
                    dve.wait_ge(done, t + 1)
                    yo = y[t % 2]
                    nc.vector.tensor_tensor(yo[:], acc[t % 2][:], mask, ALU.mult).then_inc(masked, 1)
                    dve.wait_ge(masked, 3 * t + 1)
                    ys = yo[:].rearrange("p s m b -> p m s b")
                    hi = xh[:, :, t * SG * B:(t + 1) * SG * B].rearrange("p m (s b) -> p m s b", b=B)
                    lo = xl[:, :, t * SG * B:(t + 1) * SG * B].rearrange("p m (s b) -> p m s b", b=B)
                    nc.vector.tensor_copy(hi, ys).then_inc(masked, 1)
                    dve.wait_ge(masked, 3 * t + 2)
                    nc.vector.tensor_tensor(lo, ys, f32(hi), ALU.subtract).then_inc(masked, 1)

            @block.tensor
            def _(pe):
                pe.wait_ge(x_lo, 1)
                for t in range(steps):
                    pe.wait_ge(t_lo, t + 1)
                    pe.wait_ge(split, t + 1)
                    if t >= 2:
                        pe.wait_ge(masked, 3 * (t - 2) + 1)
                    for s in range(SG):
                        for dd in range(KT):
                            n = KT - dd
                            out = acc[t % 2][:, s, dd:KT, :]
                            w_hi, w_lo = (m[t % 2][:, s, dd * P:(dd + 1) * P] for m in (th, tl))
                            x_h, x_l = (m[:, t * SG + s, 0:n, :] for m in (rh, rl))
                            last = three_passes(nc, out, w_hi, w_lo, x_h, x_l, dd == 0, dd == KT - 1)
                    last.then_inc(done, 1)


def gate_up_phase(nc, d, g, hh, hl, tag, w_dram, ternary, func, gate_scale, up_scale):
    xh, xl = g["xh"], g["xl"]
    W = KT * P
    with ExitStack() as ctx:
        c = Core(nc, ctx)
        raw = [c.sb(f"{tag}_raw{n}", [P, 2 * W]) for n in range(2)]
        wh = [c.sb(f"{tag}_wh{n}", [P, 2 * W], F32R) for n in range(2)]
        wl = None if ternary else [c.sb(f"{tag}_wl{n}", [P, 2 * W], F32R) for n in range(2)]
        sgn = c.sb(f"{tag}_sgn", [P, 2 * W]) if ternary else None
        sg = [c.sb(f"{tag}_sg{n}", [P, TOK]) for n in range(2)]
        hf = c.sb(f"{tag}_hf", [P, TOK])
        acc = [c.ps(f"{tag}_acc{n}", [P, 2, TOK]) for n in range(2)]
        w_in = [c.sem(f"{tag}_w_in{n}") for n in range(2)]
        w_hi, w_ready, done, gated, h_full, h_done = (
            c.sem(f"{tag}_{n}") for n in ("w_hi", "w_ready", "done", "gated", "h_full", "h_done"))
        with nc.Block() as block:
            @block.sync
            def _(sp):
                def load(t, u, i):
                    if not (isinstance(t, int) and t < 2):
                        sp.wait_ge(w_ready, t - 1)
                    sp.dma_start(raw[u][:], w_dram[at(t)].rearrange("o p m -> (o p) m")).then_inc(w_in[u], 16)

                run_steps(sp, IT, 2, load)

            @block.scalar
            def _(act):
                def high_part(t, u, i):
                    act.wait_ge(w_in[u], 16 * (i + 1))
                    if not (isinstance(t, int) and t < 2):
                        act.wait_ge(done, t - 1)
                    nc.scalar.activation(wh[u][:], raw[u][:], ACT.Copy).then_inc(w_hi, 1)

                def gate(t, u, i):
                    act.wait_ge(done, t + 1)
                    if not (isinstance(t, int) and t < 2):
                        act.wait_ge(h_full, t - 1)
                    nc.scalar.activation(sg[u][:], acc[u][:, 0, :], func, scale=gate_scale(t)).then_inc(gated, 1)

                def step(t, u, i):
                    if not ternary:
                        if isinstance(t, int) and t == 0:
                            high_part(0, 0, 0)
                            high_part(1, 1, 0)
                        elif isinstance(t, int) and t == IT - 1:
                            pass
                        elif not isinstance(t, int):
                            high_part(t + 1, 1 - u, i if u == 0 else i + 1)
                        elif t + 1 < IT and t >= 1:
                            high_part(t + 1, 1 - u, (t + 1) // 2)
                    gate(t, u, i)

                run_steps(act, IT, 2, step)

            @block.gpsimd
            def _(pool):
                def low_part(t, u, i):
                    pool.wait_ge(w_hi, t + 1)
                    nc.gpsimd.tensor_tensor(wl[u][:], raw[u][:], f32(wh[u][:]), ALU.subtract).then_inc(w_ready, 1)

                if not ternary:
                    run_steps(pool, IT, 2, low_part)

            @block.vector
            def _(dve):
                def to_ternary(t, u, i):
                    dve.wait_ge(w_in[u], 16 * (i + 1))
                    if not (isinstance(t, int) and t < 2):
                        dve.wait_ge(done, t - 1)
                    for n in range(2):
                        nc.vector.tensor_scalar(sgn[:, n * W:(n + 1) * W], raw[u][:, n * W:(n + 1) * W], g["thr3"][:, 3 + n:4 + n], None,
                                                ALU.is_lt, ALU.bypass).then_inc(w_hi, 1)
                    for n in range(2):
                        if n == 0:
                            dve.wait_ge(w_hi, 2 * t + 2)
                        last = nc.vector.scalar_tensor_tensor(wh[u][:, n * W:(n + 1) * W], raw[u][:, n * W:(n + 1) * W], g["thr3"][:, n:n + 1],
                                                              sgn[:, n * W:(n + 1) * W], ALU.is_gt, ALU.subtract)
                    last.then_inc(w_ready, 1)
                    dve.wait_ge(w_ready, t + 1)

                def hidden(t, u, i):
                    dve.wait_ge(gated, t + 1)
                    nc.vector.scalar_tensor_tensor(hf[:], acc[u][:, 1, :], up_scale(t), sg[u][:], ALU.mult, ALU.mult).then_inc(h_full, 1)
                    dve.wait_ge(h_full, t + 1)
                    th, tl = (m[:, at(t), :].rearrange("p o n -> p (o n)") for m in (hh, hl))
                    nc.vector.tensor_copy(th, hf[:]).then_inc(h_done, 1)
                    dve.wait_ge(h_done, 2 * t + 1)
                    nc.vector.tensor_tensor(tl, hf[:], f32(th), ALU.subtract).then_inc(h_done, 1)
                    dve.wait_ge(h_done, 2 * t + 2)

                def step(t, u, i):
                    if ternary:
                        if isinstance(t, int) and t == 0:
                            to_ternary(0, 0, 0)
                            to_ternary(1, 1, 0)
                        elif not isinstance(t, int):
                            to_ternary(t + 1, 1 - u, i if u == 0 else i + 1)
                        elif t + 1 < IT:
                            to_ternary(t + 1, 1 - u, (t + 1) // 2)
                    hidden(t, u, i)

                
                run_steps(dve, IT, 2, step)

            @block.tensor
            def _(pe):
                def product(t, u, i):
                    pe.wait_ge(w_ready, t + 1)
                    if not (isinstance(t, int) and t < 2):
                        pe.wait_ge(h_full, t - 1)
                    for n in range(2):
                        for k in range(KT):
                            cols = slice(n * W + k * P, n * W + (k + 1) * P)
                            for half in range(2):
                                out = acc[u][:, n, half * HALF:(half + 1) * HALF]
                                x_h, x_l = (m[:, k, half * HALF:(half + 1) * HALF] for m in (xh, xl))
                                if ternary:
                                    nc.tensor.matmul(out, wh[u][:, cols], x_h, start=k == 0, stop=False)
                                    last = nc.tensor.matmul(out, wh[u][:, cols], x_l, start=False, stop=k == KT - 1)
                                else:
                                    last = three_passes(nc, out, wh[u][:, cols], wl[u][:, cols], x_h, x_l, k == 0, k == KT - 1)
                    last.then_inc(done, 1)

                run_steps(pe, IT, 2, product)


def accumulate_phase(nc, d, g, tag, n_k, m_tiles, w_dram, moving, finish, unroll=2, ternary=False,
                     produce=None, load_extra=None, first=None):
    M = m_tiles * P
    with ExitStack() as ctx:
        c = Core(nc, ctx)
        R = 2
        raw = [c.sb(f"{tag}_raw{n}", [P, M]) for n in range(R)]
        wh = [c.sb(f"{tag}_wh{n}", [P, M], F32R) for n in range(R)]
        wl = None if ternary else [c.sb(f"{tag}_wl{n}", [P, M], F32R) for n in range(R)]
        sgn = c.sb(f"{tag}_sgn", [P, M]) if ternary else None
        acc = c.ps(f"{tag}_acc", [P, m_tiles, TOK])
        w_in = [c.sem(f"{tag}_w_in{n}") for n in range(R)]
        w_hi, w_ready, used, made, sums = (c.sem(f"{tag}_{n}") for n in ("w_hi", "w_ready", "used", "made", "sums"))
        link = c.sem(f"{tag}_dve_chain")
        per = unroll // 2

        with nc.Block() as block:
            @block.sync
            def _(sp):
                def load(t, u, i):
                    if not (isinstance(t, int) and t < 2):
                        sp.wait_ge(w_ready, t - 1)
                    sp.dma_start(raw[u % 2][:], w_dram[at(t)].rearrange("o p m -> (o p) m")).then_inc(w_in[u % 2], 16)
                    if load_extra:
                        load_extra(sp, t, u, i, made)

                run_steps(sp, n_k, unroll, load)

            @block.scalar
            def _(act):
                def high_part(t, u, i):
                    act.wait_ge(w_in[u % 2], 16 * (i * per + u // 2 + 1))
                    if not (isinstance(t, int) and t < 2):
                        act.wait_ge(used, t - 1)
                    nc.scalar.activation(wh[u % 2][:], raw[u % 2][:], ACT.Copy).then_inc(w_hi, 1)

                if not ternary:
                    run_steps(act, n_k, unroll, high_part)

            @block.gpsimd
            def _(pool):
                def low_part(t, u, i):
                    pool.wait_ge(w_hi, t + 1)
                    nc.gpsimd.tensor_tensor(wl[u % 2][:], raw[u % 2][:], f32(wh[u % 2][:]), ALU.subtract).then_inc(w_ready, 1)

                if not ternary:
                    run_steps(pool, n_k, unroll, low_part)

            @block.vector
            def _(dve):
                def to_ternary(t, u, i):
                    dve.wait_ge(w_in[u % 2], 16 * (i * per + u // 2 + 1))
                    if not (isinstance(t, int) and t < 2):
                        dve.wait_ge(used, t - 1)
                    nc.vector.tensor_scalar(sgn[:], raw[u % 2][:], g["thr3"][:, 5:6], None, ALU.is_lt, ALU.bypass).then_inc(w_hi, 1)
                    dve.wait_ge(w_hi, t + 1)
                    nc.vector.scalar_tensor_tensor(wh[u % 2][:], raw[u % 2][:], g["thr3"][:, 2:3], sgn[:],
                                                   ALU.is_gt, ALU.subtract).then_inc(w_ready, 1)
                    dve.wait_ge(w_ready, t + 1)

                def make(t, u, i):
                    if not (isinstance(t, int) and t < 2):
                        dve.wait_ge(used, t - 1)
                    produce(dve, t, u, i, made)

                if ternary:
                    run_steps(dve, n_k, unroll, to_ternary)
                if produce:
                    run_steps(dve, n_k, unroll, make)
                count = [0]

                def chain(ins):
                    count[0] += 1
                    ins.then_inc(link, 1)
                    dve.wait_ge(link, count[0])

                for m in range(m_tiles):
                    dve.wait_ge(sums, m + 1)
                    finish(chain, m, acc[:, m, :])

            @block.tensor
            def _(pe):
                if first:
                    first(pe, acc)

                def product(t, u, i):
                    pe.wait_ge(w_ready, t + 1)
                    if produce:
                        pe.wait_ge(made, 2 * t + 2)
                    opens = isinstance(t, int) and t == 0 and not first
                    closes = isinstance(t, int) and t == n_k - 1
                    for m in range(m_tiles):
                        cols = slice(m * P, (m + 1) * P)
                        for half in range(2):
                            out = acc[:, m, half * HALF:(half + 1) * HALF]
                            x_h, x_l = moving(t, u, i, half)
                            if ternary:
                                nc.tensor.matmul(out, wh[u % 2][:, cols], x_h, start=opens, stop=False)
                                last = nc.tensor.matmul(out, wh[u % 2][:, cols], x_l, start=False, stop=closes)
                            else:
                                last = three_passes(nc, out, wh[u % 2][:, cols], wl[u % 2][:, cols], x_h, x_l, opens, closes)
                        if closes:
                            last.then_inc(sums, 1)
                    if not closes:
                        last.then_inc(used, 1)

                run_steps_closing(pe, n_k, unroll, product)


def run_steps_closing(eng, n, unroll, step):
    if n % unroll or n <= 2 * unroll:
        run_steps(eng, n, unroll, step)
        return
    whole = n // unroll
    for u in range(unroll):
        step(u, u, 0)
    with eng.Fori(1, whole - 1) as i:
        for u in range(unroll):
            step(i * unroll + u, u, i)
    for u in range(unroll):
        step((whole - 1) * unroll + u, u, whole - 1)


def split_finish(nc, hi, lo):
    def finish(chain, m, acc):
        chain(nc.vector.tensor_copy(hi[:, m, :], acc))
        chain(nc.vector.tensor_tensor(lo[:, m, :], acc, f32(hi[:, m, :]), ALU.subtract))
    return finish


def residual_finish(nc, g, op, scalar):
    resid, xh, xl = g["resid"], g["xh"], g["xl"]

    def finish(chain, m, acc):
        chain(nc.vector.scalar_tensor_tensor(resid[:, m, :], acc, scalar(m), resid[:, m, :], op, ALU.add))
        chain(nc.vector.tensor_copy(xh[:, m, :], resid[:, m, :]))
        chain(nc.vector.tensor_tensor(xl[:, m, :], resid[:, m, :], f32(xh[:, m, :]), ALU.subtract))
    return finish


def masked_finish(nc, mask, hf, hi, lo):
    def finish(chain, m, acc):
        mk = mask(m).rearrange("p (b o) -> p b o", o=1).to_broadcast([P, B, S])
        chain(nc.vector.tensor_tensor(hf[:].rearrange("p (b s) -> p b s", b=B), acc.rearrange("p (b s) -> p b s", b=B), mk, ALU.mult))
        chain(nc.vector.tensor_copy(hi[:, m, :], hf[:]))
        chain(nc.vector.tensor_tensor(lo[:, m, :], hf[:], f32(hi[:, m, :]), ALU.subtract))
    return finish


def resident(hi, lo):
    def moving(t, u, i, half):
        cols = slice(half * HALF, (half + 1) * HALF)
        if isinstance(t, int):
            return hi[:, t, cols], lo[:, t, cols]
        return tuple(m[:, at(t), cols].rearrange("p o n -> p (o n)") for m in (hi, lo))
    return moving


def early(n, k):
    return isinstance(n, int) and n < k


def project_phase(nc, d, g):
    xh, xl = g["xh"], g["xl"]
    W = REP * D
    V_GROUPS = HK // REP
    n_groups = GROUPS + V_GROUPS
    NQ = GROUPS * TT
    NV = V_GROUPS * TT
    ACC = 4
    PIECE = TT // KT
    with ExitStack() as ctx:
        c = Core(nc, ctx)
        raw = [c.sb(f"q_raw{n}", [P, KT, W]) for n in range(2)]
        wh = [c.sb(f"q_wh{n}", [P, KT, W], F32R) for n in range(2)]
        wl = [c.sb(f"q_wl{n}", [P, KT, W], F32R) for n in range(2)]
        sq = c.sb("q_sq", [P, REP, D])
        ss, rt, rs = ([c.sb(f"q_{x}{n}", [P, REP]) for n in range(2)] for x in ("ss", "rt", "rs"))
        qn, qc, qs, qr = ([c.sb(f"q_{x}{n}", [P, REP, D]) for n in range(2)] for x in ("qn", "qc", "qs", "qr"))
        st = [c.sb(f"q_st{n}", [P, BPT, REP, S]) for n in range(2)]
        vs = [c.sb(f"q_vs{n}", [P, W]) for n in range(2)]
        eps = c.sb("q_eps", [P, 1])
        acc = [c.ps(f"q_acc{n}", [P, REP, D]) for n in range(ACC)]
        tp = [c.ps(f"q_tp{n}", [P, REP, P]) for n in range(2)]
        w_in = [c.sem(f"qkv_w_in{n}") for n in range(2)]
        w_hi, w_ready = c.sem("qkv_w_hi"), c.sem("qkv_w_ready")
        done, squared, summed, rooted, inverse, normed, cosed, sined, rotated, turned, staged, eps_set, v_staged = (
            c.sem(f"qkv_{n}") for n in ("done", "squared", "summed", "rooted", "inverse", "normed", "cosed", "sined",
                                        "rotated", "turned", "staged", "eps_set", "v_staged"))
        stored = [c.sem(f"qkv_stored{n}") for n in range(2)]
        v_stored = [c.sem(f"qkv_v_stored{n}") for n in range(2)]

        def rotary_steps(eng, step):
            for slot in range(2):
                for tile in range(TT):
                    step(slot, slot, tile, slot * TT + tile, 0)
            with eng.Fori(1, HK // 2) as i:
                for slot in range(2):
                    for tile in range(TT):
                        step(i * 2 + slot, slot, tile, i * (2 * TT) + (slot * TT + tile), 0)
            for grp in range(HK, GROUPS):
                for tile in range(TT):
                    step(grp, grp % 2, tile, grp * TT + tile, 1)

        with nc.Block() as block:
            @block.sync
            def _(sp):
                def load(grp, slot):
                    sp.dma_start(raw[slot][:], d["w1_qkv"][at(grp)].rearrange("o p (k m) -> (o p) k m", k=KT)).then_inc(w_in[slot], 16)

                load(0, 0)
                load(1, 1)

                def step(grp, slot, tile, n, table):
                    if tile == 1 and not (isinstance(grp, int) and grp + 2 >= n_groups):
                        sp.wait_ge(w_ready, (grp + 1) * KT)
                        load(grp + 2, slot)
                    u = tile % 2
                    sp.wait_ge(staged, n + 1)
                    dst = g["qk_scr"][tile * BPT:(tile + 1) * BPT, :, at(grp), :].rearrange("b p o r -> p b (o r)")
                    sp.dma_start(dst, st[u][:].rearrange("p b r s -> p b (r s)")).then_inc(stored[u], 16)

                rotary_steps(sp, step)
                for n in range(NV):
                    grp, tile = divmod(n, TT)
                    sp.wait_ge(v_staged, n + 1)
                    sp.dma_start(g["v_scr"][tile * P:(tile + 1) * P, grp * W:(grp + 1) * W], vs[n % 2][:]).then_inc(v_stored[n % 2], 16)
                for u in range(2):
                    sp.wait_ge(stored[u], 16 * (NQ // 2))
                    sp.wait_ge(v_stored[u], 16 * (NV // 2))

            def weight_piece(grp, tile):
                return tile // PIECE if tile % PIECE == 0 and not (isinstance(grp, int) and grp + 1 >= n_groups) else None

            @block.gpsimd
            def _(pool):
                def low_part(grp, slot, k):
                    pool.wait_ge(w_hi, grp * KT + k + 1)
                    nc.gpsimd.tensor_tensor(wl[slot][:, k], raw[slot][:, k], f32(wh[slot][:, k]), ALU.subtract).then_inc(w_ready, 1)

                def step(grp, slot, tile, n, table):
                    u = tile % 2
                    pool.wait_ge(normed, n + 1)
                    if not early(n, 2):
                        pool.wait_ge(rotated, n - 1)
                    tab = g["rope_c"][:, table, tile, :].rearrange("p (o n) -> p o n", o=1).to_broadcast([P, REP, D])
                    nc.gpsimd.tensor_tensor(qc[u][:], qn[u][:], tab, ALU.mult).then_inc(cosed, 1)
                    k = weight_piece(grp, tile)
                    if k is not None:
                        low_part(grp + 1, 1 - slot, k)

                for k in range(KT):
                    low_part(0, 0, k)
                rotary_steps(pool, step)
                for k in range(KT):
                    low_part(n_groups - 1, 1, k)

            @block.scalar
            def _(act):
                act.wait_ge(eps_set, 1)

                def high_part(grp, slot, k):
                    if k == 0:
                        act.wait_ge(w_in[slot], (grp - slot) * 8 + 16)
                        if not early(grp, 2):
                            act.wait_ge(done, (grp - 1) * TT)
                    nc.scalar.activation(wh[slot][:, k], raw[slot][:, k], ACT.Copy).then_inc(w_hi, 1)

                def evacuate(n, u):
                    act.wait_ge(turned, n + 1)
                    if not early(n, 2):
                        act.wait_ge(stored[u], (n - u) * 8)
                    nc.scalar.activation(st[u][:].rearrange("p b r s -> p r b s"),
                                         tp[u][:].rearrange("p r (b s) -> p r b s", b=BPT), ACT.Copy).then_inc(staged, 1)

                def step(grp, slot, tile, n, table):
                    u = tile % 2
                    act.wait_ge(done, n + 1)
                    if not early(n, 1):
                        act.wait_ge(summed, n)
                    nc.scalar.activation(sq[:], acc[tile % ACC][:], ACT.Square).then_inc(squared, 1)
                    if not early(n, 3):
                        evacuate(n - 3, 1 - u)
                    k = weight_piece(grp, tile)
                    if k is not None:
                        high_part(grp + 1, 1 - slot, k)
                    act.wait_ge(summed, n + 1)
                    if not early(n, 2):
                        act.wait_ge(inverse, n - 1)
                    nc.scalar.activation(rt[u][:], ss[u][:], ACT.Sqrt, bias=eps[:], scale=1.0 / D).then_inc(rooted, 1)

                for k in range(KT):
                    high_part(0, 0, k)
                rotary_steps(act, step)
                for n in range(NQ - 3, NQ):
                    evacuate(n, n % 2)
                for k in range(KT):
                    high_part(n_groups - 1, 1, k)
                for n in range(NV):
                    act.wait_ge(done, NQ + n + 1)
                    if n >= 2:
                        act.wait_ge(v_stored[n % 2], 16 * (n // 2))
                    nc.scalar.activation(vs[n % 2][:], acc[n % ACC][:].rearrange("p r d -> p (r d)"), ACT.Copy).then_inc(v_staged, 1)

            @block.vector
            def _(dve):
                nc.vector.memset(eps[:], RMS_EPS).then_inc(eps_set, 1)
                hd = D // 2

                def add(n, u):
                    dve.wait_ge(cosed, n + 1)
                    dve.wait_ge(sined, 2 * n + 2)
                    if not early(n, 2):
                        dve.wait_ge(turned, n - 1)
                    nc.vector.tensor_tensor(qr[u][:], qc[u][:], qs[u][:], ALU.add).then_inc(rotated, 1)

                def step(grp, slot, tile, n, table):
                    u = tile % 2
                    dve.wait_ge(squared, n + 1)
                    if not early(n, 2):
                        dve.wait_ge(rooted, n - 1)
                    nc.vector.reduce_sum(ss[u][:], sq[:], AX_X).then_inc(summed, 1)
                    if not early(n, 1):
                        add(n - 1, 1 - u)
                    dve.wait_ge(rooted, n + 1)
                    nc.vector.reciprocal(rs[u][:], rt[u][:]).then_inc(inverse, 1)
                    dve.wait_ge(inverse, n + 1)
                    if not early(n, 2):
                        dve.wait_ge(cosed, n - 1)
                    nc.vector.tensor_tensor(qn[u][:], acc[tile % ACC][:], rs[u][:].rearrange("p (r o) -> p r o", o=1).to_broadcast([P, REP, D]),
                                            ALU.mult).then_inc(normed, 1)
                    dve.wait_ge(normed, n + 1)
                    if not early(n, 2):
                        dve.wait_ge(rotated, n - 1)
                    for half in range(2):
                        tab = g["rope_s"][:, table, tile, half * hd:(half + 1) * hd].rearrange("p (o n) -> p o n", o=1).to_broadcast([P, REP, hd])
                        nc.vector.tensor_tensor(qs[u][:, :, half * hd:(half + 1) * hd], qn[u][:, :, (1 - half) * hd:(2 - half) * hd],
                                                tab, ALU.mult).then_inc(sined, 1)

                rotary_steps(dve, step)
                add(NQ - 1, 1)

            @block.tensor
            def _(pe):
                def project(grp, slot, tile, n):
                    if tile == 0:
                        pe.wait_ge(w_ready, (grp + 1) * KT)
                    if not early(n, ACC):
                        if isinstance(n, int) and n >= NQ + ACC:
                            pe.wait_ge(v_staged, n - NQ - ACC + 1)
                        else:
                            pe.wait_ge(normed, n - ACC + 1)
                    for k in range(KT):
                        rows = slice(tile * P, (tile + 1) * P)
                        last = three_passes(nc, acc[tile % ACC][:].rearrange("p r d -> p (r d)"), xh[:, k, rows], xl[:, k, rows],
                                            wh[slot][:, k], wl[slot][:, k], k == 0, k == KT - 1)
                    last.then_inc(done, 1)

                def transpose(n, u):
                    pe.wait_ge(rotated, n + 1)
                    if not early(n, 2):
                        pe.wait_ge(staged, n - 1)
                    for r in range(REP):
                        last = nc.tensor.transpose(tp[u][:, r, :], qr[u][:, r, :], g["ident"][:])
                    last.then_inc(turned, 1)

                def step(grp, slot, tile, n, table):
                    project(grp, slot, tile, n)
                    if not early(n, 2):
                        transpose(n - 2, tile % 2)

                rotary_steps(pe, step)
                for n in range(NQ, NQ + NV):
                    project(n // TT, (n // TT) % 2, n % TT, n)
                    if n < NQ + 2:
                        transpose(n - 2, n % 2)


def attention_phase(nc, d, g):
    G = REP * S
    assert G == P
    with ExitStack() as ctx:
        c = Core(nc, ctx)
        bt = c.sb("a_bt", [1, B * NPP], I32)
        vpage = c.sb("a_vpage", [P, B * VCH], I32)
        vpf, vrow = c.sb("a_vpf", [P, B * VCH]), c.sb("a_vrow", [P, B * VCH], I32)
        kb = [c.sb(f"a_kb{n}", [P, NPP, HK, PSIZE]) for n in range(2)]
        vb = [c.sb(f"a_vb{n}", [P, VCH, HK * D]) for n in range(2)]
        qk = [c.sb(f"a_qk{n}", [P, GROUPS, G]) for n in range(2)]
        vn = [c.sb(f"a_vn{n}", [S, HK * D]) for n in range(2)]
        vidx = [c.sb(f"a_vidx{n}", [P, VCH], I32) for n in range(2)]
        mask = [c.sb(f"a_mask{n}", [P, KEYS]) for n in range(2)]
        ob = [c.sb(f"a_ob{n}", [P, HK, G]) for n in range(2)]
        sm, pr, pn = ([c.sb(f"a_{x}{n}", [P, KEYS]) for n in range(2)] for x in ("sm", "pr", "pn"))
        ptm, ptn = [c.sb(f"a_ptm{n}", [P, VCH, G]) for n in range(2)], [c.sb(f"a_ptn{n}", [S, G]) for n in range(2)]
        mx, den, rc = (c.sb(f"a_{x}", [P, 2]) for x in ("mx", "den", "rc"))
        sc = [c.ps(f"a_sc{n}", [P, 1024]) for n in range(2)]
        tpm = [c.ps(f"a_tpm{n}", [P, VCH, G]) for n in range(2)]
        tpn = c.ps("a_tpn", [S, 2, G])
        oo = c.ps("a_oo", [P, 2, G])
        tab_in, rows_made, conv, rows_taken = (c.sem(f"att_{n}") for n in ("tab_in", "rows_made", "conv", "rows_taken"))
        k_in, v_in, qk_in, vn_in, stored = ([c.sem(f"att_{x}{n}") for n in range(2)] for x in ("k_in", "v_in", "qk_in", "vn_in", "stored"))
        o_moved, gate_pool, gate_dve = (c.sem(f"att_{n}") for n in ("o_moved", "gate_pool", "gate_dve"))
        masked, scored, shifted, exped, inverse, normed, turned, moved_m, moved_n, mixed = (
            c.sem(f"att_{n}") for n in ("masked", "scored", "shifted", "exped", "inverse", "normed", "turned", "moved_m", "moved_n", "mixed"))
        NU = B * HK

        def unit_steps(eng, step, lag=0):
            for u in range(2 * HK):
                step(u, u // HK, u % HK, u)
            with eng.Fori(1, B // 2) as i:
                for u in range(2 * HK):
                    step(u, u // HK, u % HK, i * (2 * HK) + u)

        with nc.Block() as block:
            @block.sync
            def _(sp):
                sp.dma_start(bt[:], d["itok_Bx16_0_63"].rearrange("b (o n) -> o (b n)", o=1)).then_inc(tab_in, 16)
                for q in range(NPP // VCH):
                    sp.dma_start(vpage[q * PSIZE:(q + 1) * PSIZE, :], d["vpages"][q:q + 1, :].to_broadcast([PSIZE, B * VCH])).then_inc(tab_in, 16)
                sp.wait_ge(tab_in, 16 * 5)

                def load(b, s, i):
                    pages = nc.values_load_multi_w_load_instructions(
                        bt[0:1, bass.ds(b * NPP, NPP)], engines=[mybir.EngineType.SP], min_val=0, max_val=PAGES - 1,
                        skip_runtime_bounds_check_because="the block table names pages of the cache")[1]
                    if not early(b, 2):
                        sp.wait_ge(mixed, (b - 1) * HK)
                    sp.dma_start(qk[s][:], g["qk_scr"][at(b)].rearrange("o p g r -> (o p) g r")).then_inc(qk_in[s], 16)
                    sp.dma_start(vn[s][:], g["v_scr"][bass.ds(b * S, S), :]).then_inc(vn_in[s], 16)
                    for j in range(NPP):
                        sp.dma_start(kb[s][:, j].rearrange("p h k -> p (h k)"),
                                     d["kT_pages"][bass.ds(pages[j], 1)].rearrange("o p f -> (o p) f")).then_inc(k_in[s], 16)

                def store(b, s):
                    sp.wait_ge(o_moved, (b + 1) * HK)
                    sp.dma_start(g["o_scr"][at(b)].rearrange("o p r -> (o p) r"), ob[s][:].rearrange("p h r -> p (h r)")).then_inc(stored[s], 16)

                load(0, 0, 0)
                load(1, 1, 0)
                with sp.Fori(1, B // 2) as i:
                    for s in range(2):
                        load(i * 2 + s, s, i)
                        store(i * 2 + (s - 2), s)
                for s in range(2):
                    store(B - 2 + s, s)
                    sp.wait_ge(stored[s], 16 * (B // 2))

            @block.gpsimd
            def _(pool):
                pool.wait_ge(rows_made, 1)

                def load_values(b, s):
                    nc.gpsimd.tensor_copy(vidx[s][:], vrow[:, bass.ds(b * VCH, VCH)]).then_inc(rows_taken, 1)
                    pool.wait_ge(rows_taken, b + 1)
                    pool.sem_inc(gate_pool, 1)
                    for j in range(VCH):
                        nc.gpsimd.indirect_dma_start(
                            vb[s][:, j, :], None, d["v_rows"],
                            bass.IndirectOffsetOnAxis(ap=vidx[s][:, j:j + 1], axis=0)).then_inc(v_in[s], 16)

                def batch(b, s, n0, prefetch):
                    for h in range(HK):
                        n, v = n0 + h, h % 2
                        if prefetch and h == 3:
                            pool.wait_ge(mixed, b * HK)
                            load_values(b + 1, 1 - s)
                        pool.wait_ge(inverse, n + 1)
                        if not early(n, 2):
                            pool.wait_ge(turned, n - 1)
                        pool.sem_inc(gate_pool, 1)
                        nc.gpsimd.tensor_scalar(pn[v][:], pr[v][:], rc[:, v:v + 1], 1.0, ALU.mult, ALU.mult).then_inc(normed, 1)

                load_values(0, 0)
                load_values(1, 1)
                batch(0, 0, 0, False)
                batch(1, 1, HK, True)
                with pool.Fori(1, B // 2 - 1) as i:
                    for s in range(2):
                        batch(i * 2 + s, s, i * (2 * HK) + s * HK, True)
                batch(B - 2, 0, NU - 2 * HK, True)
                batch(B - 1, 1, NU - HK, False)

            @block.scalar
            def _(act):
                def move_main(n, u):
                    act.wait_ge(turned, n + 1)
                    if not early(n, 2):
                        act.wait_ge(mixed, n - 1)
                    nc.scalar.activation(ptm[u][:], tpm[u][:], ACT.Copy).then_inc(moved_m, 1)

                def step(u, s, h, n):
                    act.wait_ge(shifted, n + 1)
                    if not early(n, 2):
                        act.wait_ge(normed, n - 1)
                    v = u % 2
                    nc.scalar.activation(pr[v][:], sm[v][:], ACT.Exp, bias=mx[:, v:v + 1], scale=-1.0,
                                         accum_out=den[:, v:v + 1]).then_inc(exped, 1)
                    if not early(n, 1):
                        move_main(n - 1, 1 - v)

                unit_steps(act, step)
                move_main(NU - 1, 1)

            @block.vector
            def _(dve):
                dve.wait_ge(tab_in, 16 * 5)
                nc.vector.tensor_copy(vpf[:], vpage[:]).then_inc(conv, 1)
                dve.wait_ge(conv, 1)
                nc.vector.tensor_scalar(vrow[:], vpf[:], float(PSIZE), g["cols"][:, 7:8], ALU.mult, ALU.add).then_inc(rows_made, 1)

                def make_mask(b, s):
                    if not early(b, 2):
                        dve.wait_ge(shifted, (b - 1) * HK)
                    nc.vector.tensor_scalar(mask[s][:], g["keyidx"][:], g["lens"][:, 1, at(b)], NEG, ALU.is_ge, ALU.mult).then_inc(masked, 1)
                    dve.wait_ge(masked, b + 1)

                def move_out(n, v, s, h):
                    dve.wait_ge(mixed, n + 1)
                    if h == 0 and not early(n, 2 * HK):
                        dve.wait_ge(stored[s], (n - s * HK))
                    nc.vector.tensor_copy(ob[s][:, h, :], oo[:, v, :]).then_inc(o_moved, 1)

                def move_new(n, v):
                    dve.wait_ge(turned, n + 1)
                    if not early(n, 2):
                        dve.wait_ge(mixed, n - 1)
                    nc.vector.tensor_copy(ptn[v][:], tpn[:, v, :]).then_inc(moved_n, 1)

                def step(u, s, h, n, i):
                    v = u % 2
                    if h == 0:
                        make_mask(i * 2 + s, s)
                    dve.wait_ge(scored, n + 1)
                    if not early(n, 2):
                        dve.wait_ge(exped, n - 1)
                    dve.sem_inc(gate_dve, 1)
                    nc.vector.tensor_tensor_reduce(out=sm[v][:], in0=sc[v][:, 0:KEYS], in1=mask[s][:], scale=-ATT_SCALE, scalar=3e38,
                                                   op0=ALU.add, op1=ALU.min, accum_out=mx[:, v:v + 1]).then_inc(shifted, 1)
                    dve.wait_ge(exped, n + 1)
                    if not early(n, 2):
                        dve.wait_ge(normed, n - 1)
                    nc.vector.reciprocal(rc[:, v:v + 1], den[:, v:v + 1]).then_inc(inverse, 1)
                    if not early(n, 2):
                        w = u - 2 if u >= 2 else u + 2 * HK - 2
                        move_out(n - 2, v, w // HK, w % HK)
                    if not early(n, 1):
                        move_new(n - 1, 1 - v)

                for u in range(2 * HK):
                    step(u, u // HK, u % HK, u, 0)
                with dve.Fori(1, B // 2) as i:
                    for u in range(2 * HK):
                        step(u, u // HK, u % HK, i * (2 * HK) + u, i)
                move_out(NU - 2, 0, 1, HK - 2)
                move_new(NU - 1, 1)
                move_out(NU - 1, 1, 1, HK - 1)

            @block.tensor
            def _(pe):
                def score(n, u, s, h, i):
                    v = u % 2
                    if h == 0:
                        pe.wait_ge(k_in[s], (i + 1) * (16 * NPP))
                        pe.wait_ge(qk_in[s], (i + 1) * 16)
                    if not early(n, 2):
                        pe.wait_ge(shifted, n - 1)
                    new = qk[s][:, HK + h // REP, (h % REP) * S:(h % REP + 1) * S]
                    nc.tensor.matmul(sc[v][:, 0:CACHE].rearrange("p (j k) -> p j k", k=PSIZE), qk[s][:, h, :], kb[s][:, :, h, :], start=True, stop=True)
                    nc.tensor.matmul(sc[v][:, CACHE:KEYS], qk[s][:, h, :], new, start=True, stop=True).then_inc(scored, 1)

                def turn(n, u):
                    v = u % 2
                    pe.wait_ge(normed, n + 1)
                    if not early(n, 2):
                        pe.wait_ge(moved_m, n - 1)
                        pe.wait_ge(moved_n, n - 1)
                    for j in range(VCH):
                        nc.tensor.transpose(tpm[v][:, j, :], pn[v][:, j * P:(j + 1) * P], g["ident"][:])
                    nc.tensor.transpose(tpn[:, v, :], pn[v][:, CACHE:KEYS], g["ident"][:]).then_inc(turned, 1)

                def mix(n, u, s, h, i):
                    v = u % 2
                    if h == 0:
                        pe.wait_ge(v_in[s], (i + 1) * (16 * VCH))
                        pe.wait_ge(vn_in[s], (i + 1) * 16)
                    pe.wait_ge(moved_m, n + 1)
                    pe.wait_ge(moved_n, n + 1)
                    if not early(n, 2):
                        pe.wait_ge(o_moved, n - 1)
                    for j in range(VCH):
                        nc.tensor.matmul(oo[:, v, :], vb[s][:, j, h * D:(h + 1) * D], ptm[v][:, j, :], start=j == 0, stop=False)
                    nc.tensor.matmul(oo[:, v, :], vn[s][:, h * D:(h + 1) * D], ptn[v][:], start=False, stop=True).then_inc(mixed, 1)

                def step(u, n, i):
                    score(n, u, u // HK, u % HK, i)
                    if not early(n, 2):
                        w = u - 2 if u >= 2 else u + 2 * HK - 2
                        mix(n - 2, w, w // HK, w % HK, i if u >= 2 else i - 1)
                    if not early(n, 1):
                        turn(n - 1, u + 1)

                for u in range(2 * HK):
                    step(u, u, 0)
                with pe.Fori(1, B // 2) as i:
                    for u in range(2 * HK):
                        step(u, i * (2 * HK) + u, i)
                last = B // 2 - 1
                mix(NU - 2, 2 * HK - 2, 1, HK - 2, last)
                turn(NU - 1, 1)
                mix(NU - 1, 2 * HK - 1, 1, HK - 1, last)


def output_projection(nc, d, g, cf):
    xh, xl = g["xh"], g["xl"]
    with ExitStack() as ctx:
        c = Core(nc, ctx)
        ring = [c.sb(f"wo_o{n}", [P, B, P]) for n in range(2)]
        mh, ml = ([c.sb(f"wo_{x}{n}", [P, TOK], F32R) for n in range(2)] for x in ("mh", "ml"))
        o_in = [c.sem(f"wo_o_in{n}") for n in range(2)]

        def load_extra(sp, t, u, i, made):
            if u % REP:
                return
            s = u // REP
            if not early(t, 2 * REP):
                sp.wait_ge(made, (t - REP) * 2)
            sp.dma_start(ring[s][:], g["o_scr"][:, :, bass.ds(t * S, P)].rearrange("b p r -> p b r")).then_inc(o_in[s], 16)

        def produce(dve, t, u, i, made):
            s, r = u // REP, u % REP
            if r == 0:
                dve.wait_ge(o_in[s], (i + 1) * 16)
            src = ring[s][:, :, r * S:(r + 1) * S]
            hi, lo = (m[u % 2][:].rearrange("p (b s) -> p b s", b=B) for m in (mh, ml))
            nc.vector.tensor_copy(hi, src).then_inc(made, 1)
            dve.wait_ge(made, t * 2 + 1)
            nc.vector.tensor_tensor(lo, src, f32(hi), ALU.subtract).then_inc(made, 1)

        def moving(t, u, i, half):
            cols = slice(half * HALF, (half + 1) * HALF)
            return mh[u % 2][:, cols], ml[u % 2][:, cols]

        def finish(chain, m, acc):
            chain(nc.vector.tensor_copy(cf[:, m, :], acc))
            chain(nc.vector.tensor_copy(xh[:, m, :], acc))
            chain(nc.vector.tensor_tensor(xl[:, m, :], acc, f32(xh[:, m, :]), ALU.subtract))

        accumulate_phase(nc, d, g, "wo", HQ, KT, d["w1_o"], moving, finish, unroll=2 * REP, produce=produce, load_extra=load_extra)


def route_phase(nc, d, g, cf, sel_t, mb):
    E = EXPERTS
    with ExitStack() as ctx:
        c = Core(nc, ctx)
        gw, gb = c.sb("r_gw", [P, KT, E]), c.sb("r_gb", [P, E])
        z, eq, sel = (c.sb(f"r_{x}", [P, TT, E]) for x in ("z", "eq", "sel"))
        mx, taken = c.sb("r_mx", [P, TT]), c.sb("r_taken", [P, TT])
        pick = c.sb("r_pick", [E, E, P])
        pz = c.ps("r_pz", [P, TT, E])
        ptr = c.ps("r_ptr", [E, TOK])
        pb = c.ps("r_pb", [P, 2, TOK])
        w_in, link, logits, chosen, turned, out, spread, copied = (
            c.sem(f"route_{n}") for n in ("w_in", "chain", "logits", "chosen", "turned", "out", "spread", "copied"))
        with nc.Block() as block:
            @block.sync
            def _(sp):
                sp.dma_start(gw[:], d["w1_gate"]).then_inc(w_in, 16)
                sp.dma_start(gb[:], d["L1_ffn_gate_b"].rearrange("(a s) -> a s", a=1).to_broadcast([P, E])).then_inc(w_in, 16)
                sp.dma_start(pick[:], d["pick"]).then_inc(w_in, 16)

            @block.tensor
            def _(pe):
                pe.wait_ge(w_in, 48)
                for t in range(TT):
                    for k in range(KT):
                        last = nc.tensor.matmul(pz[:, t, :], cf[:, k, t * P:(t + 1) * P], gw[:, k, :], start=k == 0, stop=k == KT - 1)
                last.then_inc(logits, 1)
                pe.wait_ge(chosen, 1)
                for t in range(TT):
                    last = nc.tensor.transpose(ptr[:, t * P:(t + 1) * P], sel[:, t, :], g["ident"][:])
                last.then_inc(turned, 1)
                pe.wait_ge(out, 1)
                for j in range(E):
                    if j >= 2:
                        pe.wait_ge(copied, j - 1)
                    for half in range(2):
                        cols = slice(half * HALF, (half + 1) * HALF)
                        last = nc.tensor.matmul(pb[:, j % 2, cols], pick[:, j, :], sel_t[:, cols], start=True, stop=True)
                    last.then_inc(spread, 1)

            @block.vector
            def _(dve):
                count = [0]

                def chain(ins):
                    count[0] += 1
                    ins.then_inc(link, 1)
                    dve.wait_ge(link, count[0])

                dve.wait_ge(logits, 1)
                dve.wait_ge(w_in, 48)
                chain(nc.vector.tensor_tensor(z[:], pz[:], gb[:].rearrange("p (o e) -> p o e", o=1).to_broadcast([P, TT, E]), ALU.add))
                chain(nc.vector.reduce_max(mx[:], z[:], AX_X))
                chain(nc.vector.tensor_tensor(eq[:], z[:], mx[:].rearrange("p (t o) -> p t o", o=1).to_broadcast([P, TT, E]), ALU.is_equal))
                chain(nc.vector.memset(taken[:], 0.0))
                for j in range(E):
                    chain(nc.vector.tensor_tensor(sel[:, :, j], eq[:, :, j], taken[:], ALU.is_gt))
                    chain(nc.vector.tensor_tensor(taken[:], taken[:], eq[:, :, j], ALU.max))
                dve.sem_inc(chosen, 1)
                dve.wait_ge(turned, 1)
                nc.vector.tensor_copy(sel_t[:], ptr[:]).then_inc(out, 1)

            @block.scalar
            def _(act):
                for j in range(E):
                    act.wait_ge(spread, j + 1)
                    nc.scalar.activation(mb[:, j, :], pb[:, j % 2, :], ACT.Copy).then_inc(copied, 1)


def expert_phase(nc, d, g, sel_t, mb, eb):
    xh, xl = g["xh"], g["xl"]
    with ExitStack() as ctx:
        c = Core(nc, ctx)
        mh, ml = ([c.sb(f"moe_{x}{n}", [P, TOK], F32R) for n in range(2)] for x in ("mh", "ml"))

        def produce(dve, t, u, i, made):
            m = mb[:, at(i), :].rearrange("p o n -> p (o n)")
            nc.vector.tensor_tensor(mh[u % 2][:], f32(xh[:, u, :]), m, ALU.mult).then_inc(made, 1)
            nc.vector.tensor_tensor(ml[u % 2][:], f32(xl[:, u, :]), m, ALU.mult).then_inc(made, 1)

        def moving(t, u, i, half):
            cols = slice(half * HALF, (half + 1) * HALF)
            return mh[u % 2][:, cols], ml[u % 2][:, cols]

        def first(pe, acc):
            for m in range(KT):
                for half in range(2):
                    cols = slice(half * HALF, (half + 1) * HALF)
                    nc.tensor.matmul(acc[:, m, cols], eb[:, m * P:(m + 1) * P], sel_t[:, cols], start=True, stop=False)

        accumulate_phase(nc, d, g, "moe", EXPERTS * KT, KT, d["w1_e"], moving, residual_finish(nc, g, ALU.mult, lambda m: 1.0),
                         unroll=KT, produce=produce, first=first)


def load_small(nc, tag, pairs):
    with ExitStack() as ctx:
        c = Core(nc, ctx)
        loaded = c.sem(f"{tag}_loaded")
        with nc.Block() as block:
            @block.sync
            def _(sp):
                for dst, src in pairs:
                    sp.dma_start(dst, src).then_inc(loaded, 16)
                sp.wait_ge(loaded, 16 * len(pairs))


def clear_phase(nc):
    with nc.Block() as block:
        @block.sync
        def _(sp):
            sp.sem_clear(range(min(Core.used), max(Core.used) + 1))
    Core.used.clear()


def store_phase(nc, g, out):
    with ExitStack() as ctx:
        c = Core(nc, ctx)
        stored = c.sem("out_stored")
        with nc.Block() as block:
            @block.sync
            def _(sp):
                sp.dma_start(out, g["resid"][:]).then_inc(stored, 16)
                sp.wait_ge(stored, 16)


def program(nc, d, out, upto=99):
    Core.used.clear()
    with ExitStack() as ctx:
        c = Core(nc, ctx)
        g = {
            "resid": c.sb("resid", [P, KT, TOK]), "xh": c.sb("xh", [P, KT, TOK], F32R), "xl": c.sb("xl", [P, KT, TOK], F32R),
            "ident": c.sb("ident_sb", [P, P]), "cols": c.sb("cols_sb", [P, 8]), "keyidx": c.sb("keyidx_sb", [P, KEYS]),
            "lens": c.sb("lens", [P, 4, B]), "lmask": c.sb("lmask", [P, KT, B]), "amask": c.sb("amask", [P, B]),
            "bmask": c.sb("bmask", [P, 2, B]), "rope_c": c.sb("rope_c", [P, 2, TT, D]), "rope_s": c.sb("rope_s", [P, 2, TT, D]),
            "scale3": c.sb("scale3", [P, 3]), "thr3": c.sb("thr3", [P, 6]),
            "kpad": nc.dram_tensor("kpad", [S, KPAD], F32).ap(),
            "qk_scr": nc.dram_tensor("qk_scr", [B, P, GROUPS, REP * S], F32).ap(),
            "v_scr": nc.dram_tensor("v_scr", [TOK, HK * D], F32).ap(),
            "o_scr": nc.dram_tensor("o_scr", [B, P, HQ * S], F32).ap(),
        }
        vec = c.sb("vectors", [P, 2 * IT + 4 * KT])
        AG, AU, AD, BIAS2, PROBS = 0, IT, 2 * IT, 2 * IT + KT, 2 * IT + 2 * KT
        xh, xl = g["xh"], g["xl"]
        setup_phase(nc, d, g)
        load_small(nc, "vec", [(vec[:, 0:2 * IT + 2 * KT + 2], d["vectors"])])

        def column(base):
            return lambda t: vec[:, base + t:base + t + 1] if isinstance(t, int) else vec[:, bass.ds(t + base, 1)]

        conv_phase(nc, d, g)
        if upto > 0:
            with ExitStack() as inner:
                ci = Core(nc, inner)
                hh, hl = ci.sb("hh", [P, IT, TOK], F32R), ci.sb("hl", [P, IT, TOK], F32R)
                gate_up_phase(nc, d, g, hh, hl, "f0", d["w0_gu"], False, ACT.Silu, column(AG), column(AU))
                resid = g["resid"]

                def finish0(chain, m, acc):
                    r = resid[:, m, :].rearrange("p (b s) -> p s b", b=B)
                    chain(nc.vector.scalar_tensor_tensor(r, acc.rearrange("p (s b) -> p s b", b=B), vec[:, AD + m:AD + m + 1], r, ALU.mult, ALU.add))
                    chain(nc.vector.tensor_copy(xh[:, m, :], resid[:, m, :]))
                    chain(nc.vector.tensor_tensor(xl[:, m, :], resid[:, m, :], f32(xh[:, m, :]), ALU.subtract))

                accumulate_phase(nc, d, g, "d0", IT, KT, d["w0_d"], resident(hh, hl), finish0)
        if upto > 1:
            project_phase(nc, d, g)
            attention_phase(nc, d, g)
            with ExitStack() as inner:
                ci = Core(nc, inner)
                cf = ci.sb("cf", [P, KT, TOK])
                output_projection(nc, d, g, cf)
                if upto > 2:
                    sel_t, mb, eb = ci.sb("sel_t", [EXPERTS, TOK]), ci.sb("mb", [P, EXPERTS, TOK]), ci.sb("eb", [EXPERTS, H])
                    load_small(nc, "eb", [(eb[:], d["L1_ffn_expert_b"])])
                    route_phase(nc, d, g, cf, sel_t, mb)
                    expert_phase(nc, d, g, sel_t, mb, eb)
        clear_phase(nc)
        if upto > 3:
            with ExitStack() as inner:
                ci = Core(nc, inner)
                hf = ci.sb("l_hf", [P, TOK])
                lh, ll = ci.sb("l_h", [P, 2, TOK], F32R), ci.sb("l_l", [P, 2, TOK], F32R)
                accumulate_phase(nc, d, g, "a2", KT, 1, d["w2_b"], resident(xh, xl), masked_finish(nc, lambda m: g["amask"][:], hf, lh, ll))
                accumulate_phase(nc, d, g, "b2", 1, KT, d["w2_a"], resident(lh, ll), split_finish(nc, xh, xl))

                def scaled(chain, m, acc):
                    chain(nc.vector.tensor_scalar(hf[:], acc, vec[:, PROBS + m:PROBS + m + 1], None, ALU.mult, ALU.bypass))
                    chain(nc.vector.tensor_copy(lh[:, m, :], hf[:]))
                    chain(nc.vector.tensor_tensor(ll[:, m, :], hf[:], f32(lh[:, m, :]), ALU.subtract))

                accumulate_phase(nc, d, g, "c2", KT, 2, d["w2_fa"], resident(xh, xl), scaled)

                def wide_then_low(t, u, i, half):
                    cols = slice(half * HALF, (half + 1) * HALF)
                    return (xh[:, t, cols], xl[:, t, cols]) if t < KT else (lh[:, t - KT, cols], ll[:, t - KT, cols])

                accumulate_phase(nc, d, g, "e2", KT + 2, KT, d["w2_wb"], wide_then_low,
                                 residual_finish(nc, g, ALU.add, lambda m: vec[:, BIAS2 + m:BIAS2 + m + 1]), unroll=4)
                if upto > 4:
                    accumulate_phase(nc, d, g, "a3", KT, 2, d["w3_la"], resident(xh, xl), masked_finish(nc, lambda m: g["bmask"][:, m, :], hf, lh, ll))
                    accumulate_phase(nc, d, g, "b3", KT + 2, KT, d["w3_wb"], wide_then_low, split_finish(nc, xh, xl), unroll=4)
        if upto > 4:
            with ExitStack() as inner:
                ci = Core(nc, inner)
                hh, hl = ci.sb("hh3", [P, IT, TOK], F32R), ci.sb("hl3", [P, IT, TOK], F32R)
                sc3 = g["scale3"]
                gate_up_phase(nc, d, g, hh, hl, "f3", d["w3_gu"], True, ACT.Copy, lambda t: sc3[:, 0:1], lambda t: sc3[:, 1:2])
                accumulate_phase(nc, d, g, "d3", IT, KT, d["w3_d"], resident(hh, hl),
                                 residual_finish(nc, g, ALU.mult, lambda m: sc3[:, 2:3]), ternary=True)
        store_phase(nc, g, out)


def tiles_of(w, k_tiles, cols):
    full = np.zeros((k_tiles * P, cols), np.float32)
    full[:w.shape[0], :w.shape[1]] = w
    return full.reshape(k_tiles, P, cols)


def gate_up_tiles(wg, wu):
    both = np.stack([tiles_of(w.T, KT, IT * P) for w in (wg, wu)])
    return np.ascontiguousarray(both.reshape(2, KT, P, IT, P).transpose(3, 2, 0, 1, 4)).reshape(IT, P, 2 * KT * P)


def vector_columns(v, tiles):
    full = np.zeros(tiles * P, np.float32)
    full[:v.shape[0]] = v
    return full.reshape(tiles, P).T


def layouts(i):
    i = {k: np.asarray(v) for k, v in i.items()}
    a = {k: i[k] for k in ("itok_B_78_3631", "itok_B_207_1644", "itok_B_3_7", "itok_B_0_4", "itok_Bx16_0_63", "L0_cond_log_dt", "L0_cond_D",
                           "L1_cond_q_norm_w", "L1_cond_k_norm_w", "L1_ffn_gate_b", "L1_ffn_expert_b")}
    x = i["x"]
    a["xT"] = x.transpose(2, 0, 1).reshape(KT, P, TOK).transpose(1, 0, 2)
    a["x_rev"] = x.transpose(2, 1, 0).reshape(KT, P, S, B)[:, ::-1].transpose(1, 2, 0, 3)
    for name, w in (("logA2", i["L0_cond_log_A_real"]), ("Aim2", i["L0_cond_A_imag"]), ("Cre2", i["L0_cond_C"][..., 0]), ("Cim2", i["L0_cond_C"][..., 1])):
        a[name] = np.concatenate([w.T, w.T])
    W = REP * D
    wq = i["L1_cond_Wq"].T.reshape(KT, P, HQ * D // W, W).transpose(2, 1, 0, 3)
    wk = i["L1_cond_Wk"].T.reshape(KT, P, HK * D // W, W).transpose(2, 1, 0, 3)
    wv = i["L1_cond_Wv"].T.reshape(KT, P, HK * D // W, W).transpose(2, 1, 0, 3)
    a["w1_qkv"] = np.concatenate([wq, wk, wv]).reshape(-1, P, KT * W)
    a["kT_pages"] = i["L1_cond_k_cache"].transpose(0, 3, 2, 1).reshape(PAGES, P, HK * PSIZE)
    a["v_rows"] = i["L1_cond_v_cache"].reshape(PAGES * PSIZE, HK * D)
    a["vpages"] = i["itok_Bx16_0_63"].reshape(B, VCH, NPP // VCH).transpose(2, 0, 1).reshape(NPP // VCH, B * VCH)
    a["w1_o"] = i["L1_cond_Wo"].T.reshape(HQ, P, H)
    a["w1_gate"] = i["L1_ffn_gate_w"].T.reshape(KT, P, EXPERTS).transpose(1, 0, 2)
    a["w1_e"] = i["L1_ffn_expert_w"].transpose(0, 2, 1).reshape(EXPERTS * KT, P, H)
    a["w0_gu"] = gate_up_tiles(i["L0_ffn_Wg"], i["L0_ffn_Wu"])
    a["w0_d"] = tiles_of(i["L0_ffn_Wd"].T, IT, H)
    a["w3_gu"] = gate_up_tiles(i["L3_ffn_w_gate"], i["L3_ffn_w_up"])
    a["w3_d"] = tiles_of(i["L3_ffn_w_down"].T, IT, H)
    a["vectors"] = np.concatenate([vector_columns(i["L0_ffn_ag"], IT), vector_columns(i["L0_ffn_au"], IT), vector_columns(i["L0_ffn_ad"], KT),
                                   vector_columns(i["L2_ffn_b"], KT), vector_columns(np.repeat(i["L2_ffn_probs"], 16), 2)], axis=1)
    a["w2_b"] = i["L2_cond_B"].reshape(ADAPTERS * RANK2, H).T.reshape(KT, P, P)
    a["w2_a"] = i["L2_cond_A"].transpose(0, 2, 1).reshape(1, P, H)
    a["w2_fa"] = i["L2_ffn_A"].reshape(-1, H).T.reshape(KT, P, 2 * P)
    a["w2_wb"] = np.concatenate([i["L2_ffn_W"].T, i["L2_ffn_B"].transpose(0, 2, 1).reshape(-1, H)]).reshape(KT + 2, P, H)
    a["w3_la"] = tiles_of(i["L3_cond_lora_A"].transpose(1, 0, 2).reshape(H, LABELS * RANK3), KT, 2 * P)
    low = np.concatenate([i["L3_cond_lora_B_w"].T] * LABELS)
    a["w3_wb"] = np.concatenate([i["L3_cond_weight"].T, low, np.zeros((2 * P - LABELS * RANK3, H), np.float32)]).reshape(KT + 2, P, H)

    row = np.arange(P)
    a["posbase"] = np.repeat(i["itok_B_207_1644"], S).reshape(TT, P).T
    a["seqpos"] = np.tile((row % S).astype(np.float32)[:, None], (1, TT))
    a["inv_freq"] = np.tile((1.0 / THETA ** (np.arange(0, D, 2, dtype=np.float32) / D)).astype(np.float32), (P, 1))
    upper = row < P // 2
    a["signs"] = np.stack([np.where(upper, 2.0, 0.0), np.where(upper, 0.0, -2.0), np.where(upper, -2.0, 0.0), np.where(upper, 0.0, -2.0)], 1).astype(np.float32)
    a["positions"] = np.tile(np.concatenate([np.arange(LO_N), LO_N * np.arange(HI_N)]).astype(np.float32), (P, 1))
    a["ident"] = np.eye(P, dtype=np.float32)
    a["keyidx"] = np.tile(np.concatenate([np.arange(CACHE), -np.ones(S)]).astype(np.float32), (P, 1))
    cols = np.zeros((P, 8), np.float32)
    for m in range(KT):
        cols[:, m] = m * P + row
    cols[:, 4] = row // RANK2
    cols[:, 5], cols[:, 6] = row // RANK3, (P + row) // RANK3
    cols[:, 7] = row % PSIZE
    a["cols"] = cols
    pick = np.zeros((EXPERTS, EXPERTS, P), np.float32)
    for j in range(EXPERTS):
        pick[j, j] = 1.0
    a["pick"] = pick
    return {k: np.ascontiguousarray(v) for k, v in a.items()}


def kernel(**inputs):
    import concourse.bacc as bacc
    from concourse.bass_utils import run_bass_kernel_spmd

    nc = bacc.Bacc("TRN2", target_bir_lowering=False, num_devices=1)
    arrays, d = {}, {}
    for name, a in layouts(inputs).items():
        arrays[f"in_{name}"] = a
        d[name] = nc.dram_tensor(f"in_{name}", a.shape, mybir.dt.from_np(a.dtype), kind="ExternalInput").ap()
    out = nc.dram_tensor("out_x", [P, KT, TOK], F32, kind="ExternalOutput").ap()
    program(nc, d, out)
    r = run_bass_kernel_spmd(nc, [arrays], core_ids=[0])
    got = r.results[0]["out_x"]
    return np.ascontiguousarray(got.reshape(P, KT, B, S).transpose(2, 3, 1, 0).reshape(B, S, H))
```

```python
from contextlib import ExitStack

import numpy as np

import concourse.bass as bass
from concourse import mybir

F32 = mybir.dt.float32
F32R = mybir.dt.float32r
I32 = mybir.dt.int32
BF16 = mybir.dt.bfloat16
ALU = mybir.AluOpType
ACT = mybir.ActivationFunctionType
AX_X = mybir.AxisListType.X

P = 128
B, S, H = 32, 32, 512
TOK = B * S
HALF = TOK // 2
KT = H // P
INTER = 1376
IT = -(-INTER // P)
N_STATE = 64
LO_N, HI_N = 32, H // 32
D = 128
HQ, HK = 32, 8
REP = HQ // HK
PAGES, PSIZE, NPP = 64, 32, 16
CACHE = NPP * PSIZE
KEYS = CACHE + S
VCH = CACHE // P
GROUPS = (HQ + HK) // REP
TT = TOK // P
BPT = P // S
EXPERTS = 8
ADAPTERS, RANK2 = 8, 16
LABELS, RANK3 = 5, 32
LABEL_PAD = 8
THETA = 10000.0
RMS_EPS = 1e-6
BIT_EPS = 1e-5
ATT_SCALE = 1.0 / float(np.sqrt(D))
NEG = -1e30
KPAD = P + H

TWO_PI = 2.0 * np.pi
MAGIC = 1.5 * 2.0 ** 23
PI_1 = 6.28125
PI_2 = float(np.round((TWO_PI - PI_1) * 2.0 ** 20) / 2.0 ** 20)
PI_3 = float(TWO_PI - PI_1 - PI_2)
PI_SAFE = 3.1415925
LN2_1, LN2_2 = 0.693359375, -2.12194440e-4


def run_steps(eng, n, unroll, step):
    for u in range(min(unroll, n)):
        step(u, u, 0)
    whole = n // unroll
    if whole > 2:
        with eng.Fori(1, whole) as i:
            for u in range(unroll):
                step(i * unroll + u, u, i)
    else:
        for i in range(1, whole):
            for u in range(unroll):
                step(i * unroll + u, u, i)
    for t in range(max(whole, 1) * unroll, n):
        step(t, t % unroll, t // unroll)


def early(n, k):
    return isinstance(n, int) and n < k


def at(i, n=1):
    return bass.ds(i, n)


def f32(ap):
    return ap.bitcast(F32)


class Core:
    used = []

    def __init__(self, nc, ctx):
        self.nc, self.ctx = nc, ctx

    def sb(self, name, shape, dt=F32):
        return self.ctx.enter_context(self.nc.sbuf_tensor(name, shape, dt))

    def ps(self, name, shape):
        return self.ctx.enter_context(self.nc.psum_tensor(name, shape, F32))

    def sem(self, name):
        handle = self.ctx.enter_context(self.nc.semaphore(name))
        self.used.append(handle.num)
        return handle


def three_passes(nc, out, w_hi, w_lo, x_hi, x_lo, start, stop):
    nc.tensor.matmul(out, w_hi, x_hi, start=start, stop=False)
    nc.tensor.matmul(out, w_hi, x_lo, start=False, stop=False)
    return nc.tensor.matmul(out, w_lo, x_hi, start=False, stop=stop)


def arithmetic(nc, chain):
    def tt(out, a, b_, op):
        chain(nc.vector.tensor_tensor(out, a, b_, op))

    def tsc(out, a, s1, s2, op0, op1):
        chain(nc.vector.tensor_scalar(out, a, s1, s2, op0, op1))

    def reduce_angle(x, k):
        tsc(k, x, 1.0 / TWO_PI, MAGIC, ALU.mult, ALU.add)
        tsc(k, k, -MAGIC, 0.0, ALU.add, ALU.add)
        for part in (PI_1, PI_2, PI_3):
            chain(nc.vector.scalar_tensor_tensor(x, k, -part, x, ALU.mult, ALU.add))
        tsc(x, x, PI_SAFE, -PI_SAFE, ALU.min, ALU.max)

    def cosine_angle(out, x, t):
        tsc(t, x, np.pi / 2, -TWO_PI, ALU.is_gt, ALU.mult)
        chain(nc.vector.scalar_tensor_tensor(out, x, np.pi / 2, t, ALU.add, ALU.add))
        tsc(out, out, PI_SAFE, -PI_SAFE, ALU.min, ALU.max)

    return tt, tsc, reduce_angle, cosine_angle


def setup_phase(nc, d, g):
    with ExitStack() as ctx:
        c = Core(nc, ctx)
        ai2, cre, cim = (c.sb(f"s_{n}", [P, S]) for n in ("ai", "cre", "cim"))
        two, two_e, two_k, two_r = (c.sb(f"s_two{n}", [P, 2 * S]) for n in ("", "_e", "_k", "_r"))
        two_b = c.sb("s_two_b", [P, 2 * S], I32)
        sgn = c.sb("s_sgn", [P, 4])
        bits = c.sb("s_bits", [P, S], I32)
        posn = c.sb("s_posn", [P, LO_N + HI_N])
        tmp = [c.sb(f"s_t{n}", [P, S]) for n in range(16)]
        LN = LO_N + HI_N
        mag = c.sb("s_mag", [P, S, LN])
        ang = c.sb("s_ang", [P, S, LN])
        angc = c.sb("s_angc", [P, S, LN])
        kk = c.sb("s_kk", [P, S, LN])
        kk2 = c.sb("s_kk2", [P, S, LN])
        low = c.sb("s_low", [P, S, LO_N])
        gco = c.sb("s_gco", [P, S, HI_N])
        gtm = c.sb("s_gtm", [P, S, HI_N])
        ks = c.sb("s_ks", [HI_N, S, LO_N])
        d16 = c.sb("s_d16", [1, S])
        zer = c.sb("s_zer", [S, P])
        ints, posi, spos, invf, nw = (g[n] for n in ("ints", "posi", "spos", "invf", "nw"))
        pk = c.ps("s_pk", [HI_N, S, LO_N])

        in_l = c.sem("setup_lengths_in")
        in_k, in_m, zero_in = c.sem("setup_kernel_in"), c.sem("setup_masks_in"), c.sem("setup_zeros")
        link, act_done, pe_done = c.sem("setup_dve_chain"), c.sem("setup_act_done"), c.sem("setup_pe_done")
        dve_ready, k_out, res_in = c.sem("setup_dve_ready"), c.sem("setup_k_out"), c.sem("setup_resid_in")

        with nc.Block() as block:
            @block.sync
            def _(sp):
                for dst, src in ((two[:, S:2 * S], "logA2"), (ai2[:], "Aim2"), (cre[:], "Cre2"), (cim[:], "Cim2")):
                    sp.dma_start(dst, d[src]).then_inc(in_k, 16)
                sp.dma_start(sgn[:], d["signs"]).then_inc(in_k, 16)
                sp.dma_start(posn[:], d["positions"]).then_inc(in_k, 16)
                sp.dma_start(two[:, 0:S], d["L0_cond_log_dt"].rearrange("(a s) -> a s", a=1).to_broadcast([P, S])).then_inc(in_k, 16)
                sp.dma_start(d16[:], d["L0_cond_D"].rearrange("(a s) -> a s", a=1)).then_inc(in_k, 16)
                sp.dma_start(g["cols"][:], d["cols"]).then_inc(in_l, 16)
                sp.dma_start(ints[:, 0, :], d["itok_B_78_3631"].rearrange("(a s) -> a s", a=1).to_broadcast([P, B])).then_inc(in_l, 16)
                sp.dma_start(posi[:], d["posbase"]).then_inc(in_m, 16)
                sp.dma_start(spos[:], d["seqpos"]).then_inc(in_m, 16)
                sp.dma_start(invf[:], d["inv_freq"]).then_inc(in_m, 16)
                for n, src in enumerate(("itok_B_207_1644", "itok_B_3_7", "itok_B_0_4"), start=1):
                    sp.dma_start(ints[:, n, :], d[src].rearrange("(a s) -> a s", a=1).to_broadcast([P, B])).then_inc(in_m, 16)
                for n, src in enumerate(("L1_cond_q_norm_w", "L1_cond_k_norm_w")):
                    sp.dma_start(nw[:, n, :], d[src].rearrange("(a s) -> a s", a=1).to_broadcast([P, D])).then_inc(in_m, 16)
                for dst, src in ((g["ident"], "ident"), (g["keyidx"], "keyidx")):
                    sp.dma_start(dst[:], d[src]).then_inc(in_m, 16)
                sp.dma_start(g["bt"][:], d["itok_Bx16_0_63"].rearrange("b (o n) -> o (b n)", o=1)).then_inc(in_m, 16)
                for q in range(NPP // VCH):
                    sp.dma_start(g["vpage"][q * PSIZE:(q + 1) * PSIZE, :], d["vpages"][q:q + 1, :].to_broadcast([PSIZE, B * VCH])).then_inc(in_m, 16)
                sp.dma_start(g["vec"][:, 0:d["vectors"].shape[1]], d["vectors"]).then_inc(in_m, 16)
                sp.dma_start(g["resid"][:], d["xT"]).then_inc(res_in, 16)
                sp.wait_ge(zero_in, 1)
                sp.dma_start(g["kpad"][:, 0:P], zer[:]).then_inc(k_out, 16)
                sp.wait_ge(dve_ready, 3)
                sp.dma_start(g["kpad"][:, P:KPAD].rearrange("s (a c) -> a s c", c=LO_N), ks[:]).then_inc(k_out, 16)
                sp.wait_ge(k_out, 32)
                sp.wait_ge(res_in, 16)
                sp.wait_ge(in_m, 16 * 16)

            @block.gpsimd
            def _(pool):
                nc.gpsimd.memset(zer[:], 0.0).then_inc(zero_in, 1)

            @block.scalar
            def _(act):
                act.wait_ge(dve_ready, 1)
                nc.scalar.activation(mag[:], mag[:], ACT.Exp).then_inc(act_done, 1)
                nc.scalar.activation(kk[:], ang[:], ACT.Sin)
                nc.scalar.activation(kk2[:], angc[:], ACT.Sin)
                nc.scalar.activation(tmp[7][:], tmp[5][:], ACT.Sin)
                nc.scalar.activation(tmp[8][:], tmp[6][:], ACT.Sin).then_inc(act_done, 1)

            @block.vector
            def _(dve):
                count = [0]

                def chain(ins):
                    count[0] += 1
                    ins.then_inc(link, 1)
                    dve.wait_ge(link, count[0])

                tt, tsc, reduce_angle, cosine_angle = arithmetic(nc, chain)
                dt, nre, dre, dim = two_e[:, 0:S], two_e[:, S:2 * S], tmp[2], tmp[3]
                def exact_exp(out, x, k, r, bits):
                    tsc(r, x, -87.0, 88.0, ALU.max, ALU.min)
                    tsc(k, r, 1.0 / np.log(2.0), MAGIC, ALU.mult, ALU.add)
                    tsc(k, k, -MAGIC, 0.0, ALU.add, ALU.add)
                    for part in (LN2_1, LN2_2):
                        chain(nc.vector.scalar_tensor_tensor(r, k, -part, r, ALU.mult, ALU.add))
                    tsc(bits, k, 127.0, 2.0 ** 23, ALU.add, ALU.mult)
                    tsc(k, r, 1.0 / 5040, 1.0 / 720, ALU.mult, ALU.add)
                    for coef in (1.0 / 120, 1.0 / 24, 1.0 / 6, 0.5, 1.0, 1.0):
                        tt(k, k, r, ALU.mult)
                        tsc(k, k, coef, 0.0, ALU.add, ALU.add)
                    tt(out, k, bits.bitcast(F32), ALU.mult)

                dve.wait_ge(in_k, 16 * 8)
                exact_exp(two_e[:], two[:], two_k[:], two_r[:], two_b[:])
                chain(nc.vector.scalar_tensor_tensor(dre[:], nre, -1.0, dt, ALU.mult, ALU.mult))
                tt(dim[:], ai2[:], dt, ALU.mult)
                exact_exp(tmp[4][:], dre[:], tmp[9][:], tmp[10][:], bits[:])
                chain(nc.vector.tensor_copy(tmp[5][:], dim[:]))
                reduce_angle(tmp[5][:], tmp[9][:])
                cosine_angle(tmp[6][:], tmp[5][:], tmp[9][:])
                pb = posn[:].rearrange("p (o n) -> p o n", o=1).to_broadcast([P, S, LN])
                tt(mag[:], dre[:].rearrange("p (s o) -> p s o", o=1).to_broadcast([P, S, LN]), pb, ALU.mult)
                tt(ang[:], dim[:].rearrange("p (s o) -> p s o", o=1).to_broadcast([P, S, LN]), pb, ALU.mult)
                reduce_angle(ang[:], kk[:])
                cosine_angle(angc[:], ang[:], kk[:])
                dve.sem_inc(dve_ready, 1)
                dve.wait_ge(act_done, 2)
                sin_, cos_, e = tmp[7], tmp[8], tmp[4]
                nr, ni, q, den, cr, ci, al, be = (tmp[n] for n in (9, 10, 11, 12, 13, 14, 15, 5))
                tt(nr[:], e[:], cos_[:], ALU.mult)
                tsc(nr[:], nr[:], -1.0, 0.0, ALU.add, ALU.add)
                tt(ni[:], e[:], sin_[:], ALU.mult)
                tt(den[:], nre, nre, ALU.mult)
                tt(q[:], ai2[:], ai2[:], ALU.mult)
                tt(den[:], den[:], q[:], ALU.add)
                chain(nc.vector.reciprocal(den[:], den[:]))
                tt(cr[:], ni[:], ai2[:], ALU.mult)
                tt(q[:], nr[:], nre, ALU.mult)
                tt(cr[:], cr[:], q[:], ALU.subtract)
                tt(cr[:], cr[:], den[:], ALU.mult)
                tt(ci[:], ni[:], nre, ALU.mult)
                tt(q[:], nr[:], ai2[:], ALU.mult)
                tt(ci[:], ci[:], q[:], ALU.add)
                tt(ci[:], ci[:], den[:], ALU.mult)
                tsc(ci[:], ci[:], -1.0, 0.0, ALU.mult, ALU.add)
                tt(nr[:], cre[:], cr[:], ALU.mult)
                tt(q[:], cim[:], ci[:], ALU.mult)
                tt(nr[:], nr[:], q[:], ALU.subtract)
                tt(ni[:], cre[:], ci[:], ALU.mult)
                tt(q[:], cim[:], cr[:], ALU.mult)
                tt(ni[:], ni[:], q[:], ALU.add)
                tsc(al[:], nr[:], sgn[:, 0:1], None, ALU.mult, ALU.bypass)
                chain(nc.vector.scalar_tensor_tensor(al[:], ni[:], sgn[:, 1:2], al[:], ALU.mult, ALU.add))
                tsc(be[:], ni[:], sgn[:, 2:3], None, ALU.mult, ALU.bypass)
                chain(nc.vector.scalar_tensor_tensor(be[:], nr[:], sgn[:, 3:4], be[:], ALU.mult, ALU.add))
                hi_c, hi_s, hi_m = kk2[:, :, LO_N:], kk[:, :, LO_N:], mag[:, :, LO_N:]
                wide = [P, S, HI_N]
                tt(gco[:], hi_c, al[:].rearrange("p (s o) -> p s o", o=1).to_broadcast(wide), ALU.mult)
                tt(gtm[:], hi_s, be[:].rearrange("p (s o) -> p s o", o=1).to_broadcast(wide), ALU.mult)
                tt(gco[:], gco[:], gtm[:], ALU.add)
                tt(gco[:], gco[:], hi_m, ALU.mult)
                hp = P // 2
                tt(low[0:hp], kk2[0:hp, :, 0:LO_N], mag[0:hp, :, 0:LO_N], ALU.mult)
                chain(nc.vector.tensor_tensor(low[hp:P], kk[hp:P, :, 0:LO_N], mag[hp:P, :, 0:LO_N], ALU.mult))
                dve.sem_inc(dve_ready, 1)
                dve.wait_ge(pe_done, 1)
                chain(nc.vector.tensor_copy(ks[:], pk[:]))
                nc.vector.tensor_tensor(ks[0:1, :, 0], ks[0:1, :, 0], d16[:], ALU.add).then_inc(dve_ready, 1)
                dve.wait_ge(in_l, 32)
                chain(nc.vector.tensor_copy(g["lens"][:, 0, :], ints[:, 0, :]))
                for m in range(KT):
                    tsc(g["lmask"][:, m, :], g["lens"][:, 0, :], g["cols"][:, m:m + 1], None, ALU.is_gt, ALU.bypass)

            @block.tensor
            def _(pe):
                pe.wait_ge(dve_ready, 2)
                for s in range(S):
                    last = nc.tensor.matmul(pk[:, s, :], gco[:, s, :], low[:, s, :], start=True, stop=True)
                last.then_inc(pe_done, 1)


def rotary_angles(nc, d, g, chain):
    tt, tsc, reduce_angle, cosine_angle = arithmetic(nc, chain)
    fr, fk, fw = g["fr"], g["fk"], [P, TT, D // 2]
    chain(nc.vector.tensor_copy(g["lens"][:, 1:4, :], g["ints"][:, 1:4, :]))
    tsc(g["amask"][:], g["lens"][:, 2, :], g["cols"][:, 4:5], None, ALU.is_equal, ALU.bypass)
    for m in range(2):
        tsc(g["bmask"][:, m, :], g["lens"][:, 3, :], g["cols"][:, 5 + m:6 + m], 0.5, ALU.is_equal, ALU.mult)
    chain(nc.vector.tensor_copy(g["vpf"][:], g["vpage"][:]))
    tsc(g["vrow"][:], g["vpf"][:], float(PSIZE), g["cols"][:, 7:8], ALU.mult, ALU.add)
    chain(nc.vector.tensor_copy(g["posf"][:], g["posi"][:]))
    tt(g["posf"][:], g["posf"][:], g["spos"][:], ALU.add)
    tt(fr[:, 0], g["posf"][:].rearrange("p (t o) -> p t o", o=1).to_broadcast(fw),
       g["invf"][:].rearrange("p (o n) -> p o n", o=1).to_broadcast(fw), ALU.mult)
    reduce_angle(fr[:, 0], fk[:, 0])
    cosine_angle(fr[:, 1], fr[:, 0], fk[:, 1])


def rotary_tables(nc, d, g, chain):
    tt, tsc, _, _ = arithmetic(nc, chain)
    fk, nw, fw, hd = g["fk"], g["nw"], [P, TT, D // 2], D // 2
    for n in range(2):
        for half in range(2):
            w = nw[:, n, half * hd:(half + 1) * hd].rearrange("p (o n) -> p o n", o=1).to_broadcast(fw)
            tt(g["rope_c"][:, n, :, half * hd:(half + 1) * hd], fk[:, 1], w, ALU.mult)
            other = 1 - half
            tt(g["rope_s"][:, n, :, other * hd:(other + 1) * hd], fk[:, 0], w, ALU.mult)
        tsc(g["rope_s"][:, n, :, 0:hd], g["rope_s"][:, n, :, 0:hd], -1.0, 0.0, ALU.mult, ALU.add)


def conv_phase(nc, d, g):
    SG = 4
    steps = S // SG
    TZ, TP = 4, 2
    xh, xl = g["xh"], g["xl"]
    with ExitStack() as ctx:
        c = Core(nc, ctx)
        xr = c.sb("c_xr", [P, S, KT, B])
        rh, rl = c.sb("c_rh", [P, S, KT, B], F32R), c.sb("c_rl", [P, S, KT, B], F32R)
        tz = [c.sb(f"c_tz{n}", [P, SG, H]) for n in range(TZ)]
        th = [c.sb(f"c_th{n}", [P, SG, H], F32R) for n in range(TP)]
        tl = [c.sb(f"c_tl{n}", [P, SG, H], F32R) for n in range(TP)]
        y = [c.sb(f"c_y{n}", [P, SG, KT, B]) for n in range(2)]
        acc = [c.ps(f"c_acc{n}", [P, SG, KT, B]) for n in range(2)]
        x_in, x_in2, x_hi, x_lo = (c.sem(f"conv_{n}") for n in ("x_in", "x_in2", "x_hi", "x_lo"))
        t_in = [c.sem(f"conv_t_in{n}") for n in range(TZ)]
        t_hi, t_lo, done, masked, split = (c.sem(f"conv_{n}") for n in ("t_hi", "t_lo", "done", "masked", "split"))
        with nc.Block() as block:
            @block.sync
            def _(sp):
                def load(t):
                    win = bass.AP(tensor=g["kpad"].tensor, offset=g["kpad"].offset + t * SG * KPAD + 1,
                                  ap=[[1, P], [KPAD, SG], [1, H]])
                    sp.dma_start(tz[t % TZ][:], win).then_inc(t_in[t % TZ], 16)

                load(0)
                sp.dma_start(xr[:, 0:S // 2], d["x_rev"][:, 0:S // 2]).then_inc(x_in, 16)
                load(1)
                sp.dma_start(xr[:, S // 2:S], d["x_rev"][:, S // 2:S]).then_inc(x_in2, 16)
                for t in range(2, steps):
                    if t >= TZ:
                        sp.wait_ge(t_lo, t - TZ + 1)
                        sp.wait_ge(split, t - TZ + 1)
                    load(t)

            def high_part(act, t):
                act.wait_ge(t_in[t % TZ], 16 * (t // TZ + 1))
                if t >= TP:
                    act.wait_ge(done, t - TP + 1)
                nc.scalar.activation(th[t % TP][:], tz[t % TZ][:], ACT.Copy).then_inc(t_hi, 1)

            @block.scalar
            def _(act):
                high_part(act, 0)
                for n, arrived in enumerate((x_in, x_in2)):
                    part = slice(n * S // 2, (n + 1) * S // 2)
                    act.wait_ge(arrived, 16)
                    nc.scalar.activation(rh[:, part], xr[:, part], ACT.Copy).then_inc(x_hi, 1)
                    high_part(act, n + 1)
                for t in range(3, steps):
                    high_part(act, t)

            @block.gpsimd
            def _(pool):
                for t in range(steps):
                    pool.wait_ge(t_hi, t + 1)
                    nc.gpsimd.tensor_tensor(tl[t % TP][:, 0:2], tz[t % TZ][:, 0:2], f32(th[t % TP][:, 0:2]), ALU.subtract).then_inc(t_lo, 1)

            @block.vector
            def _(dve):
                mask = g["lmask"][:].rearrange("p (o m) b -> p o m b", o=1).to_broadcast([P, SG, KT, B])

                def low_half(t):
                    dve.wait_ge(t_hi, t + 1)
                    nc.vector.tensor_tensor(tl[t % TP][:, 2:4], tz[t % TZ][:, 2:4], f32(th[t % TP][:, 2:4]), ALU.subtract).then_inc(split, 1)

                low_half(0)
                for n in range(2):
                    part = slice(n * S // 2, (n + 1) * S // 2)
                    dve.wait_ge(x_hi, n + 1)
                    nc.vector.tensor_tensor(rl[:, part], xr[:, part], f32(rh[:, part]), ALU.subtract).then_inc(x_lo, 1)
                    low_half(n + 1)
                for t in range(steps):
                    if t + 2 < steps and t >= 1:
                        low_half(t + 2)
                    dve.wait_ge(done, t + 1)
                    yo = y[t % 2]
                    nc.vector.tensor_tensor(yo[:], acc[t % 2][:], mask, ALU.mult).then_inc(masked, 1)
                    dve.wait_ge(masked, 3 * t + 1)
                    ys = yo[:].rearrange("p s m b -> p m s b")
                    hi = xh[:, :, t * SG * B:(t + 1) * SG * B].rearrange("p m (s b) -> p m s b", b=B)
                    lo = xl[:, :, t * SG * B:(t + 1) * SG * B].rearrange("p m (s b) -> p m s b", b=B)
                    nc.vector.tensor_copy(hi, ys).then_inc(masked, 1)
                    dve.wait_ge(masked, 3 * t + 2)
                    nc.vector.tensor_tensor(lo, ys, f32(hi), ALU.subtract).then_inc(masked, 1)

            @block.tensor
            def _(pe):
                for t in range(steps):
                    pe.wait_ge(x_lo, 1 if t < steps // 2 else 2)
                    pe.wait_ge(t_lo, t + 1)
                    pe.wait_ge(split, t + 1)
                    if t >= 2:
                        pe.wait_ge(masked, 3 * (t - 2) + 1)
                    for s in range(SG):
                        for dd in range(KT):
                            n = KT - dd
                            out = acc[t % 2][:, s, dd:KT, :]
                            w_hi, w_lo = (m[t % TP][:, s, dd * P:(dd + 1) * P] for m in (th, tl))
                            x_h, x_l = (m[:, t * SG + s, 0:n, :] for m in (rh, rl))
                            last = three_passes(nc, out, w_hi, w_lo, x_h, x_l, dd == 0, dd == KT - 1)
                    last.then_inc(done, 1)


class WeightSlots:
    def __init__(self, c, tag, cols, ternary_only=False):
        self.raw = [c.sb(f"{tag}_raw{n}", [P, cols]) for n in range(2)]
        self.hi = [c.sb(f"{tag}_hi{n}", [P, cols], F32R) for n in range(2)]
        self.lo = [self.raw[n] if ternary_only else c.sb(f"{tag}_lo{n}", [P, cols], F32R) for n in range(2)]


class WeightStream:
    def __init__(self, nc, c, tag, slots, w_dram, cols, n_k, unroll, thresholds=None):
        self.nc, self.w_dram, self.n_k, self.unroll = nc, w_dram, n_k, unroll
        self.per = unroll // 2
        self.raw, self.hi, self.lo = ([x[:, 0:cols] for x in part] for part in (slots.raw, slots.hi, slots.lo))
        self.thresholds = thresholds
        self.sign = c.sb(f"{tag}_sign", [P, H]) if thresholds else None
        self.w_in = [c.sem(f"{tag}_w_in{n}") for n in range(2)]
        self.w_hi, self.w_ready, self.used = (c.sem(f"{tag}_{n}") for n in ("w_hi", "w_ready", "used"))
        self.ahead = False

    def load(self, sp, t, u, i):
        if not early(t, 2):
            sp.wait_ge(self.w_ready, self.ready(t - 2))
        sp.dma_start(self.raw[u % 2], self.w_dram[at(t)].rearrange("o p m -> (o p) m")).then_inc(self.w_in[u % 2], 16)

    def high_part(self, act, t, u, i):
        act.wait_ge(self.w_in[u % 2], 16 * (i * self.per + u // 2 + 1))
        if not early(t, 2):
            act.wait_ge(self.used, t - 1)
        self.nc.scalar.activation(self.hi[u % 2], self.raw[u % 2], ACT.Copy).then_inc(self.w_hi, 1)

    def low_part(self, pool, t, u, i):
        pool.wait_ge(self.w_hi, t + 1)
        self.nc.gpsimd.tensor_tensor(self.lo[u % 2], self.raw[u % 2], f32(self.hi[u % 2]), ALU.subtract).then_inc(self.w_ready, 1)

    def to_ternary(self, dve, t, u, i):
        parts = len(self.thresholds)
        dve.wait_ge(self.w_in[u % 2], 16 * (i * self.per + u // 2 + 1))
        if not early(t, 2):
            dve.wait_ge(self.used, t - 1)
        for n, (above, below) in enumerate(self.thresholds):
            cols = slice(n * H, (n + 1) * H)
            raw, sign = self.raw[u % 2][:, cols], self.sign[:]
            if n:
                dve.wait_ge(self.w_ready, parts * t + n)
            self.nc.vector.tensor_scalar(sign, raw, below, None, ALU.is_lt, ALU.bypass).then_inc(self.w_hi, 1)
            dve.wait_ge(self.w_hi, parts * t + (n + 1))
            self.nc.vector.scalar_tensor_tensor(self.hi[u % 2][:, cols], raw, above, sign, ALU.is_gt, ALU.subtract).then_inc(self.w_ready, 1)
        dve.wait_ge(self.w_ready, parts * t + parts)

    def ready(self, t):
        return t + 1 if not self.thresholds else len(self.thresholds) * (t + 1)

    def run(self, eng, step):
        run_steps(eng, self.n_k, self.unroll, lambda t, u, i: None if self.ahead and early(t, 2) else step(eng, t, u, i))

    def ahead_load(self, sp):
        for t in range(2):
            self.load(sp, t, t, 0)
        self.ahead = True

    def ahead_high(self, act):
        for t in range(2):
            self.high_part(act, t, t, 0)

    def ahead_low(self, pool):
        for t in range(2):
            self.low_part(pool, t, t, 0)

    def ahead_ternary(self, dve):
        for t in range(2):
            self.to_ternary(dve, t, t, 0)


def gate_up_phase(nc, d, g, hh, hl, tag, w, func, gate_scale, up_scale, following, gate_room, vector_first=None, scalar_last=None):
    xh, xl = g["xh"], g["xl"]
    W = KT * P
    ternary = w.thresholds
    with ExitStack() as ctx:
        c = Core(nc, ctx)
        sg = [gate_room[:, n * TOK:(n + 1) * TOK] for n in range(2)]
        hf = gate_room[:, 2 * TOK:3 * TOK]
        acc = [c.ps(f"{tag}_acc{n}", [P, 2, TOK]) for n in range(2)]
        gated, h_full, h_done = (c.sem(f"{tag}_{n}") for n in ("gated", "h_full", "h_done"))
        link, first_done = c.sem(f"{tag}_dve_chain"), c.sem(f"{tag}_first_done")
        with nc.Block() as block:
            @block.sync
            def _(sp):
                w.run(sp, w.load)
                following.ahead_load(sp)

            @block.scalar
            def _(act):
                def gate(t, u, i):
                    act.wait_ge(w.used, t + 1)
                    if not early(t, 2):
                        act.wait_ge(h_full, t - 1)
                    nc.scalar.activation(sg[u], acc[u][:, 0, :], func, scale=gate_scale(t)).then_inc(gated, 1)

                def step(t, u, i):
                    if not ternary:
                        if early(t, 1):
                            if not w.ahead:
                                w.high_part(act, 0, 0, 0)
                                w.high_part(act, 1, 1, 0)
                        elif not isinstance(t, int):
                            w.high_part(act, t + 1, 1 - u, i if u == 0 else i + 1)
                        elif t + 1 < IT:
                            w.high_part(act, t + 1, 1 - u, (t + 1) // 2)
                        else:
                            following.ahead_high(act)
                    gate(t, u, i)

                run_steps(act, IT, 2, step)
                if scalar_last:
                    act.wait_ge(first_done, 1)
                    scalar_last()

            @block.gpsimd
            def _(pool):
                if not ternary:
                    w.run(pool, w.low_part)
                    following.ahead_low(pool)

            @block.vector
            def _(dve):
                def hidden(t, u, i):
                    dve.wait_ge(gated, t + 1)
                    nc.vector.scalar_tensor_tensor(hf, acc[u][:, 1, :], up_scale(t), sg[u], ALU.mult, ALU.mult).then_inc(h_full, 1)
                    dve.wait_ge(h_full, t + 1)
                    th, tl = (m[:, at(t), :].rearrange("p o n -> p (o n)") for m in (hh, hl))
                    nc.vector.tensor_copy(th, hf).then_inc(h_done, 1)
                    dve.wait_ge(h_done, 2 * t + 1)
                    nc.vector.tensor_tensor(tl, hf, f32(th), ALU.subtract).then_inc(h_done, 1)
                    dve.wait_ge(h_done, 2 * t + 2)

                def step(t, u, i):
                    if ternary:
                        if early(t, 1):
                            if not w.ahead:
                                w.to_ternary(dve, 0, 0, 0)
                                w.to_ternary(dve, 1, 1, 0)
                        elif not isinstance(t, int):
                            w.to_ternary(dve, t + 1, 1 - u, i if u == 0 else i + 1)
                        elif t + 1 < IT:
                            w.to_ternary(dve, t + 1, 1 - u, (t + 1) // 2)
                        else:
                            following.ahead_ternary(dve)
                    hidden(t, u, i)

                if vector_first:
                    count = [0]

                    def chain(ins):
                        count[0] += 1
                        ins.then_inc(link, 1)
                        dve.wait_ge(link, count[0])

                    vector_first(chain)
                    dve.sem_inc(first_done, 1)
                run_steps(dve, IT, 2, step)

            @block.tensor
            def _(pe):
                def product(t, u, i):
                    pe.wait_ge(w.w_ready, w.ready(t))
                    if not early(t, 2):
                        pe.wait_ge(h_full, t - 1)
                    for n in range(2):
                        for k in range(KT):
                            cols = slice(n * W + k * P, n * W + (k + 1) * P)
                            for half in range(2):
                                out = acc[u][:, n, half * HALF:(half + 1) * HALF]
                                x_h, x_l = (m[:, k, half * HALF:(half + 1) * HALF] for m in (xh, xl))
                                if ternary:
                                    nc.tensor.matmul(out, w.hi[u][:, cols], x_h, start=k == 0, stop=False)
                                    last = nc.tensor.matmul(out, w.hi[u][:, cols], x_l, start=False, stop=k == KT - 1)
                                else:
                                    last = three_passes(nc, out, w.hi[u][:, cols], w.lo[u][:, cols], x_h, x_l, k == 0, k == KT - 1)
                    last.then_inc(w.used, 1)

                run_steps(pe, IT, 2, product)


def accumulate_phase(nc, d, g, tag, w, moving, finish, produce=None, load_extra=None, first=None, vector_first=None,
                     side=None, store=None, following=None):
    n_k, unroll, ternary = w.n_k, w.unroll, w.thresholds
    with ExitStack() as ctx:
        c = Core(nc, ctx)
        acc = c.ps(f"{tag}_acc", [P, KT, TOK])
        made, sums, whole_done, high_done, low_done, low_done_g = (
            c.sem(f"{tag}_{n}") for n in ("made", "sums", "whole_done", "high_done", "low_done", "low_done_gpsimd"))
        stored, link = c.sem(f"{tag}_stored"), c.sem(f"{tag}_dve_chain")
        low_on_gpsimd = [m for m in range(KT) if finish.low and finish.whole and m % 2]

        with nc.Block() as block:
            @block.sync
            def _(sp):
                def step(t, u, i):
                    if not (w.ahead and early(t, 2)):
                        w.load(sp, t, u, i)
                    if load_extra:
                        load_extra(sp, t, u, i, made)

                run_steps(sp, n_k, unroll, step)
                if following:
                    following.ahead_load(sp)
                if store:
                    for m in range(KT):
                        sp.wait_ge(whole_done, m + 1)
                        store(sp, m).then_inc(stored, 16)
                    sp.wait_ge(stored, 16 * KT)

            @block.scalar
            def _(act):
                if not ternary:
                    w.run(act, w.high_part)
                if following:
                    following.ahead_high(act)
                if finish.high:
                    for m in range(KT):
                        if finish.whole:
                            act.wait_ge(whole_done, m + 1)
                        else:
                            act.wait_ge(sums, m + 1)
                        finish.high(m, acc[:, m, :]).then_inc(high_done, 1)

            @block.gpsimd
            def _(pool):
                if not ternary:
                    w.run(pool, w.low_part)
                if following:
                    following.ahead_low(pool)
                for m in low_on_gpsimd:
                    pool.wait_ge(high_done, m + 1)
                    finish.low(nc.gpsimd, m, acc[:, m, :]).then_inc(low_done_g, 1)

            @block.vector
            def _(dve):
                def make(t, u, i):
                    if not early(t, 2):
                        dve.wait_ge(w.used, t - 1)
                    produce(dve, t, u, i, made)

                if ternary:
                    w.run(dve, w.to_ternary)
                count = [0]

                def chain(ins):
                    count[0] += 1
                    ins.then_inc(link, 1)
                    dve.wait_ge(link, count[0])

                if vector_first:
                    vector_first(chain)
                if produce:
                    run_steps(dve, n_k, unroll, make)
                if side:
                    run_steps(dve, n_k, unroll, lambda t, u, i: side(dve, t, u, i))

                def low(m):
                    if finish.low and m not in low_on_gpsimd:
                        dve.wait_ge(high_done, m + 1)
                        finish.low(nc.vector, m, acc[:, m, :]).then_inc(low_done, 1)

                for m in range(KT):
                    if finish.whole:
                        dve.wait_ge(sums, m + 1)
                        finish.whole(m, acc[:, m, :]).then_inc(whole_done, 1)
                        if m:
                            low(m - 1)
                    else:
                        low(m)
                if finish.whole:
                    low(KT - 1)

            @block.tensor
            def _(pe):
                if first:
                    first(pe, acc)

                def product(t, u, i):
                    pe.wait_ge(w.w_ready, w.ready(t))
                    if produce:
                        pe.wait_ge(made, 2 * t + 2)
                    opens = isinstance(t, int) and t == 0 and not first
                    closes = isinstance(t, int) and t == n_k - 1
                    for m in range(KT):
                        cols = slice(m * P, (m + 1) * P)
                        for half in range(2):
                            out = acc[:, m, half * HALF:(half + 1) * HALF]
                            x_h, x_l = moving(t, u, i, half)
                            if ternary:
                                nc.tensor.matmul(out, w.hi[u % 2][:, cols], x_h, start=opens, stop=False)
                                last = nc.tensor.matmul(out, w.hi[u % 2][:, cols], x_l, start=False, stop=closes)
                            else:
                                last = three_passes(nc, out, w.hi[u % 2][:, cols], w.lo[u % 2][:, cols], x_h, x_l, opens, closes)
                        if closes:
                            last.then_inc(sums, 1)
                    if not closes:
                        last.then_inc(w.used, 1)

                run_steps_closing(pe, n_k, unroll, product)


def run_steps_closing(eng, n, unroll, step):
    if n % unroll or n <= 2 * unroll:
        run_steps(eng, n, unroll, step)
        return
    whole = n // unroll
    for u in range(unroll):
        step(u, u, 0)
    with eng.Fori(1, whole - 1) as i:
        for u in range(unroll):
            step(i * unroll + u, u, i)
    for u in range(unroll):
        step((whole - 1) * unroll + u, u, whole - 1)


class Finish:
    def __init__(self, whole=None, high=None, low=None):
        self.whole, self.high, self.low = whole, high, low


def split_sums(nc, g):
    xh, xl = g["xh"], g["xl"]
    return Finish(high=lambda m, acc: nc.scalar.activation(xh[:, m, :], acc, ACT.Copy),
                  low=lambda eng, m, acc: eng.tensor_tensor(xl[:, m, :], acc, f32(xh[:, m, :]), ALU.subtract))


def onto_residual(nc, g, scalar, batch_major=True, split=True):
    resid, xh, xl = g["resid"], g["xh"], g["xl"]

    def whole(m, acc):
        r = resid[:, m, :]
        if not batch_major:
            r, acc = r.rearrange("p (b s) -> p s b", b=B), acc.rearrange("p (s b) -> p s b", b=B)
        return nc.vector.scalar_tensor_tensor(r, acc, scalar(m), r, ALU.mult, ALU.add)

    if not split:
        return Finish(whole=whole)
    return Finish(whole=whole, high=lambda m, acc: nc.scalar.activation(xh[:, m, :], resid[:, m, :], ACT.Copy),
                  low=lambda eng, m, acc: eng.tensor_tensor(xl[:, m, :], resid[:, m, :], f32(xh[:, m, :]), ALU.subtract))


def resident(hi, lo):
    def moving(t, u, i, half):
        cols = slice(half * HALF, (half + 1) * HALF)
        if isinstance(t, int):
            return hi[:, t, cols], lo[:, t, cols]
        return tuple(m[:, at(t), cols].rearrange("p o n -> p (o n)") for m in (hi, lo))
    return moving


def project_phase(nc, d, g):
    xh, xl = g["xh"], g["xl"]
    W = REP * D
    V_GROUPS = HK // REP
    n_groups = GROUPS + V_GROUPS
    NQ = GROUPS * TT
    NV = V_GROUPS * TT
    ACC = 4
    with ExitStack() as ctx:
        c = Core(nc, ctx)
        raw = [c.sb(f"q_raw{n}", [P, KT, W]) for n in range(2)]
        wh = [c.sb(f"q_wh{n}", [P, KT, W], F32R) for n in range(2)]
        wl = [c.sb(f"q_wl{n}", [P, KT, W], F32R) for n in range(2)]
        sq = c.sb("q_sq", [P, REP, D])
        ss, rt, rs = ([c.sb(f"q_{x}{n}", [P, REP]) for n in range(2)] for x in ("ss", "rt", "rs"))
        qn, qc, qs, qr = ([c.sb(f"q_{x}{n}", [P, REP, D]) for n in range(2)] for x in ("qn", "qc", "qs", "qr"))
        st = [c.sb(f"q_st{n}", [P, BPT, REP, S]) for n in range(2)]
        vs = [c.sb(f"q_vs{n}", [P, W]) for n in range(2)]
        eps = c.sb("q_eps", [P, 1])
        acc = [c.ps(f"q_acc{n}", [P, REP, D]) for n in range(ACC)]
        tp = [c.ps(f"q_tp{n}", [P, REP, P]) for n in range(2)]
        p_tot = c.ps("q_ptot", [P, 4])
        tot, ones = c.sb("q_tot", [P, 3]), c.sb("q_ones", [P, P])
        row_sums, totals, link = c.sem("qkv_row_sums"), c.sem("qkv_totals"), c.sem("qkv_chain")
        w_in = [c.sem(f"qkv_w_in{n}") for n in range(2)]
        w_hi, w_ready = c.sem("qkv_w_hi"), c.sem("qkv_w_ready")
        done, squared, summed, rooted, inverse, normed, cosed, sined, rotated, turned, staged, eps_set, v_staged = (
            c.sem(f"qkv_{n}") for n in ("done", "squared", "summed", "rooted", "inverse", "normed", "cosed", "sined",
                                        "rotated", "turned", "staged", "eps_set", "v_staged"))
        stored = [c.sem(f"qkv_stored{n}") for n in range(2)]
        v_stored = [c.sem(f"qkv_v_stored{n}") for n in range(2)]

        def rotary_steps(eng, step):
            for slot in range(2):
                for tile in range(TT):
                    step(slot, slot, tile, slot * TT + tile, 0)
            with eng.Fori(1, HK // 2) as i:
                for slot in range(2):
                    for tile in range(TT):
                        step(i * 2 + slot, slot, tile, i * (2 * TT) + (slot * TT + tile), 0)
            for grp in range(HK, GROUPS):
                for tile in range(TT):
                    step(grp, grp % 2, tile, grp * TT + tile, 1)

        with nc.Block() as block:
            @block.sync
            def _(sp):
                def load(grp, slot):
                    sp.dma_start(raw[slot][:], d["w1_qkv"][at(grp)].rearrange("o p (k m) -> (o p) k m", k=KT)).then_inc(w_in[slot], 16)

                load(0, 0)
                load(1, 1)

                def step(grp, slot, tile, n, table):
                    if tile == 1 and not (isinstance(grp, int) and grp + 2 >= n_groups):
                        sp.wait_ge(w_ready, (grp + 1) * KT)
                        load(grp + 2, slot)
                    u = tile % 2
                    sp.wait_ge(staged, n + 1)
                    dst = g["qk_scr"][tile * BPT:(tile + 1) * BPT, :, at(grp), :].rearrange("b p o r -> p b (o r)")
                    sp.dma_start(dst, st[u][:].rearrange("p b r s -> p b (r s)")).then_inc(stored[u], 16)

                rotary_steps(sp, step)
                for n in range(NV):
                    grp, tile = divmod(n, TT)
                    sp.wait_ge(v_staged, n + 1)
                    sp.dma_start(g["v_scr"][tile * P:(tile + 1) * P, grp * W:(grp + 1) * W], vs[n % 2][:]).then_inc(v_stored[n % 2], 16)
                for u in range(2):
                    sp.wait_ge(stored[u], 16 * (NQ // 2))
                    sp.wait_ge(v_stored[u], 16 * (NV // 2))

            def weight_piece(grp, tile):
                return tile - 1 if 1 <= tile <= KT and not (isinstance(grp, int) and grp + 1 >= n_groups) else None

            @block.gpsimd
            def _(pool):
                def low_part(grp, slot, k):
                    pool.wait_ge(w_hi, grp * KT + k + 1)
                    nc.gpsimd.tensor_tensor(wl[slot][:, k], raw[slot][:, k], f32(wh[slot][:, k]), ALU.subtract).then_inc(w_ready, 1)

                def step(grp, slot, tile, n, table):
                    u = tile % 2
                    pool.wait_ge(normed, n + 1)
                    if not early(n, 2):
                        pool.wait_ge(rotated, n - 1)
                    tab = g["rope_c"][:, table, tile, :].rearrange("p (o n) -> p o n", o=1).to_broadcast([P, REP, D])
                    nc.gpsimd.tensor_tensor(qc[u][:], qn[u][:], tab, ALU.mult).then_inc(cosed, 1)
                    k = weight_piece(grp, tile)
                    if k is not None:
                        low_part(grp + 1, 1 - slot, k)

                for k in range(KT):
                    low_part(0, 0, k)
                rotary_steps(pool, step)
                for k in range(KT):
                    low_part(n_groups - 1, 1, k)

            @block.scalar
            def _(act):
                act.wait_ge(eps_set, 1)

                def high_part(grp, slot, k):
                    if k == 0:
                        act.wait_ge(w_in[slot], (grp - slot) * 8 + 16)
                        if not early(grp, 2):
                            act.wait_ge(done, (grp - 1) * TT)
                    nc.scalar.activation(wh[slot][:, k], raw[slot][:, k], ACT.Copy).then_inc(w_hi, 1)

                def evacuate(n, u):
                    act.wait_ge(turned, n + 1)
                    if not early(n, 2):
                        act.wait_ge(stored[u], (n - u) * 8)
                    nc.scalar.activation(st[u][:].rearrange("p b r s -> p r b s"),
                                         tp[u][:].rearrange("p r (b s) -> p r b s", b=BPT), ACT.Copy).then_inc(staged, 1)

                def step(grp, slot, tile, n, table):
                    u = tile % 2
                    act.wait_ge(done, n + 1)
                    if not early(n, 1):
                        act.wait_ge(summed, n)
                    nc.scalar.activation(sq[:], acc[tile % ACC][:], ACT.Square).then_inc(squared, 1)
                    if not early(n, 3):
                        evacuate(n - 3, 1 - u)
                    k = weight_piece(grp, tile)
                    if k is not None:
                        high_part(grp + 1, 1 - slot, k)
                    act.wait_ge(summed, n + 1)
                    if not early(n, 2):
                        act.wait_ge(inverse, n - 1)
                    nc.scalar.activation(rt[u][:], ss[u][:], ACT.Sqrt, bias=eps[:], scale=1.0 / D).then_inc(rooted, 1)

                for k in range(KT):
                    high_part(0, 0, k)
                rotary_steps(act, step)
                for n in range(NQ - 3, NQ):
                    evacuate(n, n % 2)
                for k in range(KT):
                    high_part(n_groups - 1, 1, k)
                for n in range(NV):
                    act.wait_ge(done, NQ + n + 1)
                    if n >= 2:
                        act.wait_ge(v_stored[n % 2], 16 * (n // 2))
                    nc.scalar.activation(vs[n % 2][:], acc[n % ACC][:].rearrange("p r d -> p (r d)"), ACT.Copy).then_inc(v_staged, 1)

            @block.vector
            def _(dve):
                nc.vector.memset(eps[:], RMS_EPS).then_inc(eps_set, 1)
                hd = D // 2
                count = [0]

                def chain(ins):
                    count[0] += 1
                    ins.then_inc(link, 1)
                    dve.wait_ge(link, count[0])

                chain(nc.vector.memset(ones[:], 1.0))
                chain(nc.vector.reduce_sum(tot[:], g["rows"][:].rearrange("p t n -> p n t"), AX_X))
                dve.sem_inc(row_sums, 1)
                dve.wait_ge(totals, 1)
                chain(nc.vector.tensor_scalar(g["scale3"][:], p_tot[:, 0:3], 1.0 / (INTER * H), None, ALU.mult, ALU.bypass))
                chain(nc.vector.tensor_scalar(g["thr3"][:, 0:3], g["scale3"][:], BIT_EPS, 0.5, ALU.add, ALU.mult))
                chain(nc.vector.tensor_scalar(g["thr3"][:, 3:6], g["thr3"][:, 0:3], -1.0, 0.0, ALU.mult, ALU.add))

                def add(n, u):
                    dve.wait_ge(cosed, n + 1)
                    dve.wait_ge(sined, 2 * n + 2)
                    if not early(n, 2):
                        dve.wait_ge(turned, n - 1)
                    nc.vector.tensor_tensor(qr[u][:], qc[u][:], qs[u][:], ALU.add).then_inc(rotated, 1)

                def step(grp, slot, tile, n, table):
                    u = tile % 2
                    dve.wait_ge(squared, n + 1)
                    if not early(n, 2):
                        dve.wait_ge(rooted, n - 1)
                    nc.vector.reduce_sum(ss[u][:], sq[:], AX_X).then_inc(summed, 1)
                    if not early(n, 1):
                        add(n - 1, 1 - u)
                    dve.wait_ge(rooted, n + 1)
                    nc.vector.reciprocal(rs[u][:], rt[u][:]).then_inc(inverse, 1)
                    dve.wait_ge(inverse, n + 1)
                    if not early(n, 2):
                        dve.wait_ge(cosed, n - 1)
                    nc.vector.tensor_tensor(qn[u][:], acc[tile % ACC][:], rs[u][:].rearrange("p (r o) -> p r o", o=1).to_broadcast([P, REP, D]),
                                            ALU.mult).then_inc(normed, 1)
                    dve.wait_ge(normed, n + 1)
                    if not early(n, 2):
                        dve.wait_ge(rotated, n - 1)
                    for half in range(2):
                        tab = g["rope_s"][:, table, tile, half * hd:(half + 1) * hd].rearrange("p (o n) -> p o n", o=1).to_broadcast([P, REP, hd])
                        nc.vector.tensor_tensor(qs[u][:, :, half * hd:(half + 1) * hd], qn[u][:, :, (1 - half) * hd:(2 - half) * hd],
                                                tab, ALU.mult).then_inc(sined, 1)

                rotary_steps(dve, step)
                add(NQ - 1, 1)

            @block.tensor
            def _(pe):
                pe.wait_ge(row_sums, 1)
                nc.tensor.matmul(p_tot[:, 0:3], ones[:], tot[:], start=True, stop=True).then_inc(totals, 1)

                def project(grp, slot, tile, n):
                    if tile == 0:
                        pe.wait_ge(w_ready, (grp + 1) * KT)
                    if not early(n, ACC):
                        if isinstance(n, int) and n >= NQ + ACC:
                            pe.wait_ge(v_staged, n - NQ - ACC + 1)
                        else:
                            pe.wait_ge(normed, n - ACC + 1)
                    for k in range(KT):
                        rows = slice(tile * P, (tile + 1) * P)
                        last = three_passes(nc, acc[tile % ACC][:].rearrange("p r d -> p (r d)"), xh[:, k, rows], xl[:, k, rows],
                                            wh[slot][:, k], wl[slot][:, k], k == 0, k == KT - 1)
                    last.then_inc(done, 1)

                def transpose(n, u):
                    pe.wait_ge(rotated, n + 1)
                    if not early(n, 2):
                        pe.wait_ge(staged, n - 1)
                    for r in range(REP):
                        last = nc.tensor.transpose(tp[u][:, r, :], qr[u][:, r, :], g["ident"][:])
                    last.then_inc(turned, 1)

                def step(grp, slot, tile, n, table):
                    project(grp, slot, tile, n)
                    if not early(n, 2):
                        transpose(n - 2, tile % 2)

                rotary_steps(pe, step)
                for n in range(NQ, NQ + NV):
                    project(n // TT, (n // TT) % 2, n % TT, n)
                    if n < NQ + 2:
                        transpose(n - 2, n % 2)


def attention_phase(nc, d, g):
    G = REP * S
    assert G == P
    with ExitStack() as ctx:
        c = Core(nc, ctx)
        bt, vrow = g["bt"], g["vrow"]
        kb = [c.sb(f"a_kb{n}", [P, NPP, HK, PSIZE]) for n in range(2)]
        vb = [c.sb(f"a_vb{n}", [P, VCH, HK * D]) for n in range(2)]
        qk = [c.sb(f"a_qk{n}", [P, GROUPS, G]) for n in range(2)]
        vn = [c.sb(f"a_vn{n}", [S, HK * D]) for n in range(2)]
        vidx = [c.sb(f"a_vidx{n}", [P, VCH], I32) for n in range(2)]
        mask = [c.sb(f"a_mask{n}", [P, KEYS]) for n in range(2)]
        length = [c.sb(f"a_length{n}", [P, 1]) for n in range(2)]
        ob = [c.sb(f"a_ob{n}", [P, HK, G]) for n in range(2)]
        sm, pr, pn = ([c.sb(f"a_{x}{n}", [P, KEYS]) for n in range(2)] for x in ("sm", "pr", "pn"))
        ptm, ptn = [c.sb(f"a_ptm{n}", [P, VCH, G]) for n in range(2)], [c.sb(f"a_ptn{n}", [S, G]) for n in range(2)]
        mx, den, rc = (c.sb(f"a_{x}", [P, 2]) for x in ("mx", "den", "rc"))
        sc = [c.ps(f"a_sc{n}", [P, 1024]) for n in range(2)]
        tpm = [c.ps(f"a_tpm{n}", [P, VCH, G]) for n in range(2)]
        tpn = c.ps("a_tpn", [S, 2, G])
        oo = c.ps("a_oo", [P, 2, G])
        rows_taken, length_taken = c.sem("att_rows_taken"), c.sem("att_length_taken")
        k_in, v_in, qk_in, vn_in, stored = ([c.sem(f"att_{x}{n}") for n in range(2)] for x in ("k_in", "v_in", "qk_in", "vn_in", "stored"))
        o_moved, gate_pool, gate_dve = (c.sem(f"att_{n}") for n in ("o_moved", "gate_pool", "gate_dve"))
        masked, scored, shifted, exped, inverse, normed, turned, moved_m, moved_n, mixed = (
            c.sem(f"att_{n}") for n in ("masked", "scored", "shifted", "exped", "inverse", "normed", "turned", "moved_m", "moved_n", "mixed"))
        NU = B * HK

        def unit_steps(eng, step, lag=0):
            for u in range(2 * HK):
                step(u, u // HK, u % HK, u)
            with eng.Fori(1, B // 2) as i:
                for u in range(2 * HK):
                    step(u, u // HK, u % HK, i * (2 * HK) + u)

        with nc.Block() as block:
            @block.sync
            def _(sp):
                def load(b, s, i):
                    pages = nc.values_load_multi_w_load_instructions(
                        bt[0:1, bass.ds(b * NPP, NPP)], engines=[mybir.EngineType.SP], min_val=0, max_val=PAGES - 1,
                        skip_runtime_bounds_check_because="the block table names pages of the cache")[1]
                    if not early(b, 2):
                        sp.wait_ge(mixed, (b - 1) * HK)
                    for j in range(NPP):
                        sp.dma_start(kb[s][:, j].rearrange("p h k -> p (h k)"),
                                     d["kT_pages"][bass.ds(pages[j], 1)].rearrange("o p f -> (o p) f")).then_inc(k_in[s], 16)
                    sp.dma_start(qk[s][:], g["qk_scr"][at(b)].rearrange("o p g r -> (o p) g r")).then_inc(qk_in[s], 16)
                    sp.dma_start(vn[s][:], g["v_scr"][bass.ds(b * S, S), :]).then_inc(vn_in[s], 16)

                def store(b, s):
                    sp.wait_ge(o_moved, (b + 1) * HK)
                    sp.dma_start(g["o_scr"][at(b)].rearrange("o p r -> (o p) r"), ob[s][:].rearrange("p h r -> p (h r)")).then_inc(stored[s], 16)

                load(0, 0, 0)
                load(1, 1, 0)
                with sp.Fori(1, B // 2) as i:
                    for s in range(2):
                        load(i * 2 + s, s, i)
                        store(i * 2 + (s - 2), s)
                for s in range(2):
                    store(B - 2 + s, s)
                    sp.wait_ge(stored[s], 16 * (B // 2))

            @block.gpsimd
            def _(pool):
                def take_rows(b, s):
                    nc.gpsimd.tensor_copy(vidx[s][:], vrow[:, bass.ds(b * VCH, VCH)]).then_inc(rows_taken, 1)
                    pool.wait_ge(rows_taken, b + 1)
                    pool.sem_inc(gate_pool, 1)

                def load_values(s, j):
                    nc.gpsimd.indirect_dma_start(vb[s][:, j, :], None, d["v_rows"],
                                                 bass.IndirectOffsetOnAxis(ap=vidx[s][:, j:j + 1], axis=0)).then_inc(v_in[s], 16)

                def batch(b, s, n0, prefetch):
                    for h in range(HK):
                        n, v = n0 + h, h % 2
                        if prefetch and h == 2:
                            pool.wait_ge(mixed, b * HK)
                            take_rows(b + 1, 1 - s)
                        pool.wait_ge(inverse, n + 1)
                        if not early(n, 2):
                            pool.wait_ge(turned, n - 1)
                        pool.sem_inc(gate_pool, 1)
                        nc.gpsimd.tensor_scalar(pn[v][:], pr[v][:], rc[:, v:v + 1], 1.0, ALU.mult, ALU.mult).then_inc(normed, 1)
                        if prefetch and 2 <= h < 2 + VCH:
                            load_values(1 - s, h - 2)

                for s in range(2):
                    take_rows(s, s)
                    for j in range(VCH):
                        load_values(s, j)
                batch(0, 0, 0, False)
                batch(1, 1, HK, True)
                with pool.Fori(1, B // 2 - 1) as i:
                    for s in range(2):
                        batch(i * 2 + s, s, i * (2 * HK) + s * HK, True)
                batch(B - 2, 0, NU - 2 * HK, True)
                batch(B - 1, 1, NU - HK, False)

            @block.scalar
            def _(act):
                def move_main(n, u):
                    act.wait_ge(turned, n + 1)
                    if not early(n, 2):
                        act.wait_ge(mixed, n - 1)
                    nc.scalar.activation(ptm[u][:], tpm[u][:], ACT.Copy).then_inc(moved_m, 1)

                def step(u, s, h, n):
                    act.wait_ge(shifted, n + 1)
                    if not early(n, 2):
                        act.wait_ge(normed, n - 1)
                    v = u % 2
                    nc.scalar.activation(pr[v][:], sm[v][:], ACT.Exp, bias=mx[:, v:v + 1], scale=-1.0,
                                         accum_out=den[:, v:v + 1]).then_inc(exped, 1)
                    if not early(n, 1):
                        move_main(n - 1, 1 - v)

                unit_steps(act, step)
                move_main(NU - 1, 1)

            @block.vector
            def _(dve):
                def move_out(n, v, s, h):
                    dve.wait_ge(mixed, n + 1)
                    if h == 0 and not early(n, 2 * HK):
                        dve.wait_ge(stored[s], (n - s * HK))
                    nc.vector.tensor_copy(ob[s][:, h, :], oo[:, v, :]).then_inc(o_moved, 1)

                def move_new(n, v):
                    dve.wait_ge(turned, n + 1)
                    if not early(n, 2):
                        dve.wait_ge(mixed, n - 1)
                    nc.vector.tensor_copy(ptn[v][:], tpn[:, v, :]).then_inc(moved_n, 1)

                def take_length(b, s):
                    nc.vector.tensor_copy(length[s][:], g["lens"][:, 1, at(b)]).then_inc(length_taken, 1)

                def make_mask(b, s):
                    dve.wait_ge(length_taken, b + 1)
                    if not early(b, 2):
                        dve.wait_ge(shifted, (b - 1) * HK)
                    dve.sem_inc(gate_dve, 1)
                    nc.vector.tensor_scalar(mask[s][:], g["keyidx"][:], length[s][:], NEG, ALU.is_ge, ALU.mult).then_inc(masked, 1)

                def step(u, s, h, n, i, more=True):
                    v = u % 2
                    if h == 0:
                        dve.wait_ge(masked, i * 2 + s + 1)
                    dve.wait_ge(scored, n + 1)
                    if not early(n, 2):
                        dve.wait_ge(exped, n - 1)
                    dve.sem_inc(gate_dve, 1)
                    nc.vector.tensor_tensor_reduce(out=sm[v][:], in0=sc[v][:, 0:KEYS], in1=mask[s][:], scale=-ATT_SCALE, scalar=3e38,
                                                   op0=ALU.add, op1=ALU.min, accum_out=mx[:, v:v + 1]).then_inc(shifted, 1)
                    dve.wait_ge(exped, n + 1)
                    if not early(n, 2):
                        dve.wait_ge(normed, n - 1)
                    nc.vector.reciprocal(rc[:, v:v + 1], den[:, v:v + 1]).then_inc(inverse, 1)
                    if not early(n, 2):
                        w = u - 2 if u >= 2 else u + 2 * HK - 2
                        move_out(n - 2, v, w // HK, w % HK)
                    if not early(n, 1):
                        move_new(n - 1, 1 - v)
                    if more and h == 4:
                        take_length(i * 2 + (s + 1), 1 - s)
                    if more and h == 5:
                        make_mask(i * 2 + (s + 1), 1 - s)

                take_length(0, 0)
                make_mask(0, 0)
                for u in range(2 * HK):
                    step(u, u // HK, u % HK, u, 0)
                with dve.Fori(1, B // 2 - 1) as i:
                    for u in range(2 * HK):
                        step(u, u // HK, u % HK, i * (2 * HK) + u, i)
                last = B // 2 - 1
                for u in range(2 * HK):
                    step(u, u // HK, u % HK, last * (2 * HK) + u, last, more=u < HK)
                move_out(NU - 2, 0, 1, HK - 2)
                move_new(NU - 1, 1)
                move_out(NU - 1, 1, 1, HK - 1)

            @block.tensor
            def _(pe):
                def score(n, u, s, h, i):
                    v = u % 2
                    if h == 0:
                        pe.wait_ge(k_in[s], (i + 1) * (16 * NPP))
                        pe.wait_ge(qk_in[s], (i + 1) * 16)
                    if not early(n, 2):
                        pe.wait_ge(shifted, n - 1)
                    new = qk[s][:, HK + h // REP, (h % REP) * S:(h % REP + 1) * S]
                    nc.tensor.matmul(sc[v][:, 0:CACHE].rearrange("p (j k) -> p j k", k=PSIZE), qk[s][:, h, :], kb[s][:, :, h, :], start=True, stop=True)
                    nc.tensor.matmul(sc[v][:, CACHE:KEYS], qk[s][:, h, :], new, start=True, stop=True).then_inc(scored, 1)

                def turn(n, u):
                    v = u % 2
                    pe.wait_ge(normed, n + 1)
                    if not early(n, 2):
                        pe.wait_ge(moved_m, n - 1)
                        pe.wait_ge(moved_n, n - 1)
                    for j in range(VCH):
                        nc.tensor.transpose(tpm[v][:, j, :], pn[v][:, j * P:(j + 1) * P], g["ident"][:])
                    nc.tensor.transpose(tpn[:, v, :], pn[v][:, CACHE:KEYS], g["ident"][:]).then_inc(turned, 1)

                def mix(n, u, s, h, i):
                    v = u % 2
                    if h == 0:
                        pe.wait_ge(v_in[s], (i + 1) * (16 * VCH))
                        pe.wait_ge(vn_in[s], (i + 1) * 16)
                    pe.wait_ge(moved_m, n + 1)
                    pe.wait_ge(moved_n, n + 1)
                    if not early(n, 2):
                        pe.wait_ge(o_moved, n - 1)
                    for j in range(VCH):
                        nc.tensor.matmul(oo[:, v, :], vb[s][:, j, h * D:(h + 1) * D], ptm[v][:, j, :], start=j == 0, stop=False)
                    nc.tensor.matmul(oo[:, v, :], vn[s][:, h * D:(h + 1) * D], ptn[v][:], start=False, stop=True).then_inc(mixed, 1)

                def step(u, n, i):
                    score(n, u, u // HK, u % HK, i)
                    if not early(n, 2):
                        w = u - 2 if u >= 2 else u + 2 * HK - 2
                        mix(n - 2, w, w // HK, w % HK, i if u >= 2 else i - 1)
                    if not early(n, 1):
                        turn(n - 1, u + 1)

                for u in range(2 * HK):
                    step(u, u, 0)
                with pe.Fori(1, B // 2) as i:
                    for u in range(2 * HK):
                        step(u, i * (2 * HK) + u, i)
                last = B // 2 - 1
                mix(NU - 2, 2 * HK - 2, 1, HK - 2, last)
                turn(NU - 1, 1)
                mix(NU - 1, 2 * HK - 1, 1, HK - 1, last)


def output_projection(nc, d, g, w, following):
    xh, xl = g["xh"], g["xl"]
    with ExitStack() as ctx:
        c = Core(nc, ctx)
        ring = [c.sb(f"wo_o{n}", [P, B, P]) for n in range(2)]
        mh, ml = ([c.sb(f"wo_{x}{n}", [P, TOK], F32R) for n in range(2)] for x in ("mh", "ml"))
        o_in = [c.sem(f"wo_o_in{n}") for n in range(2)]

        def load_extra(sp, t, u, i, made):
            if u % REP:
                return
            s = u // REP
            if not early(t, 2 * REP):
                sp.wait_ge(made, (t - REP) * 2)
            sp.dma_start(ring[s][:], g["o_scr"][:, :, bass.ds(t * S, P)].rearrange("b p r -> p b r")).then_inc(o_in[s], 16)

        def produce(dve, t, u, i, made):
            s, r = u // REP, u % REP
            if r == 0:
                dve.wait_ge(o_in[s], (i + 1) * 16)
            src = ring[s][:, :, r * S:(r + 1) * S]
            hi, lo = (m[u % 2][:].rearrange("p (b s) -> p b s", b=B) for m in (mh, ml))
            nc.vector.tensor_copy(hi, src).then_inc(made, 1)
            dve.wait_ge(made, t * 2 + 1)
            nc.vector.tensor_tensor(lo, src, f32(hi), ALU.subtract).then_inc(made, 1)

        def moving(t, u, i, half):
            cols = slice(half * HALF, (half + 1) * HALF)
            return mh[u % 2][:, cols], ml[u % 2][:, cols]

        accumulate_phase(nc, d, g, "wo", w, moving, split_sums(nc, g), produce=produce, load_extra=load_extra, following=following)


class LowRankWeights:
    PARTS = (("w2_b", KT * P), ("w3_la", KT * 2 * P), ("w3_wb", (KT + 2) * H))

    def __init__(self, nc, kept):
        self.hi = [kept.sb(f"lr_hi_{n}", [P, w], F32R) for n, w in self.PARTS]
        self.lo = [kept.sb(f"lr_lo_{n}", [P, w], F32R) for n, w in self.PARTS]
        self.fold_hi, self.fold_lo = kept.sb("lr_fold_hi", [P, H], F32R), kept.sb("lr_fold_lo", [P, H], F32R)

    def stage(self, c):
        self.a = c.sb("lr_a", [P, KT, P])
        self.fa = c.sb("lr_fa", [P, KT, 2 * P])
        self.wb = c.sb("lr_wb", [P, KT + 2, H])
        self.mixed = c.sb("lr_mixed", [P, 2, P])
        self.raw = [c.sb(f"lr_raw_{n}", [P, w]) for n, w in self.PARTS]
        self.fold_in = c.sem("lr_fold_in")
        self.part_in = [c.sem(f"lr_in_{n}") for n, w in self.PARTS]

    def load(self, sp, d):
        for dst, name in ((self.a, "w2_a"), (self.fa, "w2_fa"), (self.wb, "w2_wb")):
            sp.dma_start(dst[:], d[name]).then_inc(self.fold_in, 16)
        for n, (name, w) in enumerate(self.PARTS):
            sp.dma_start(self.raw[n][:], d[name].rearrange("p k c -> p (k c)")).then_inc(self.part_in[n], 16)

    def parts(self, n):
        k_tiles = KT + 2 if n == 2 else KT
        return tuple(x[n][:].rearrange("p (k c) -> p k c", k=k_tiles) for x in (self.hi, self.lo))


def route_phase(nc, d, g, w, sel_t, mb, eb, lr, probs, old_semaphores):
    E = EXPERTS
    xh, xl = g["xh"], g["xl"]
    with ExitStack() as ctx:
        c = Core(nc, ctx)
        lr.stage(c)
        gw, gb = c.sb("r_gw", [P, KT, E]), c.sb("r_gb", [P, E])
        gh, gl = c.sb("r_gh", [P, KT, E], F32R), c.sb("r_gl", [P, KT, E], F32R)
        z_t = c.sb("r_z_t", [E, TOK])
        z, eq, sel = (c.sb(f"r_{x}", [P, TT, E]) for x in ("z", "eq", "sel"))
        mx, taken = c.sb("r_mx", [P, TT]), c.sb("r_taken", [P, TT])
        pick_raw, pick = c.sb("r_pick_raw", [E, E, P]), c.sb("r_pick", [E, E, P], F32R)
        pz = c.ps("r_pz", [P, TT, E])
        ptr = c.ps("r_ptr", [E, TOK])
        pb = c.ps("r_pb", [P, 2, TOK])
        p_fold = c.ps("r_fold", [P, H])
        w_in, link, logits, chosen, turned, out, spread, copied = (
            c.sem(f"route_{n}") for n in ("w_in", "chain", "logits", "chosen", "turned", "out", "spread", "copied"))
        g_in = c.sem("route_g_in")
        gate_hi, gate_lo, products, moved = (c.sem(f"route_{n}") for n in ("gate_hi", "gate_lo", "products", "moved"))
        picks, part_hi, part_lo, mixing, weighted, folding, fold_hi, fold_lo = (
            c.sem(f"route_{n}") for n in ("picks", "part_hi", "part_lo", "mixing", "weighted", "folding", "fold_hi", "fold_lo"))
        with nc.Block() as block:
            @block.sync
            def _(sp):
                sp.dma_start(gw[:], d["w1_gate"]).then_inc(g_in, 16)
                sp.dma_start(gb[:], d["L1_ffn_gate_b"].rearrange("(a s) -> a s", a=1).to_broadcast([P, E])).then_inc(w_in, 16)
                sp.dma_start(pick_raw[:], d["pick"]).then_inc(w_in, 16)
                sp.dma_start(eb[:], d["L1_ffn_expert_b"]).then_inc(w_in, 16)
                w.ahead_load(sp)
                lr.load(sp, d)
                sp.sem_clear(old_semaphores)

            @block.tensor
            def _(pe):
                pe.wait_ge(gate_lo, 1)
                for half in range(2):
                    cols = slice(half * HALF, (half + 1) * HALF)
                    for k in range(KT):
                        last = three_passes(nc, ptr[:, cols], gh[:, k, :], gl[:, k, :], xh[:, k, cols], xl[:, k, cols], k == 0, k == KT - 1)
                last.then_inc(products, 1)
                pe.wait_ge(moved, 1)
                for t in range(TT):
                    last = nc.tensor.transpose(pz[:, t, :], z_t[:, t * P:(t + 1) * P], g["ident"][0:E, 0:E])
                last.then_inc(logits, 1)
                pe.wait_ge(lr.fold_in, 48)
                for j in range(2):
                    for k in range(KT):
                        last = nc.tensor.matmul(p_fold[:, j * P:(j + 1) * P], lr.fa[:, k, j * P:(j + 1) * P], lr.a[:, k, :], start=k == 0, stop=k == KT - 1)
                last.then_inc(mixing, 1)
                pe.wait_ge(chosen, 1)
                for t in range(TT):
                    last = nc.tensor.transpose(ptr[:, t * P:(t + 1) * P], sel[:, t, :], g["ident"][:])
                last.then_inc(turned, 1)
                pe.wait_ge(weighted, 1)
                for k in range(KT):
                    nc.tensor.matmul(p_fold[:], lr.a[:, k, :], lr.wb[:, k, :], start=k == 0, stop=False)
                for j in range(2):
                    last = nc.tensor.matmul(p_fold[:], lr.mixed[:, j, :], lr.wb[:, KT + j, :], start=False, stop=j == 1)
                last.then_inc(folding, 1)
                pe.wait_ge(out, 1)
                pe.wait_ge(picks, 1)
                for j in range(E):
                    if j >= 2:
                        pe.wait_ge(copied, j - 1)
                    for half in range(2):
                        cols = slice(half * HALF, (half + 1) * HALF)
                        last = nc.tensor.matmul(pb[:, j % 2, cols], pick[:, j, :], sel_t[:, cols], start=True, stop=True)
                    last.then_inc(spread, 1)

            @block.vector
            def _(dve):
                count = [0]

                def chain(ins):
                    count[0] += 1
                    ins.then_inc(link, 1)
                    dve.wait_ge(link, count[0])

                dve.wait_ge(gate_hi, 1)
                nc.vector.tensor_tensor(gl[:], gw[:], f32(gh[:]), ALU.subtract).then_inc(gate_lo, 1)
                dve.wait_ge(products, 1)
                nc.vector.tensor_copy(z_t[:], ptr[:]).then_inc(moved, 1)
                dve.wait_ge(logits, 1)
                dve.wait_ge(w_in, 48)
                chain(nc.vector.tensor_tensor(z[:], pz[:], gb[:].rearrange("p (o e) -> p o e", o=1).to_broadcast([P, TT, E]), ALU.add))
                chain(nc.vector.reduce_max(mx[:], z[:], AX_X))
                chain(nc.vector.tensor_tensor(eq[:], z[:], mx[:].rearrange("p (t o) -> p t o", o=1).to_broadcast([P, TT, E]), ALU.is_equal))
                chain(nc.vector.memset(taken[:], 0.0))
                for j in range(E):
                    chain(nc.vector.tensor_tensor(sel[:, :, j], eq[:, :, j], taken[:], ALU.is_gt))
                    chain(nc.vector.tensor_tensor(taken[:], taken[:], eq[:, :, j], ALU.max))
                dve.sem_inc(chosen, 1)
                dve.wait_ge(mixing, 1)
                for j in range(2):
                    chain(nc.vector.tensor_scalar(lr.mixed[:, j, :], p_fold[:, j * P:(j + 1) * P], probs[:, j:j + 1], None, ALU.mult, ALU.bypass))
                dve.sem_inc(weighted, 1)
                dve.wait_ge(turned, 1)
                nc.vector.tensor_copy(sel_t[:], ptr[:]).then_inc(out, 1)
                dve.wait_ge(fold_hi, 1)
                nc.vector.tensor_tensor(lr.fold_lo[:], p_fold[:], f32(lr.fold_hi[:]), ALU.subtract).then_inc(fold_lo, 1)

            @block.scalar
            def _(act):
                act.wait_ge(g_in, 16)
                nc.scalar.activation(gh[:], gw[:], ACT.Copy).then_inc(gate_hi, 1)
                w.ahead_high(act)
                act.wait_ge(w_in, 48)
                nc.scalar.activation(pick[:], pick_raw[:], ACT.Copy).then_inc(picks, 1)
                for n in range(len(lr.PARTS)):
                    act.wait_ge(lr.part_in[n], 16)
                    nc.scalar.activation(lr.hi[n][:], lr.raw[n][:], ACT.Copy).then_inc(part_hi, 1)
                act.wait_ge(folding, 1)
                nc.scalar.activation(lr.fold_hi[:], p_fold[:], ACT.Copy).then_inc(fold_hi, 1)
                for j in range(E):
                    act.wait_ge(spread, j + 1)
                    nc.scalar.activation(mb[:, j, :], pb[:, j % 2, :], ACT.Copy).then_inc(copied, 1)

            @block.gpsimd
            def _(pool):
                w.ahead_low(pool)
                for n in range(len(lr.PARTS)):
                    pool.wait_ge(part_hi, n + 1)
                    nc.gpsimd.tensor_tensor(lr.lo[n][:], lr.raw[n][:], f32(lr.hi[n][:]), ALU.subtract).then_inc(part_lo, 1)


def expert_phase(nc, d, g, w, sel_t, mb, eb):
    xh, xl = g["xh"], g["xl"]
    with ExitStack() as ctx:
        c = Core(nc, ctx)
        mh, ml = ([c.sb(f"moe_{x}{n}", [P, TOK], F32R) for n in range(2)] for x in ("mh", "ml"))

        def produce(dve, t, u, i, made):
            m = mb[:, at(i), :].rearrange("p o n -> p (o n)")
            nc.vector.tensor_tensor(mh[u % 2][:], f32(xh[:, u, :]), m, ALU.mult).then_inc(made, 1)
            nc.vector.tensor_tensor(ml[u % 2][:], f32(xl[:, u, :]), m, ALU.mult).then_inc(made, 1)

        def moving(t, u, i, half):
            cols = slice(half * HALF, (half + 1) * HALF)
            return mh[u % 2][:, cols], ml[u % 2][:, cols]

        def first(pe, acc):
            for m in range(KT):
                for half in range(2):
                    cols = slice(half * HALF, (half + 1) * HALF)
                    nc.tensor.matmul(acc[:, m, cols], eb[:, m * P:(m + 1) * P], f32(sel_t[:, cols]), start=True, stop=False)

        accumulate_phase(nc, d, g, "moe", w, moving, onto_residual(nc, g, lambda m: 1.0), produce=produce, first=first)


def low_rank_phase(nc, d, g, lr, bias, following):
    xh, xl, resid = g["xh"], g["xl"], g["resid"]
    (b_hi, b_lo), (a_hi, a_lo), (w_hi, w_lo) = (lr.parts(n) for n in range(3))
    halves = [slice(n * HALF, (n + 1) * HALF) for n in range(2)]
    LAST = (2, 3, 0, 1)
    with ExitStack() as ctx:
        c = Core(nc, ctx)
        hf = c.sb("l_hf", [P, 2, TOK])
        lh, ll = c.sb("l_h", [P, 2, TOK], F32R), c.sb("l_l", [P, 2, TOK], F32R)
        acc = c.ps("l_acc", [P, KT, TOK])
        down_sums, down_masked, down_hi, down_lo = (c.sem(f"adapter_{n}") for n in ("sums", "masked", "hi", "lo"))
        up_sums, added, x_hi, x_lo_even, x_lo_odd = (c.sem(f"layer2_{n}") for n in ("sums", "added", "hi", "lo_even", "lo_odd"))
        low_sums, low_masked, low_hi, low_lo = (c.sem(f"label_{n}") for n in ("sums", "masked", "hi", "lo"))
        out_sums, out_hi, out_lo = (c.sem(f"cond3_{n}") for n in ("sums", "hi", "lo"))

        with nc.Block() as block:
            @block.sync
            def _(sp):
                following.ahead_load(sp)

            @block.tensor
            def _(pe):
                for cols in halves:
                    for k in range(KT):
                        last = three_passes(nc, acc[:, 0, cols], b_hi[:, k, :], b_lo[:, k, :], xh[:, k, cols], xl[:, k, cols], k == 0, k == KT - 1)
                    last.then_inc(down_sums, 1)
                for n, cols in enumerate(halves):
                    pe.wait_ge(down_lo, n + 1)
                    for m in range(KT):
                        rows = slice(m * P, (m + 1) * P)
                        three_passes(nc, acc[:, m, cols], lr.fold_hi[:, rows], lr.fold_lo[:, rows], lh[:, 0, cols], ll[:, 0, cols],
                                     True, True).then_inc(up_sums, 1)
                for n, cols in enumerate(halves):
                    for j in range(2):
                        for k in range(KT):
                            pe.wait_ge(x_lo_odd if k % 2 else x_lo_even, n * 2 + k // 2 + 1)
                            last = three_passes(nc, acc[:, j, cols], a_hi[:, k, j * P:(j + 1) * P], a_lo[:, k, j * P:(j + 1) * P],
                                                xh[:, k, cols], xl[:, k, cols], k == 0, k == KT - 1)
                        last.then_inc(low_sums, 1)
                for m in LAST:
                    rows = slice(m * P, (m + 1) * P)
                    for n, cols in enumerate(halves):
                        if m < 2:
                            pe.wait_ge(low_masked, n * 2 + m + 1)
                        for k in range(KT):
                            three_passes(nc, acc[:, m, cols], w_hi[:, k, rows], w_lo[:, k, rows], xh[:, k, cols], xl[:, k, cols], k == 0, False)
                pe.wait_ge(low_lo, 4)
                for m in LAST:
                    rows = slice(m * P, (m + 1) * P)
                    for cols in halves:
                        for j in range(2):
                            last = three_passes(nc, acc[:, m, cols], w_hi[:, KT + j, rows], w_lo[:, KT + j, rows], lh[:, j, cols], ll[:, j, cols], False, j == 1)
                        last.then_inc(out_sums, 1)

            @block.vector
            def _(dve):
                def masked(j, cols, mask, n):
                    mk = mask[:, n * B // 2:(n + 1) * B // 2].rearrange("p (b o) -> p b o", o=1).to_broadcast([P, B // 2, S])
                    return nc.vector.tensor_tensor(hf[:, j, cols].rearrange("p (b s) -> p b s", s=S), acc[:, j, cols].rearrange("p (b s) -> p b s", s=S), mk, ALU.mult)

                for n, cols in enumerate(halves):
                    dve.wait_ge(down_sums, n + 1)
                    masked(0, cols, g["amask"][:], n).then_inc(down_masked, 1)
                    dve.wait_ge(down_hi, n + 1)
                    nc.vector.tensor_tensor(ll[:, 0, cols], hf[:, 0, cols], f32(lh[:, 0, cols]), ALU.subtract).then_inc(down_lo, 1)
                for n, cols in enumerate(halves):
                    def x_low(m):
                        dve.wait_ge(x_hi, n * KT + m + 1)
                        nc.vector.tensor_tensor(xl[:, m, cols], resid[:, m, cols], f32(xh[:, m, cols]), ALU.subtract).then_inc(x_lo_even, 1)

                    for m in range(KT):
                        dve.wait_ge(up_sums, n * KT + m + 1)
                        nc.vector.scalar_tensor_tensor(resid[:, m, cols], acc[:, m, cols], bias[:, m:m + 1], resid[:, m, cols], ALU.add, ALU.add).then_inc(added, 1)
                        if m % 2:
                            x_low(m - 1)
                for n, cols in enumerate(halves):
                    for j in range(2):
                        dve.wait_ge(low_sums, n * 2 + j + 1)
                        masked(j, cols, g["bmask"][:, j, :], n).then_inc(low_masked, 1)
                        dve.wait_ge(low_hi, n * 2 + j + 1)
                        nc.vector.tensor_tensor(ll[:, j, cols], hf[:, j, cols], f32(lh[:, j, cols]), ALU.subtract).then_inc(low_lo, 1)
                following.ahead_ternary(dve)
                for n in range(2 * KT):
                    m, cols = LAST[n // 2], halves[n % 2]
                    dve.wait_ge(out_hi, n + 1)
                    nc.vector.tensor_tensor(xl[:, m, cols], acc[:, m, cols], f32(xh[:, m, cols]), ALU.subtract).then_inc(out_lo, 1)

            @block.scalar
            def _(act):
                for n, cols in enumerate(halves):
                    act.wait_ge(down_masked, n + 1)
                    nc.scalar.activation(lh[:, 0, cols], hf[:, 0, cols], ACT.Copy).then_inc(down_hi, 1)
                for n, cols in enumerate(halves):
                    for m in range(KT):
                        act.wait_ge(added, n * KT + m + 1)
                        nc.scalar.activation(xh[:, m, cols], resid[:, m, cols], ACT.Copy).then_inc(x_hi, 1)
                for n, cols in enumerate(halves):
                    for j in range(2):
                        act.wait_ge(low_masked, n * 2 + j + 1)
                        nc.scalar.activation(lh[:, j, cols], hf[:, j, cols], ACT.Copy).then_inc(low_hi, 1)
                for n in range(2 * KT):
                    m, cols = LAST[n // 2], halves[n % 2]
                    act.wait_ge(out_sums, n + 1)
                    nc.scalar.activation(xh[:, m, cols], acc[:, m, cols], ACT.Copy).then_inc(out_hi, 1)

            @block.gpsimd
            def _(pool):
                for n, cols in enumerate(halves):
                    for m in (1, 3):
                        pool.wait_ge(x_hi, n * KT + m + 1)
                        nc.gpsimd.tensor_tensor(xl[:, m, cols], resid[:, m, cols], f32(xh[:, m, cols]), ALU.subtract).then_inc(x_lo_odd, 1)


def program(nc, d, out, upto=99):
    Core.used.clear()
    with ExitStack() as ctx:
        c = Core(nc, ctx)
        g = {
            "resid": c.sb("resid", [P, KT, TOK]), "xh": c.sb("xh", [P, KT, TOK], F32R), "xl": c.sb("xl", [P, KT, TOK], F32R),
            "ident": c.sb("ident_sb", [P, P]), "cols": c.sb("cols_sb", [P, 8]),
            "lens": c.sb("lens", [P, 4, B]), "vec": c.sb("vectors", [P, 2 * IT + 4 * KT]), "rows": c.sb("w3_rows", [P, IT, 3]),
            "bt": c.sb("bt_sb", [1, B * NPP], I32), "vrow": c.sb("vrow", [P, B * VCH], I32), "lmask": c.sb("lmask", [P, KT, B]), "amask": c.sb("amask", [P, B]),
            "bmask": c.sb("bmask", [P, 2, B]), 
            "scale3": c.sb("scale3", [P, 3]), "thr3": c.sb("thr3", [P, 6]),
            "kpad": nc.dram_tensor("kpad", [S, KPAD], F32).ap(),
            "qk_scr": nc.dram_tensor("qk_scr", [B, P, GROUPS, REP * S], F32).ap(),
            "v_scr": nc.dram_tensor("v_scr", [TOK, HK * D], F32).ap(),
            "o_scr": nc.dram_tensor("o_scr", [B, P, HQ * S], F32).ap(),
        }
        vec = g["vec"]
        AG, AU, AD, BIAS2, PROBS = 0, IT, 2 * IT, 2 * IT + KT, 2 * IT + 2 * KT
        xh, xl = g["xh"], g["xl"]

        def column(base):
            return lambda t: vec[:, base + t:base + t + 1] if isinstance(t, int) else vec[:, bass.ds(t + base, 1)]

        attn = ctx.enter_context(ExitStack())
        ca = Core(nc, attn)
        g["keyidx"] = ca.sb("keyidx_sb", [P, KEYS])
        rope = ca.sb("rope", [P, 2, 2, TT, D])
        g["rope_c"], g["rope_s"] = rope[:, 0], rope[:, 1]
        front = ctx.enter_context(ExitStack())
        cf_ = Core(nc, front)
        for name, shape, dt in (("ints", [P, 4, B], I32), ("posi", [P, TT], I32), ("spos", [P, TT], F32), ("posf", [P, TT], F32),
                                ("invf", [P, D // 2], F32), ("nw", [P, 2, D], F32), ("vpage", [P, B * VCH], I32), ("vpf", [P, B * VCH], F32),
                                ("fr", [P, 2, TT, D // 2], F32), ("fk", [P, 2, TT, D // 2], F32)):
            g[name] = cf_.sb("b_" + name, shape, dt)
        setup_phase(nc, d, g)
        conv_phase(nc, d, g)
        if upto > 0:
            with ExitStack() as inner:
                ci = Core(nc, inner)
                hh, hl = ci.sb("hh", [P, IT, TOK], F32R), ci.sb("hl", [P, IT, TOK], F32R)
                w_down = WeightStream(nc, ci, "d0", WeightSlots(ci, "d0", H), d["w0_d"], H, IT, 2)
                with ExitStack() as gu:
                    cg = Core(nc, gu)
                    w_gu = WeightStream(nc, cg, "gu0", WeightSlots(cg, "gu0", 2 * H), d["w0_gu"], 2 * H, IT, 2)
                    gate_up_phase(nc, d, g, hh, hl, "f0", w_gu, ACT.Silu, column(AG), column(AU), w_down,
                                  gate_room=rope[:].rearrange("p c a t d -> p (c a t d)"),
                                  vector_first=lambda chain: rotary_angles(nc, d, g, chain),
                                  scalar_last=lambda: nc.scalar.activation(g["fk"][:], g["fr"][:], ACT.Sin))

                W = KT * P
                w3 = [ci.sb(f"w3_raw{n}", [P, 3 * W]) for n in range(2)]
                w3_in, w3_sums = [ci.sem(f"w3_in{n}") for n in range(2)], ci.sem("w3_sums")
                w3_gate = ci.sem("w3_gate")

                def load_w3(sp, t, u, i, made):
                    if not early(t, 2):
                        sp.wait_ge(w3_sums, t - 1)
                    sp.dma_start(w3[u][:, 0:2 * W], d["w3_gu"][at(t)].rearrange("o p m -> (o p) m")).then_inc(w3_in[u], 16)
                    sp.dma_start(w3[u][:, 2 * W:3 * W], d["w3_d"][at(t)].rearrange("o p m -> (o p) m")).then_inc(w3_in[u], 16)

                def sum_w3(dve, t, u, i):
                    dve.wait_ge(w3_in[u], (i + 1) * 32)
                    dve.sem_inc(w3_gate, 1)
                    nc.vector.tensor_reduce(g["rows"][:, at(t), :].rearrange("p o n -> p (o n)"), w3[u][:].rearrange("p (n w) -> p n w", n=3),
                                            axis=AX_X, op=ALU.add, apply_absolute_value=True).then_inc(w3_sums, 1)

                accumulate_phase(nc, d, g, "d0", w_down, resident(hh, hl), onto_residual(nc, g, lambda m: vec[:, AD + m:AD + m + 1], batch_major=False),
                                 vector_first=lambda chain: rotary_tables(nc, d, g, chain), load_extra=load_w3, side=sum_w3)
            front.close()
        if upto > 1:
            project_phase(nc, d, g)
            attention_phase(nc, d, g)
        attn.close()
        old = range(min(Core.used), max(Core.used) + 1)
        thr, sc3 = g["thr3"], g["scale3"]
        slots = [WeightSlots(c, f"slots{n}", H) for n in range(2)]
        w_gu3 = WeightStream(nc, c, "gu3", WeightSlots(c, "gu3", 2 * H, ternary_only=True), d["w3_gu"], 2 * H, IT, 2,
                             thresholds=[(thr[:, n:n + 1], thr[:, 3 + n:4 + n]) for n in range(2)])
        w_experts = WeightStream(nc, c, "moe", slots[1], d["w1_e"], H, EXPERTS * KT, KT)
        with ExitStack() as low:
            ck = Core(nc, low)
            lr = LowRankWeights(nc, ck)
            w_out = WeightStream(nc, Core(nc, low), "wo", slots[0], d["w1_o"], H, HQ, 2 * REP)
            output_projection(nc, d, g, w_out, None)
            with ExitStack() as experts:
                ce = Core(nc, experts)
                sel_t, mb, eb = ce.sb("sel_t", [EXPERTS, TOK], F32R), ce.sb("mb", [P, EXPERTS, TOK], BF16), ce.sb("eb", [EXPERTS, H])
                route_phase(nc, d, g, w_experts, sel_t, mb, eb, lr, vec[:, PROBS:PROBS + 2], old)
                expert_phase(nc, d, g, w_experts, sel_t, mb, eb)
            low_rank_phase(nc, d, g, lr, vec[:, BIAS2:BIAS2 + KT], w_gu3)
        with ExitStack() as inner:
            ci = Core(nc, inner)
            hh, hl = ci.sb("hh3", [P, IT, TOK], F32R), ci.sb("hl3", [P, IT, TOK], F32R)
            gate_room = ci.sb("gate_room", [P, 3 * TOK])
            w_down3 = WeightStream(nc, ci, "d3", slots[0], d["w3_d"], H, IT, 2, thresholds=[(thr[:, 2:3], thr[:, 5:6])])
            gate_up_phase(nc, d, g, hh, hl, "f3", w_gu3, ACT.Copy, lambda t: sc3[:, 0:1], lambda t: sc3[:, 1:2], w_down3, gate_room[:])
            accumulate_phase(nc, d, g, "d3", w_down3, resident(hh, hl), onto_residual(nc, g, lambda m: sc3[:, 2:3], split=False),
                             store=lambda sp, m: sp.dma_start(out[:, m, :], g["resid"][:, m, :]))


def tiles_of(w, k_tiles, cols):
    full = np.zeros((k_tiles * P, cols), np.float32)
    full[:w.shape[0], :w.shape[1]] = w
    return full.reshape(k_tiles, P, cols)


def on_partitions(w, k_tiles):
    return w.reshape(k_tiles, P, -1).transpose(1, 0, 2)


def gate_up_tiles(wg, wu):
    both = np.stack([tiles_of(w.T, KT, IT * P) for w in (wg, wu)])
    return np.ascontiguousarray(both.reshape(2, KT, P, IT, P).transpose(3, 2, 0, 1, 4)).reshape(IT, P, 2 * KT * P)


def vector_columns(v, tiles):
    full = np.zeros(tiles * P, np.float32)
    full[:v.shape[0]] = v
    return full.reshape(tiles, P).T


def layouts(i):
    i = {k: np.asarray(v) for k, v in i.items()}
    a = {k: i[k] for k in ("itok_B_78_3631", "itok_B_207_1644", "itok_B_3_7", "itok_B_0_4", "itok_Bx16_0_63", "L0_cond_log_dt", "L0_cond_D",
                           "L1_cond_q_norm_w", "L1_cond_k_norm_w", "L1_ffn_gate_b", "L1_ffn_expert_b")}
    x = i["x"]
    a["xT"] = x.transpose(2, 0, 1).reshape(KT, P, TOK).transpose(1, 0, 2)
    a["x_rev"] = x.transpose(2, 1, 0).reshape(KT, P, S, B)[:, ::-1].transpose(1, 2, 0, 3)
    for name, w in (("logA2", i["L0_cond_log_A_real"]), ("Aim2", i["L0_cond_A_imag"]), ("Cre2", i["L0_cond_C"][..., 0]), ("Cim2", i["L0_cond_C"][..., 1])):
        a[name] = np.concatenate([w.T, w.T])
    W = REP * D
    wq = i["L1_cond_Wq"].T.reshape(KT, P, HQ * D // W, W).transpose(2, 1, 0, 3)
    wk = i["L1_cond_Wk"].T.reshape(KT, P, HK * D // W, W).transpose(2, 1, 0, 3)
    wv = i["L1_cond_Wv"].T.reshape(KT, P, HK * D // W, W).transpose(2, 1, 0, 3)
    a["w1_qkv"] = np.concatenate([wq, wk, wv]).reshape(-1, P, KT * W)
    a["kT_pages"] = i["L1_cond_k_cache"].transpose(0, 3, 2, 1).reshape(PAGES, P, HK * PSIZE)
    a["v_rows"] = i["L1_cond_v_cache"].reshape(PAGES * PSIZE, HK * D)
    a["vpages"] = i["itok_Bx16_0_63"].reshape(B, VCH, NPP // VCH).transpose(2, 0, 1).reshape(NPP // VCH, B * VCH)
    a["w1_o"] = i["L1_cond_Wo"].T.reshape(HQ, P, H)
    a["w1_gate"] = i["L1_ffn_gate_w"].T.reshape(KT, P, EXPERTS).transpose(1, 0, 2)
    a["w1_e"] = i["L1_ffn_expert_w"].transpose(0, 2, 1).reshape(EXPERTS * KT, P, H)
    a["w0_gu"] = gate_up_tiles(i["L0_ffn_Wg"], i["L0_ffn_Wu"])
    a["w0_d"] = tiles_of(i["L0_ffn_Wd"].T, IT, H)
    a["w3_gu"] = gate_up_tiles(i["L3_ffn_w_gate"], i["L3_ffn_w_up"])
    a["w3_d"] = tiles_of(i["L3_ffn_w_down"].T, IT, H)
    a["vectors"] = np.concatenate([vector_columns(i["L0_ffn_ag"], IT), vector_columns(i["L0_ffn_au"], IT), vector_columns(i["L0_ffn_ad"], KT),
                                   vector_columns(i["L2_ffn_b"], KT), vector_columns(np.repeat(i["L2_ffn_probs"], 16), 2)], axis=1)
    a["w2_b"] = on_partitions(i["L2_cond_B"].reshape(ADAPTERS * RANK2, H).T, KT)
    a["w2_a"] = on_partitions(i["L2_cond_A"].transpose(1, 0, 2).reshape(H, ADAPTERS * RANK2), KT)
    a["w2_fa"] = on_partitions(i["L2_ffn_A"].reshape(-1, H).T, KT)
    a["w2_wb"] = on_partitions(np.concatenate([i["L2_ffn_W"].T, i["L2_ffn_B"].transpose(0, 2, 1).reshape(-1, H)]), KT + 2)
    a["w3_la"] = tiles_of(i["L3_cond_lora_A"].transpose(1, 0, 2).reshape(H, LABELS * RANK3), KT, 2 * P).transpose(1, 0, 2)
    low = np.concatenate([i["L3_cond_lora_B_w"].T] * LABELS)
    a["w3_wb"] = on_partitions(np.concatenate([i["L3_cond_weight"].T, low, np.zeros((2 * P - LABELS * RANK3, H), np.float32)]), KT + 2)

    row = np.arange(P)
    a["posbase"] = np.repeat(i["itok_B_207_1644"], S).reshape(TT, P).T
    a["seqpos"] = np.tile((row % S).astype(np.float32)[:, None], (1, TT))
    a["inv_freq"] = np.tile((1.0 / THETA ** (np.arange(0, D, 2, dtype=np.float32) / D)).astype(np.float32), (P, 1))
    upper = row < P // 2
    a["signs"] = np.stack([np.where(upper, 2.0, 0.0), np.where(upper, 0.0, -2.0), np.where(upper, -2.0, 0.0), np.where(upper, 0.0, -2.0)], 1).astype(np.float32)
    a["positions"] = np.tile(np.concatenate([np.arange(LO_N), LO_N * np.arange(HI_N)]).astype(np.float32), (P, 1))
    a["ident"] = np.eye(P, dtype=np.float32)
    a["keyidx"] = np.tile(np.concatenate([np.arange(CACHE), -np.ones(S)]).astype(np.float32), (P, 1))
    cols = np.zeros((P, 8), np.float32)
    for m in range(KT):
        cols[:, m] = m * P + row
    cols[:, 4] = row // RANK2
    cols[:, 5], cols[:, 6] = row // RANK3, (P + row) // RANK3
    cols[:, 7] = row % PSIZE
    a["cols"] = cols
    pick = np.zeros((EXPERTS, EXPERTS, P), np.float32)
    for j in range(EXPERTS):
        pick[j, j] = 1.0
    a["pick"] = pick
    return {k: np.ascontiguousarray(v) for k, v in a.items()}


def kernel(**inputs):
    import concourse.bacc as bacc
    from concourse.bass_utils import run_bass_kernel_spmd

    nc = bacc.Bacc("TRN2", target_bir_lowering=False, num_devices=1)
    arrays, d = {}, {}
    for name, a in layouts(inputs).items():
        arrays[f"in_{name}"] = a
        d[name] = nc.dram_tensor(f"in_{name}", a.shape, mybir.dt.from_np(a.dtype), kind="ExternalInput").ap()
    out = nc.dram_tensor("out_x", [P, KT, TOK], F32, kind="ExternalOutput").ap()
    program(nc, d, out)
    r = run_bass_kernel_spmd(nc, [arrays], core_ids=[0])
    got = r.results[0]["out_x"]
    return np.ascontiguousarray(got.reshape(P, KT, B, S).transpose(2, 3, 1, 0).reshape(B, S, H))
```

```python
from contextlib import ExitStack

import numpy as np

import concourse.bass as bass
from concourse import mybir

F32 = mybir.dt.float32
F32R = mybir.dt.float32r
I32 = mybir.dt.int32
BF16 = mybir.dt.bfloat16
ALU = mybir.AluOpType
ACT = mybir.ActivationFunctionType
AX_X = mybir.AxisListType.X

P = 128
B, S, H = 32, 32, 512
TOK = B * S
HALF = TOK // 2
KT = H // P
INTER = 1376
IT = -(-INTER // P)
N_STATE = 64
LO_N, HI_N = 32, H // 32
D = 128
HQ, HK = 32, 8
REP = HQ // HK
PAGES, PSIZE, NPP = 64, 32, 16
CACHE = NPP * PSIZE
KEYS = CACHE + S
VCH = CACHE // P
GROUPS = (HQ + HK) // REP
TT = TOK // P
BPT = P // S
EXPERTS = 8
SLOT_TILES = (TOK + EXPERTS * (P - 1)) // P
ADAPTERS, RANK2 = 8, 16
LABELS, RANK3 = 5, 32
LABEL_PAD = 8
THETA = 10000.0
RMS_EPS = 1e-6
BIT_EPS = 1e-5
ATT_SCALE = 1.0 / float(np.sqrt(D))
NEG = -1e30
KPAD = P + H

TWO_PI = 2.0 * np.pi
MAGIC = 1.5 * 2.0 ** 23
PI_1 = 6.28125
PI_2 = float(np.round((TWO_PI - PI_1) * 2.0 ** 20) / 2.0 ** 20)
PI_3 = float(TWO_PI - PI_1 - PI_2)
PI_SAFE = 3.1415925
LN2_1, LN2_2 = 0.693359375, -2.12194440e-4


def run_steps(eng, n, unroll, step):
    for u in range(min(unroll, n)):
        step(u, u, 0)
    whole = n // unroll
    if whole > 2:
        with eng.Fori(1, whole) as i:
            for u in range(unroll):
                step(i * unroll + u, u, i)
    else:
        for i in range(1, whole):
            for u in range(unroll):
                step(i * unroll + u, u, i)
    for t in range(max(whole, 1) * unroll, n):
        step(t, t % unroll, t // unroll)


def early(n, k):
    return isinstance(n, int) and n < k


def at(i, n=1):
    return bass.ds(i, n)


def f32(ap):
    return ap.bitcast(F32)


class Core:
    used = []

    def __init__(self, nc, ctx):
        self.nc, self.ctx = nc, ctx

    def sb(self, name, shape, dt=F32):
        return self.ctx.enter_context(self.nc.sbuf_tensor(name, shape, dt))

    def ps(self, name, shape):
        return self.ctx.enter_context(self.nc.psum_tensor(name, shape, F32))

    def sem(self, name):
        handle = self.ctx.enter_context(self.nc.semaphore(name))
        self.used.append(handle.num)
        return handle


def three_passes(nc, out, w_hi, w_lo, x_hi, x_lo, start, stop):
    nc.tensor.matmul(out, w_hi, x_hi, start=start, stop=False)
    nc.tensor.matmul(out, w_hi, x_lo, start=False, stop=False)
    return nc.tensor.matmul(out, w_lo, x_hi, start=False, stop=stop)


def arithmetic(nc, chain):
    def tt(out, a, b_, op):
        chain(nc.vector.tensor_tensor(out, a, b_, op))

    def tsc(out, a, s1, s2, op0, op1):
        chain(nc.vector.tensor_scalar(out, a, s1, s2, op0, op1))

    def reduce_angle(x, k):
        tsc(k, x, 1.0 / TWO_PI, MAGIC, ALU.mult, ALU.add)
        tsc(k, k, -MAGIC, 0.0, ALU.add, ALU.add)
        for part in (PI_1, PI_2, PI_3):
            chain(nc.vector.scalar_tensor_tensor(x, k, -part, x, ALU.mult, ALU.add))
        tsc(x, x, PI_SAFE, -PI_SAFE, ALU.min, ALU.max)

    def cosine_angle(out, x, t):
        tsc(t, x, np.pi / 2, -TWO_PI, ALU.is_gt, ALU.mult)
        chain(nc.vector.scalar_tensor_tensor(out, x, np.pi / 2, t, ALU.add, ALU.add))
        tsc(out, out, PI_SAFE, -PI_SAFE, ALU.min, ALU.max)

    return tt, tsc, reduce_angle, cosine_angle


def setup_phase(nc, d, g):
    with ExitStack() as ctx:
        c = Core(nc, ctx)
        ai2, cre, cim = (c.sb(f"s_{n}", [P, S]) for n in ("ai", "cre", "cim"))
        two, two_e, two_k, two_r = (c.sb(f"s_two{n}", [P, 2 * S]) for n in ("", "_e", "_k", "_r"))
        two_b = c.sb("s_two_b", [P, 2 * S], I32)
        sgn = c.sb("s_sgn", [P, 4])
        bits = c.sb("s_bits", [P, S], I32)
        posn = c.sb("s_posn", [P, LO_N + HI_N])
        tmp = [c.sb(f"s_t{n}", [P, S]) for n in range(16)]
        LN = LO_N + HI_N
        mag = c.sb("s_mag", [P, S, LN])
        ang = c.sb("s_ang", [P, S, LN])
        angc = c.sb("s_angc", [P, S, LN])
        kk = c.sb("s_kk", [P, S, LN])
        kk2 = c.sb("s_kk2", [P, S, LN])
        low = c.sb("s_low", [P, S, LO_N])
        gco = c.sb("s_gco", [P, S, HI_N])
        gtm = c.sb("s_gtm", [P, S, HI_N])
        ks = c.sb("s_ks", [HI_N, S, LO_N])
        d16 = c.sb("s_d16", [1, S])
        zer = c.sb("s_zer", [S, P])
        ints, posi, spos, invf, nw = (g[n] for n in ("ints", "posi", "spos", "invf", "nw"))
        pk = c.ps("s_pk", [HI_N, S, LO_N])

        in_l = c.sem("setup_lengths_in")
        in_k, in_m, zero_in = c.sem("setup_kernel_in"), c.sem("setup_masks_in"), c.sem("setup_zeros")
        link, act_done, pe_done = c.sem("setup_dve_chain"), c.sem("setup_act_done"), c.sem("setup_pe_done")
        mag_ready, small_sines = c.sem("setup_mag_ready"), c.sem("setup_small_sines")
        dve_ready, k_out, res_in = c.sem("setup_dve_ready"), c.sem("setup_k_out"), c.sem("setup_resid_in")

        pb = posn[:].rearrange("p (o n) -> p o n", o=1).to_broadcast([P, S, LN])
        with nc.Block() as block:
            @block.sync
            def _(sp):
                for dst, src in ((two[:, S:2 * S], "logA2"), (ai2[:], "Aim2"), (cre[:], "Cre2"), (cim[:], "Cim2")):
                    sp.dma_start(dst, d[src]).then_inc(in_k, 16)
                sp.dma_start(sgn[:], d["signs"]).then_inc(in_k, 16)
                sp.dma_start(posn[:], d["positions"]).then_inc(in_k, 16)
                sp.dma_start(two[:, 0:S], d["L0_cond_log_dt"].rearrange("(a s) -> a s", a=1).to_broadcast([P, S])).then_inc(in_k, 16)
                sp.dma_start(d16[:], d["L0_cond_D"].rearrange("(a s) -> a s", a=1)).then_inc(in_k, 16)
                sp.dma_start(g["cols"][:], d["cols"]).then_inc(in_l, 16)
                sp.dma_start(ints[:, 0, :], d["itok_B_78_3631"].rearrange("(a s) -> a s", a=1).to_broadcast([P, B])).then_inc(in_l, 16)
                sp.dma_start(posi[:], d["posbase"]).then_inc(in_m, 16)
                sp.dma_start(spos[:], d["seqpos"]).then_inc(in_m, 16)
                sp.dma_start(invf[:], d["inv_freq"]).then_inc(in_m, 16)
                for n, src in enumerate(("itok_B_207_1644", "itok_B_3_7", "itok_B_0_4"), start=1):
                    sp.dma_start(ints[:, n, :], d[src].rearrange("(a s) -> a s", a=1).to_broadcast([P, B])).then_inc(in_m, 16)
                for n, src in enumerate(("L1_cond_q_norm_w", "L1_cond_k_norm_w")):
                    sp.dma_start(nw[:, n, :], d[src].rearrange("(a s) -> a s", a=1).to_broadcast([P, D])).then_inc(in_m, 16)
                for dst, src in ((g["ident"], "ident"), (g["keyidx"], "keyidx")):
                    sp.dma_start(dst[:], d[src]).then_inc(in_m, 16)
                sp.dma_start(g["bt"][:], d["itok_Bx16_0_63"].rearrange("b (o n) -> o (b n)", o=1)).then_inc(in_m, 16)
                for q in range(NPP // VCH):
                    sp.dma_start(g["vpage"][q * PSIZE:(q + 1) * PSIZE, :], d["vpages"][q:q + 1, :].to_broadcast([PSIZE, B * VCH])).then_inc(in_m, 16)
                sp.dma_start(g["vec"][:, 0:d["vectors"].shape[1]], d["vectors"]).then_inc(in_m, 16)
                sp.dma_start(g["resid"][:], d["xT"]).then_inc(res_in, 16)
                sp.dma_start(g["xr"][:, :, KT - 1:], d["x_rev"]).then_inc(g["xr_in"], 16)
                sp.wait_ge(zero_in, 1)
                sp.dma_start(g["kpad"][:, 0:P], zer[:]).then_inc(k_out, 16)
                sp.wait_ge(dve_ready, 4)
                sp.dma_start(g["kpad"][:, P:KPAD].rearrange("s (a c) -> a s c", c=LO_N), ks[:]).then_inc(k_out, 16)
                sp.wait_ge(k_out, 32)
                sp.wait_ge(res_in, 16)
                sp.wait_ge(in_m, 16 * 16)

            @block.gpsimd
            def _(pool):
                nc.gpsimd.memset(zer[:], 0.0).then_inc(zero_in, 1)
                pool.wait_ge(dve_ready, 1)
                nc.gpsimd.tensor_tensor(mag[:], tmp[2][:].rearrange("p (s o) -> p s o", o=1).to_broadcast([P, S, LN]), pb, ALU.mult).then_inc(mag_ready, 1)
                nc.gpsimd.memset(g["xr"][:, :, 0:KT - 1], 0.0).then_inc(g["xr_zeroed"], 1)

            @block.scalar
            def _(act):
                act.wait_ge(mag_ready, 1)
                nc.scalar.activation(mag[:], mag[:], ACT.Exp).then_inc(act_done, 1)
                act.wait_ge(dve_ready, 1)
                nc.scalar.activation(tmp[7][:], tmp[5][:], ACT.Sin)
                nc.scalar.activation(tmp[8][:], tmp[6][:], ACT.Sin).then_inc(small_sines, 1)
                act.wait_ge(dve_ready, 2)
                nc.scalar.activation(kk[:], ang[:], ACT.Sin)
                nc.scalar.activation(kk2[:], angc[:], ACT.Sin).then_inc(act_done, 1)

            @block.vector
            def _(dve):
                count = [0]

                def chain(ins):
                    count[0] += 1
                    ins.then_inc(link, 1)
                    dve.wait_ge(link, count[0])

                tt, tsc, reduce_angle, cosine_angle = arithmetic(nc, chain)
                dt, nre, dre, dim = two_e[:, 0:S], two_e[:, S:2 * S], tmp[2], tmp[3]
                def exact_exp(out, x, k, r, bits):
                    tsc(r, x, -87.0, 88.0, ALU.max, ALU.min)
                    tsc(k, r, 1.0 / np.log(2.0), MAGIC, ALU.mult, ALU.add)
                    tsc(k, k, -MAGIC, 0.0, ALU.add, ALU.add)
                    for part in (LN2_1, LN2_2):
                        chain(nc.vector.scalar_tensor_tensor(r, k, -part, r, ALU.mult, ALU.add))
                    tsc(bits, k, 127.0, 2.0 ** 23, ALU.add, ALU.mult)
                    tsc(k, r, 1.0 / 5040, 1.0 / 720, ALU.mult, ALU.add)
                    for coef in (1.0 / 120, 1.0 / 24, 1.0 / 6, 0.5, 1.0, 1.0):
                        tt(k, k, r, ALU.mult)
                        tsc(k, k, coef, 0.0, ALU.add, ALU.add)
                    tt(out, k, bits.bitcast(F32), ALU.mult)

                dve.wait_ge(in_k, 16 * 8)
                exact_exp(two_e[:], two[:], two_k[:], two_r[:], two_b[:])
                chain(nc.vector.scalar_tensor_tensor(dre[:], nre, -1.0, dt, ALU.mult, ALU.mult))
                tt(dim[:], ai2[:], dt, ALU.mult)
                exact_exp(tmp[4][:], dre[:], tmp[9][:], tmp[10][:], bits[:])
                chain(nc.vector.tensor_copy(tmp[5][:], dim[:]))
                reduce_angle(tmp[5][:], tmp[9][:])
                cosine_angle(tmp[6][:], tmp[5][:], tmp[9][:])
                dve.sem_inc(dve_ready, 1)
                tt(ang[:], dim[:].rearrange("p (s o) -> p s o", o=1).to_broadcast([P, S, LN]), pb, ALU.mult)
                reduce_angle(ang[:], kk[:])
                cosine_angle(angc[:], ang[:], kk[:])
                dve.sem_inc(dve_ready, 1)
                dve.wait_ge(small_sines, 1)
                sin_, cos_, e = tmp[7], tmp[8], tmp[4]
                nr, ni, q, den, cr, ci, al, be = (tmp[n] for n in (9, 10, 11, 12, 13, 14, 15, 5))
                tt(nr[:], e[:], cos_[:], ALU.mult)
                tsc(nr[:], nr[:], -1.0, 0.0, ALU.add, ALU.add)
                tt(ni[:], e[:], sin_[:], ALU.mult)
                tt(den[:], nre, nre, ALU.mult)
                tt(q[:], ai2[:], ai2[:], ALU.mult)
                tt(den[:], den[:], q[:], ALU.add)
                chain(nc.vector.reciprocal(den[:], den[:]))
                tt(cr[:], ni[:], ai2[:], ALU.mult)
                tt(q[:], nr[:], nre, ALU.mult)
                tt(cr[:], cr[:], q[:], ALU.subtract)
                tt(cr[:], cr[:], den[:], ALU.mult)
                tt(ci[:], ni[:], nre, ALU.mult)
                tt(q[:], nr[:], ai2[:], ALU.mult)
                tt(ci[:], ci[:], q[:], ALU.add)
                tt(ci[:], ci[:], den[:], ALU.mult)
                tsc(ci[:], ci[:], -1.0, 0.0, ALU.mult, ALU.add)
                tt(nr[:], cre[:], cr[:], ALU.mult)
                tt(q[:], cim[:], ci[:], ALU.mult)
                tt(nr[:], nr[:], q[:], ALU.subtract)
                tt(ni[:], cre[:], ci[:], ALU.mult)
                tt(q[:], cim[:], cr[:], ALU.mult)
                tt(ni[:], ni[:], q[:], ALU.add)
                tsc(al[:], nr[:], sgn[:, 0:1], None, ALU.mult, ALU.bypass)
                chain(nc.vector.scalar_tensor_tensor(al[:], ni[:], sgn[:, 1:2], al[:], ALU.mult, ALU.add))
                tsc(be[:], ni[:], sgn[:, 2:3], None, ALU.mult, ALU.bypass)
                chain(nc.vector.scalar_tensor_tensor(be[:], nr[:], sgn[:, 3:4], be[:], ALU.mult, ALU.add))
                dve.wait_ge(act_done, 2)
                hi_c, hi_s, hi_m = kk2[:, :, LO_N:], kk[:, :, LO_N:], mag[:, :, LO_N:]
                wide = [P, S, HI_N]
                tt(gco[:], hi_c, al[:].rearrange("p (s o) -> p s o", o=1).to_broadcast(wide), ALU.mult)
                tt(gtm[:], hi_s, be[:].rearrange("p (s o) -> p s o", o=1).to_broadcast(wide), ALU.mult)
                tt(gco[:], gco[:], gtm[:], ALU.add)
                tt(gco[:], gco[:], hi_m, ALU.mult)
                hp = P // 2
                tt(low[0:hp], kk2[0:hp, :, 0:LO_N], mag[0:hp, :, 0:LO_N], ALU.mult)
                chain(nc.vector.tensor_tensor(low[hp:P], kk[hp:P, :, 0:LO_N], mag[hp:P, :, 0:LO_N], ALU.mult))
                dve.sem_inc(dve_ready, 1)
                dve.wait_ge(pe_done, 1)
                chain(nc.vector.tensor_copy(ks[:], pk[:]))
                nc.vector.tensor_tensor(ks[0:1, :, 0], ks[0:1, :, 0], d16[:], ALU.add).then_inc(dve_ready, 1)
                dve.wait_ge(in_l, 32)
                chain(nc.vector.tensor_copy(g["lens"][:, 0, :], ints[:, 0, :]))
                for m in range(KT):
                    tsc(g["lmask"][:, m, :], g["lens"][:, 0, :], g["cols"][:, m:m + 1], None, ALU.is_gt, ALU.bypass)

            @block.tensor
            def _(pe):
                pe.wait_ge(dve_ready, 3)
                for s in range(S):
                    last = nc.tensor.matmul(pk[:, s, :], gco[:, s, :], low[:, s, :], start=True, stop=True)
                last.then_inc(pe_done, 1)


def rotary_angles(nc, d, g, chain):
    tt, tsc, reduce_angle, cosine_angle = arithmetic(nc, chain)
    fr, fk, fw = g["fr"], g["fk"], [P, TT, D // 2]
    chain(nc.vector.tensor_copy(g["lens"][:, 1:4, :], g["ints"][:, 1:4, :]))
    tsc(g["amask"][:], g["lens"][:, 2, :], g["cols"][:, 4:5], None, ALU.is_equal, ALU.bypass)
    for m in range(2):
        tsc(g["bmask"][:, m, :], g["lens"][:, 3, :], g["cols"][:, 5 + m:6 + m], 0.5, ALU.is_equal, ALU.mult)
    chain(nc.vector.tensor_copy(g["vpf"][:], g["vpage"][:]))
    tsc(g["vrow"][:], g["vpf"][:], float(PSIZE), g["cols"][:, 7:8], ALU.mult, ALU.add)
    chain(nc.vector.tensor_copy(g["posf"][:], g["posi"][:]))
    tt(g["posf"][:], g["posf"][:], g["spos"][:], ALU.add)
    tt(fr[:, 0], g["posf"][:].rearrange("p (t o) -> p t o", o=1).to_broadcast(fw),
       g["invf"][:].rearrange("p (o n) -> p o n", o=1).to_broadcast(fw), ALU.mult)
    reduce_angle(fr[:, 0], fk[:, 0])
    cosine_angle(fr[:, 1], fr[:, 0], fk[:, 1])


def rotary_tables(nc, d, g, chain):
    tt, tsc, _, _ = arithmetic(nc, chain)
    fk, nw, fw, hd = g["fk"], g["nw"], [P, TT, D // 2], D // 2
    for n in range(2):
        for half in range(2):
            w = nw[:, n, half * hd:(half + 1) * hd].rearrange("p (o n) -> p o n", o=1).to_broadcast(fw)
            tt(g["rope_c"][:, n, :, half * hd:(half + 1) * hd], fk[:, 1], w, ALU.mult)
            other = 1 - half
            tt(g["rope_s"][:, n, :, other * hd:(other + 1) * hd], fk[:, 0], w, ALU.mult)
        tsc(g["rope_s"][:, n, :, 0:hd], g["rope_s"][:, n, :, 0:hd], -1.0, 0.0, ALU.mult, ALU.add)


def conv_phase(nc, d, g, following):
    AHEAD = KT - 1
    SG = 4
    steps = S // SG
    TZ = 4
    xh, xl = g["xh"], g["xl"]
    with ExitStack() as ctx:
        c = Core(nc, ctx)
        xr = g["xr"]
        tz = [c.sb(f"c_tz{n}", [P, SG, H]) for n in range(TZ)]
        y = [c.sb(f"c_y{n}", [P, SG, KT, B]) for n in range(2)]
        acc = [c.ps(f"c_acc{n}", [P, SG, KT, B]) for n in range(2)]
        t_in = [c.sem(f"conv_t_in{n}") for n in range(TZ)]
        done, masked, hi_done, lo_done = (c.sem(f"conv_{n}") for n in ("done", "masked", "hi_done", "lo_done"))

        def places(part, t):
            return part[:, :, t * SG * B:(t + 1) * SG * B].rearrange("p m (s b) -> p m s b", b=B)

        with nc.Block() as block:
            @block.sync
            def _(sp):
                def load(t):
                    win = bass.AP(tensor=g["kpad"].tensor, offset=g["kpad"].offset + t * SG * KPAD + 1,
                                  ap=[[1, P], [KPAD, SG], [1, H]])
                    sp.dma_start(tz[t % TZ][:], win).then_inc(t_in[t % TZ], 16)

                for t in range(steps):
                    if t >= TZ:
                        sp.wait_ge(done, t - TZ + 1)
                    load(t)
                following.ahead_load(sp)

            @block.scalar
            def _(act):
                for t in range(steps):
                    act.wait_ge(masked, t + 1)
                    nc.scalar.activation(places(xh, t), y[t % 2][:].rearrange("p s m b -> p m s b"), ACT.Copy).then_inc(hi_done, 1)
                following.ahead_high(act)

            @block.gpsimd
            def _(pool):
                following.ahead_low(pool)

            @block.vector
            def _(dve):
                mask = g["lmask"][:].rearrange("p (o m) b -> p o m b", o=1).to_broadcast([P, SG, KT, B])
                for t in range(steps):
                    dve.wait_ge(done, t + 1)
                    if t >= 2:
                        dve.wait_ge(lo_done, t - 1)
                    nc.vector.tensor_tensor(y[t % 2][:], acc[t % 2][:], mask, ALU.mult).then_inc(masked, 1)
                    dve.wait_ge(hi_done, t + 1)
                    nc.vector.tensor_tensor(places(xl, t), y[t % 2][:].rearrange("p s m b -> p m s b"), f32(places(xh, t)), ALU.subtract).then_inc(lo_done, 1)

            @block.tensor
            def _(pe):
                pe.wait_ge(g["xr_in"], 16)
                pe.wait_ge(g["xr_zeroed"], 1)
                for t in range(steps):
                    pe.wait_ge(t_in[t % TZ], 16 * (t // TZ + 1))
                    if t >= 2:
                        pe.wait_ge(masked, t - 1)
                    for s in range(SG):
                        for dd in range(KT):
                            last = nc.tensor.matmul(acc[t % 2][:, s], tz[t % TZ][:, s, dd * P:(dd + 1) * P],
                                                    xr[:, t * SG + s, AHEAD - dd:AHEAD - dd + KT, :], start=dd == 0, stop=dd == KT - 1)
                    last.then_inc(done, 1)


class WeightSlots:
    def __init__(self, c, tag, cols, ternary_only=False):
        self.all_raw, self.all_hi = c.sb(f"{tag}_raw", [P, 2 * cols]), c.sb(f"{tag}_hi", [P, 2 * cols], F32R)
        all_lo = self.all_raw if ternary_only else c.sb(f"{tag}_lo", [P, 2 * cols], F32R)
        self.raw, self.hi, self.lo = ([x[:, n * cols:(n + 1) * cols] for n in range(2)] for x in (self.all_raw, self.all_hi, all_lo))


class WeightStream:
    def __init__(self, nc, c, tag, slots, w_dram, cols, n_k, unroll, thresholds=None):
        self.nc, self.w_dram, self.n_k, self.unroll = nc, w_dram, n_k, unroll
        self.per = unroll // 2
        self.raw, self.hi, self.lo = ([x[:, 0:cols] for x in part] for part in (slots.raw, slots.hi, slots.lo))
        self.thresholds = thresholds
        self.sign = c.sb(f"{tag}_sign", [P, H]) if thresholds else None
        self.w_in = [c.sem(f"{tag}_w_in{n}") for n in range(2)]
        self.w_hi, self.w_ready, self.used = (c.sem(f"{tag}_{n}") for n in ("w_hi", "w_ready", "used"))
        self.ahead = False

    def load(self, sp, t, u, i):
        if not early(t, 2):
            sp.wait_ge(self.w_ready, self.ready(t - 2))
        sp.dma_start(self.raw[u % 2], self.w_dram[at(t)].rearrange("o p m -> (o p) m")).then_inc(self.w_in[u % 2], 16)

    def high_part(self, act, t, u, i):
        act.wait_ge(self.w_in[u % 2], 16 * (i * self.per + u // 2 + 1))
        if not early(t, 2):
            act.wait_ge(self.used, t - 1)
        self.nc.scalar.activation(self.hi[u % 2], self.raw[u % 2], ACT.Copy).then_inc(self.w_hi, 1)

    def low_part(self, pool, t, u, i):
        pool.wait_ge(self.w_hi, t + 1)
        self.nc.gpsimd.tensor_tensor(self.lo[u % 2], self.raw[u % 2], f32(self.hi[u % 2]), ALU.subtract).then_inc(self.w_ready, 1)

    def to_ternary(self, dve, t, u, i):
        parts = len(self.thresholds)
        dve.wait_ge(self.w_in[u % 2], 16 * (i * self.per + u // 2 + 1))
        if not early(t, 2):
            dve.wait_ge(self.used, t - 1)
        for n, (above, below) in enumerate(self.thresholds):
            cols = slice(n * H, (n + 1) * H)
            raw, sign = self.raw[u % 2][:, cols], self.sign[:]
            if n:
                dve.wait_ge(self.w_ready, parts * t + n)
            self.nc.vector.tensor_scalar(sign, raw, below, None, ALU.is_lt, ALU.bypass).then_inc(self.w_hi, 1)
            dve.wait_ge(self.w_hi, parts * t + (n + 1))
            self.nc.vector.scalar_tensor_tensor(self.hi[u % 2][:, cols], raw, above, sign, ALU.is_gt, ALU.subtract).then_inc(self.w_ready, 1)
        dve.wait_ge(self.w_ready, parts * t + parts)

    def ready(self, t):
        return t + 1 if not self.thresholds else len(self.thresholds) * (t + 1)

    def run(self, eng, step):
        run_steps(eng, self.n_k, self.unroll, lambda t, u, i: None if self.ahead and early(t, 2) else step(eng, t, u, i))

    def ahead_load(self, sp):
        for t in range(2):
            self.load(sp, t, t, 0)
        self.ahead = True

    def ahead_high(self, act):
        for t in range(2):
            self.high_part(act, t, t, 0)

    def ahead_low(self, pool):
        for t in range(2):
            self.low_part(pool, t, t, 0)

    def ahead_ternary(self, dve):
        for t in range(2):
            self.to_ternary(dve, t, t, 0)


def gate_up_phase(nc, d, g, hh, hl, tag, w, func, gate_scale, up_scale, following, gate_room, vector_first=None, scalar_last=None):
    xh, xl = g["xh"], g["xl"]
    W = KT * P
    ternary = w.thresholds
    with ExitStack() as ctx:
        c = Core(nc, ctx)
        sg = [gate_room[:, n * TOK:(n + 1) * TOK] for n in range(2)]
        hf = gate_room[:, 2 * TOK:3 * TOK]
        acc = [c.ps(f"{tag}_acc{n}", [P, 2, TOK]) for n in range(2)]
        gated, h_full, h_done = (c.sem(f"{tag}_{n}") for n in ("gated", "h_full", "h_done"))
        link, first_done = c.sem(f"{tag}_dve_chain"), c.sem(f"{tag}_first_done")
        with nc.Block() as block:
            @block.sync
            def _(sp):
                w.run(sp, w.load)
                following.ahead_load(sp)

            @block.scalar
            def _(act):
                def gate(t, u, i):
                    act.wait_ge(w.used, t + 1)
                    if not early(t, 2):
                        act.wait_ge(h_full, t - 1)
                    nc.scalar.activation(sg[u], acc[u][:, 0, :], func, scale=gate_scale(t)).then_inc(gated, 1)

                def step(t, u, i):
                    if not ternary:
                        if early(t, 1):
                            if not w.ahead:
                                w.high_part(act, 0, 0, 0)
                                w.high_part(act, 1, 1, 0)
                        elif not isinstance(t, int):
                            w.high_part(act, t + 1, 1 - u, i if u == 0 else i + 1)
                        elif t + 1 < IT:
                            w.high_part(act, t + 1, 1 - u, (t + 1) // 2)
                        else:
                            following.ahead_high(act)
                    gate(t, u, i)

                run_steps(act, IT, 2, step)
                if scalar_last:
                    act.wait_ge(first_done, 1)
                    scalar_last()

            @block.gpsimd
            def _(pool):
                if not ternary:
                    w.run(pool, w.low_part)
                    following.ahead_low(pool)

            @block.vector
            def _(dve):
                def hidden(t, u, i):
                    dve.wait_ge(gated, t + 1)
                    nc.vector.scalar_tensor_tensor(hf, acc[u][:, 1, :], up_scale(t), sg[u], ALU.mult, ALU.mult).then_inc(h_full, 1)
                    dve.wait_ge(h_full, t + 1)
                    th, tl = (m[:, at(t), :].rearrange("p o n -> p (o n)") for m in (hh, hl))
                    nc.vector.tensor_copy(th, hf).then_inc(h_done, 1)
                    dve.wait_ge(h_done, 2 * t + 1)
                    nc.vector.tensor_tensor(tl, hf, f32(th), ALU.subtract).then_inc(h_done, 1)
                    dve.wait_ge(h_done, 2 * t + 2)

                def step(t, u, i):
                    if ternary:
                        if early(t, 1):
                            if not w.ahead:
                                w.to_ternary(dve, 0, 0, 0)
                                w.to_ternary(dve, 1, 1, 0)
                        elif not isinstance(t, int):
                            w.to_ternary(dve, t + 1, 1 - u, i if u == 0 else i + 1)
                        elif t + 1 < IT:
                            w.to_ternary(dve, t + 1, 1 - u, (t + 1) // 2)
                        else:
                            following.ahead_ternary(dve)
                    hidden(t, u, i)

                if vector_first:
                    count = [0]

                    def chain(ins):
                        count[0] += 1
                        ins.then_inc(link, 1)
                        dve.wait_ge(link, count[0])

                    vector_first(chain)
                    dve.sem_inc(first_done, 1)
                run_steps(dve, IT, 2, step)

            @block.tensor
            def _(pe):
                def product(t, u, i):
                    pe.wait_ge(w.w_ready, w.ready(t))
                    if not early(t, 2):
                        pe.wait_ge(h_full, t - 1)
                    for n in range(2):
                        for k in range(KT):
                            cols = slice(n * W + k * P, n * W + (k + 1) * P)
                            for half in range(2):
                                out = acc[u][:, n, half * HALF:(half + 1) * HALF]
                                x_h, x_l = (m[:, k, half * HALF:(half + 1) * HALF] for m in (xh, xl))
                                if ternary:
                                    nc.tensor.matmul(out, w.hi[u][:, cols], x_h, start=k == 0, stop=False)
                                    last = nc.tensor.matmul(out, w.hi[u][:, cols], x_l, start=False, stop=k == KT - 1)
                                else:
                                    last = three_passes(nc, out, w.hi[u][:, cols], w.lo[u][:, cols], x_h, x_l, k == 0, k == KT - 1)
                    last.then_inc(w.used, 1)

                run_steps(pe, IT, 2, product)


def accumulate_phase(nc, d, g, tag, w, moving, finish, produce=None, load_extra=None, first=None, vector_first=None,
                     side=None, store=None, following=None, token_major=False):
    n_k, unroll, ternary = w.n_k, w.unroll, w.thresholds
    with ExitStack() as ctx:
        c = Core(nc, ctx)
        acc = c.ps(f"{tag}_acc", [P, KT, TOK])
        made, sums, whole_done, high_done, low_done, low_done_g = (
            c.sem(f"{tag}_{n}") for n in ("made", "sums", "whole_done", "high_done", "low_done", "low_done_gpsimd"))
        stored, link = c.sem(f"{tag}_stored"), c.sem(f"{tag}_dve_chain")
        low_on_gpsimd = [m for m in range(KT) if finish.low and finish.whole and m % 2]

        with nc.Block() as block:
            @block.sync
            def _(sp):
                def step(t, u, i):
                    if not (w.ahead and early(t, 2)):
                        w.load(sp, t, u, i)
                    if load_extra:
                        load_extra(sp, t, u, i, made)

                run_steps(sp, n_k, unroll, step)
                if following:
                    following.ahead_load(sp)
                if store:
                    for m in range(KT):
                        sp.wait_ge(whole_done, m + 1)
                        store(sp, m).then_inc(stored, 16)
                    sp.wait_ge(stored, 16 * KT)

            @block.scalar
            def _(act):
                if not ternary:
                    w.run(act, w.high_part)
                if following:
                    following.ahead_high(act)
                if finish.high:
                    for m in range(KT):
                        if finish.whole:
                            act.wait_ge(whole_done, m + 1)
                        else:
                            act.wait_ge(sums, m + 1)
                        finish.high(m, acc[:, m, :]).then_inc(high_done, 1)

            @block.gpsimd
            def _(pool):
                if not ternary:
                    w.run(pool, w.low_part)
                if following:
                    following.ahead_low(pool)
                for m in low_on_gpsimd:
                    pool.wait_ge(high_done, m + 1)
                    finish.low(nc.gpsimd, m, acc[:, m, :]).then_inc(low_done_g, 1)

            @block.vector
            def _(dve):
                def make(t, u, i):
                    if not early(t, 2):
                        dve.wait_ge(w.used, t - 1)
                    produce(dve, t, u, i, made)

                if ternary:
                    w.run(dve, w.to_ternary)
                count = [0]

                def chain(ins):
                    count[0] += 1
                    ins.then_inc(link, 1)
                    dve.wait_ge(link, count[0])

                if vector_first:
                    vector_first(chain)
                if produce:
                    run_steps(dve, n_k, unroll, make)
                if side:
                    run_steps(dve, n_k, unroll, lambda t, u, i: side(dve, t, u, i))

                def low(m):
                    if finish.low and m not in low_on_gpsimd:
                        dve.wait_ge(high_done, m + 1)
                        finish.low(nc.vector, m, acc[:, m, :]).then_inc(low_done, 1)

                for m in range(KT):
                    if finish.whole:
                        dve.wait_ge(sums, m + 1)
                        finish.whole(m, acc[:, m, :]).then_inc(whole_done, 1)
                        if m:
                            low(m - 1)
                    else:
                        low(m)
                if finish.whole:
                    low(KT - 1)

            @block.tensor
            def _(pe):
                if first:
                    first(pe, acc)

                def product(t, u, i):
                    pe.wait_ge(w.w_ready, w.ready(t))
                    if produce:
                        pe.wait_ge(made, 2 * t + 2)
                    opens = isinstance(t, int) and t == 0 and not first
                    closes = isinstance(t, int) and t == n_k - 1
                    for m in range(KT):
                        cols = slice(m * P, (m + 1) * P)
                        for half in range(2):
                            out = acc[:, m, half * HALF:(half + 1) * HALF]
                            x_h, x_l = moving(t, u, i, 2 * m + half if token_major else half)
                            if token_major:
                                last = three_passes(nc, out, x_h, x_l, w.hi[u % 2], w.lo[u % 2], opens, closes)
                            elif ternary:
                                nc.tensor.matmul(out, w.hi[u % 2][:, cols], x_h, start=opens, stop=False)
                                last = nc.tensor.matmul(out, w.hi[u % 2][:, cols], x_l, start=False, stop=closes)
                            else:
                                last = three_passes(nc, out, w.hi[u % 2][:, cols], w.lo[u % 2][:, cols], x_h, x_l, opens, closes)
                        if closes:
                            last.then_inc(sums, 1)
                    if not closes:
                        last.then_inc(w.used, 1)

                run_steps_closing(pe, n_k, unroll, product)


def run_steps_closing(eng, n, unroll, step):
    if n % unroll or n <= 2 * unroll:
        run_steps(eng, n, unroll, step)
        return
    whole = n // unroll
    for u in range(unroll):
        step(u, u, 0)
    with eng.Fori(1, whole - 1) as i:
        for u in range(unroll):
            step(i * unroll + u, u, i)
    for u in range(unroll):
        step((whole - 1) * unroll + u, u, whole - 1)


class Finish:
    def __init__(self, whole=None, high=None, low=None):
        self.whole, self.high, self.low = whole, high, low


def onto_residual(nc, g, scalar, batch_major=True, split=True):
    resid, xh, xl = g["resid"], g["xh"], g["xl"]

    def whole(m, acc):
        r = resid[:, m, :]
        if not batch_major:
            r, acc = r.rearrange("p (b s) -> p s b", b=B), acc.rearrange("p (s b) -> p s b", b=B)
        return nc.vector.scalar_tensor_tensor(r, acc, scalar(m), r, ALU.mult, ALU.add)

    if not split:
        return Finish(whole=whole)
    return Finish(whole=whole, high=lambda m, acc: nc.scalar.activation(xh[:, m, :], resid[:, m, :], ACT.Copy),
                  low=lambda eng, m, acc: eng.tensor_tensor(xl[:, m, :], resid[:, m, :], f32(xh[:, m, :]), ALU.subtract))


def resident(hi, lo):
    def moving(t, u, i, half):
        cols = slice(half * HALF, (half + 1) * HALF)
        if isinstance(t, int):
            return hi[:, t, cols], lo[:, t, cols]
        return tuple(m[:, at(t), cols].rearrange("p o n -> p (o n)") for m in (hi, lo))
    return moving


def project_phase(nc, d, g, cache):
    xh, xl = g["xh"], g["xl"]
    W = REP * D
    V_GROUPS = HK // REP
    n_groups = GROUPS + V_GROUPS
    NQ = GROUPS * TT
    NV = V_GROUPS * TT
    ACC = 4
    with ExitStack() as ctx:
        c = Core(nc, ctx)
        raw = [c.sb(f"q_raw{n}", [P, KT, W]) for n in range(2)]
        wh = [c.sb(f"q_wh{n}", [P, KT, W], F32R) for n in range(2)]
        wl = [c.sb(f"q_wl{n}", [P, KT, W], F32R) for n in range(2)]
        sq = c.sb("q_sq", [P, REP, D])
        ss, rt, rs = ([c.sb(f"q_{x}{n}", [P, REP]) for n in range(2)] for x in ("ss", "rt", "rs"))
        qn, qc, qs, qr = ([c.sb(f"q_{x}{n}", [P, REP, D]) for n in range(2)] for x in ("qn", "qc", "qs", "qr"))
        st = [c.sb(f"q_st{n}", [P, BPT, REP, S]) for n in range(2)]
        vs = [c.sb(f"q_vs{n}", [P, W]) for n in range(2)]
        eps = c.sb("q_eps", [P, 1])
        acc = [c.ps(f"q_acc{n}", [P, REP, D]) for n in range(ACC)]
        tp = [c.ps(f"q_tp{n}", [P, REP, P]) for n in range(2)]
        p_tot = c.ps("q_ptot", [P, 4])
        tot, ones = c.sb("q_tot", [P, 3]), c.sb("q_ones", [P, P])
        row_sums, totals, link = c.sem("qkv_row_sums"), c.sem("qkv_totals"), c.sem("qkv_chain")
        w_in = [c.sem(f"qkv_w_in{n}") for n in range(2)]
        w_hi, w_ready = c.sem("qkv_w_hi"), c.sem("qkv_w_ready")
        done, squared, summed, rooted, inverse, normed, cosed, sined, rotated, turned, staged, eps_set, v_staged = (
            c.sem(f"qkv_{n}") for n in ("done", "squared", "summed", "rooted", "inverse", "normed", "cosed", "sined",
                                        "rotated", "turned", "staged", "eps_set", "v_staged"))
        stored = [c.sem(f"qkv_stored{n}") for n in range(2)]
        v_stored = [c.sem(f"qkv_v_stored{n}") for n in range(2)]

        def rotary_steps(eng, step):
            for slot in range(2):
                for tile in range(TT):
                    step(slot, slot, tile, slot * TT + tile, 0)
            with eng.Fori(1, HK // 2) as i:
                for slot in range(2):
                    for tile in range(TT):
                        step(i * 2 + slot, slot, tile, i * (2 * TT) + (slot * TT + tile), 0)
            for grp in range(HK, GROUPS):
                for tile in range(TT):
                    step(grp, grp % 2, tile, grp * TT + tile, 1)

        with nc.Block() as block:
            @block.sync
            def _(sp):
                def load(grp, slot):
                    sp.dma_start(raw[slot][:], d["w1_qkv"][at(grp)].rearrange("o p (k m) -> (o p) k m", k=KT)).then_inc(w_in[slot], 16)

                load(0, 0)
                load(1, 1)
                cache.load_keys(sp, 0, 0)

                def step(grp, slot, tile, n, table):
                    if tile == 1 and not (isinstance(grp, int) and grp + 2 >= n_groups):
                        sp.wait_ge(w_ready, (grp + 1) * KT)
                        load(grp + 2, slot)
                    u = tile % 2
                    sp.wait_ge(staged, n + 1)
                    dst = g["qk_scr"][tile * BPT:(tile + 1) * BPT, :, at(grp), :].rearrange("b p o r -> p b (o r)")
                    sp.dma_start(dst, st[u][:].rearrange("p b r s -> p b (r s)")).then_inc(stored[u], 16)

                rotary_steps(sp, step)
                for n in range(NV):
                    grp, tile = divmod(n, TT)
                    sp.wait_ge(v_staged, n + 1)
                    sp.dma_start(g["v_scr"][tile * P:(tile + 1) * P, grp * W:(grp + 1) * W], vs[n % 2][:]).then_inc(v_stored[n % 2], 16)
                for u in range(2):
                    sp.wait_ge(stored[u], 16 * (NQ // 2))
                    sp.wait_ge(v_stored[u], 16 * (NV // 2))

            def weight_piece(grp, tile):
                return tile - 1 if 1 <= tile <= KT and not (isinstance(grp, int) and grp + 1 >= n_groups) else None

            @block.gpsimd
            def _(pool):
                def low_part(grp, slot, k):
                    pool.wait_ge(w_hi, grp * KT + k + 1)
                    nc.gpsimd.tensor_tensor(wl[slot][:, k], raw[slot][:, k], f32(wh[slot][:, k]), ALU.subtract).then_inc(w_ready, 1)

                def step(grp, slot, tile, n, table):
                    u = tile % 2
                    pool.wait_ge(normed, n + 1)
                    if not early(n, 2):
                        pool.wait_ge(rotated, n - 1)
                    tab = g["rope_c"][:, table, tile, :].rearrange("p (o n) -> p o n", o=1).to_broadcast([P, REP, D])
                    nc.gpsimd.tensor_tensor(qc[u][:], qn[u][:], tab, ALU.mult).then_inc(cosed, 1)
                    k = weight_piece(grp, tile)
                    if k is not None:
                        low_part(grp + 1, 1 - slot, k)

                for k in range(KT):
                    low_part(0, 0, k)
                cache.take_rows(pool, 0, 0)
                for j in range(VCH):
                    cache.load_values(0, j)
                rotary_steps(pool, step)
                for k in range(KT):
                    low_part(n_groups - 1, 1, k)

            @block.scalar
            def _(act):
                act.wait_ge(eps_set, 1)

                def high_part(grp, slot, k):
                    if k == 0:
                        act.wait_ge(w_in[slot], (grp - slot) * 8 + 16)
                        if not early(grp, 2):
                            act.wait_ge(done, (grp - 1) * TT)
                    nc.scalar.activation(wh[slot][:, k], raw[slot][:, k], ACT.Copy).then_inc(w_hi, 1)

                def evacuate(n, u):
                    act.wait_ge(turned, n + 1)
                    if not early(n, 2):
                        act.wait_ge(stored[u], (n - u) * 8)
                    nc.scalar.activation(st[u][:].rearrange("p b r s -> p r b s"),
                                         tp[u][:].rearrange("p r (b s) -> p r b s", b=BPT), ACT.Copy).then_inc(staged, 1)

                def step(grp, slot, tile, n, table):
                    u = tile % 2
                    act.wait_ge(done, n + 1)
                    if not early(n, 1):
                        act.wait_ge(summed, n)
                    nc.scalar.activation(sq[:], acc[tile % ACC][:], ACT.Square).then_inc(squared, 1)
                    if not early(n, 3):
                        evacuate(n - 3, 1 - u)
                    k = weight_piece(grp, tile)
                    if k is not None:
                        high_part(grp + 1, 1 - slot, k)
                    act.wait_ge(summed, n + 1)
                    if not early(n, 2):
                        act.wait_ge(inverse, n - 1)
                    nc.scalar.activation(rt[u][:], ss[u][:], ACT.Sqrt, bias=eps[:], scale=1.0 / D).then_inc(rooted, 1)

                for k in range(KT):
                    high_part(0, 0, k)
                rotary_steps(act, step)
                for n in range(NQ - 3, NQ):
                    evacuate(n, n % 2)
                for k in range(KT):
                    high_part(n_groups - 1, 1, k)
                for n in range(NV):
                    act.wait_ge(done, NQ + n + 1)
                    if n >= 2:
                        act.wait_ge(v_stored[n % 2], 16 * (n // 2))
                    nc.scalar.activation(vs[n % 2][:], acc[n % ACC][:].rearrange("p r d -> p (r d)"), ACT.Copy).then_inc(v_staged, 1)

            @block.vector
            def _(dve):
                nc.vector.memset(eps[:], RMS_EPS).then_inc(eps_set, 1)
                hd = D // 2
                count = [0]

                def chain(ins):
                    count[0] += 1
                    ins.then_inc(link, 1)
                    dve.wait_ge(link, count[0])

                chain(nc.vector.memset(ones[:], 1.0))
                chain(nc.vector.reduce_sum(tot[:], g["rows"][:].rearrange("p t n -> p n t"), AX_X))
                dve.sem_inc(row_sums, 1)
                dve.wait_ge(totals, 1)
                chain(nc.vector.tensor_scalar(g["scale3"][:], p_tot[:, 0:3], 1.0 / (INTER * H), None, ALU.mult, ALU.bypass))
                chain(nc.vector.tensor_scalar(g["thr3"][:, 0:3], g["scale3"][:], BIT_EPS, 0.5, ALU.add, ALU.mult))
                chain(nc.vector.tensor_scalar(g["thr3"][:, 3:6], g["thr3"][:, 0:3], -1.0, 0.0, ALU.mult, ALU.add))

                def add(n, u):
                    dve.wait_ge(cosed, n + 1)
                    dve.wait_ge(sined, 2 * n + 2)
                    if not early(n, 2):
                        dve.wait_ge(turned, n - 1)
                    nc.vector.tensor_tensor(qr[u][:], qc[u][:], qs[u][:], ALU.add).then_inc(rotated, 1)

                def step(grp, slot, tile, n, table):
                    u = tile % 2
                    dve.wait_ge(squared, n + 1)
                    if not early(n, 2):
                        dve.wait_ge(rooted, n - 1)
                    nc.vector.reduce_sum(ss[u][:], sq[:], AX_X).then_inc(summed, 1)
                    if not early(n, 1):
                        add(n - 1, 1 - u)
                    dve.wait_ge(rooted, n + 1)
                    nc.vector.reciprocal(rs[u][:], rt[u][:]).then_inc(inverse, 1)
                    dve.wait_ge(inverse, n + 1)
                    if not early(n, 2):
                        dve.wait_ge(cosed, n - 1)
                    nc.vector.tensor_tensor(qn[u][:], acc[tile % ACC][:], rs[u][:].rearrange("p (r o) -> p r o", o=1).to_broadcast([P, REP, D]),
                                            ALU.mult).then_inc(normed, 1)
                    dve.wait_ge(normed, n + 1)
                    if not early(n, 2):
                        dve.wait_ge(rotated, n - 1)
                    for half in range(2):
                        tab = g["rope_s"][:, table, tile, half * hd:(half + 1) * hd].rearrange("p (o n) -> p o n", o=1).to_broadcast([P, REP, hd])
                        nc.vector.tensor_tensor(qs[u][:, :, half * hd:(half + 1) * hd], qn[u][:, :, (1 - half) * hd:(2 - half) * hd],
                                                tab, ALU.mult).then_inc(sined, 1)

                rotary_steps(dve, step)
                add(NQ - 1, 1)

            @block.tensor
            def _(pe):
                pe.wait_ge(row_sums, 1)
                nc.tensor.matmul(p_tot[:, 0:3], ones[:], tot[:], start=True, stop=True).then_inc(totals, 1)

                def project(grp, slot, tile, n):
                    if tile == 0:
                        pe.wait_ge(w_ready, (grp + 1) * KT)
                    if not early(n, ACC):
                        if isinstance(n, int) and n >= NQ + ACC:
                            pe.wait_ge(v_staged, n - NQ - ACC + 1)
                        else:
                            pe.wait_ge(normed, n - ACC + 1)
                    for k in range(KT):
                        rows = slice(tile * P, (tile + 1) * P)
                        last = three_passes(nc, acc[tile % ACC][:].rearrange("p r d -> p (r d)"), xh[:, k, rows], xl[:, k, rows],
                                            wh[slot][:, k], wl[slot][:, k], k == 0, k == KT - 1)
                    last.then_inc(done, 1)

                def transpose(n, u):
                    pe.wait_ge(rotated, n + 1)
                    if not early(n, 2):
                        pe.wait_ge(staged, n - 1)
                    for r in range(REP):
                        last = nc.tensor.transpose(tp[u][:, r, :], qr[u][:, r, :], g["ident"][:])
                    last.then_inc(turned, 1)

                def step(grp, slot, tile, n, table):
                    project(grp, slot, tile, n)
                    if not early(n, 2):
                        transpose(n - 2, tile % 2)

                rotary_steps(pe, step)
                for n in range(NQ, NQ + NV):
                    project(n // TT, (n // TT) % 2, n % TT, n)
                    if n < NQ + 2:
                        transpose(n - 2, n % 2)


class CacheLoads:
    def __init__(self, nc, c, d, g):
        self.nc, self.d, self.g = nc, d, g
        self.keys = [c.sb("a_kb0", [P, NPP, HK, PSIZE])]
        self.values = [c.sb("a_vb0", [P, VCH, HK * D])]
        self.rows = [c.sb(f"a_vidx{n}", [P, VCH], I32) for n in range(2)]
        self.k_in, self.v_in = ([c.sem(f"att_{x}{n}") for n in range(2)] for x in ("k_in", "v_in"))
        self.rows_taken, self.gate = c.sem("att_rows_taken"), c.sem("att_gate_pool")

    def second_slot(self, c):
        self.keys.append(c.sb("a_kb1", [P, NPP, HK, PSIZE]))
        self.values.append(c.sb("a_vb1", [P, VCH, HK * D]))

    def load_keys(self, sp, b, s, slot_free=None):
        pages = self.nc.values_load_multi_w_load_instructions(
            self.g["bt"][0:1, bass.ds(b * NPP, NPP)], engines=[mybir.EngineType.SP], min_val=0, max_val=PAGES - 1,
            skip_runtime_bounds_check_because="the block table names pages of the cache")[1]
        if slot_free:
            slot_free()
        for j in range(NPP):
            sp.dma_start(self.keys[s][:, j].rearrange("p h k -> p (h k)"),
                         self.d["kT_pages"][bass.ds(pages[j], 1)].rearrange("o p f -> (o p) f")).then_inc(self.k_in[s], 16)

    def take_rows(self, pool, b, s):
        self.nc.gpsimd.tensor_copy(self.rows[s][:], self.g["vrow"][:, bass.ds(b * VCH, VCH)]).then_inc(self.rows_taken, 1)
        pool.wait_ge(self.rows_taken, b + 1)
        pool.sem_inc(self.gate, 1)

    def load_values(self, s, j):
        self.nc.gpsimd.indirect_dma_start(self.values[s][:, j, :], None, self.d["v_rows"],
                                          bass.IndirectOffsetOnAxis(ap=self.rows[s][:, j:j + 1], axis=0)).then_inc(self.v_in[s], 16)


def attention_phase(nc, d, g, cache):
    G = REP * S
    assert G == P
    with ExitStack() as ctx:
        c = Core(nc, ctx)
        cache.second_slot(c)
        kb, vb, k_in, v_in = cache.keys, cache.values, cache.k_in, cache.v_in
        qk = [c.sb(f"a_qk{n}", [P, GROUPS, G]) for n in range(2)]
        vn = [c.sb(f"a_vn{n}", [S, HK * D]) for n in range(2)]
        mask = [c.sb(f"a_mask{n}", [P, KEYS]) for n in range(2)]
        length = [c.sb(f"a_length{n}", [P, 1]) for n in range(2)]
        ob = [c.sb(f"a_ob{n}", [P, HK, G]) for n in range(2)]
        sm, pr, pn = ([c.sb(f"a_{x}{n}", [P, KEYS]) for n in range(2)] for x in ("sm", "pr", "pn"))
        ptm, ptn = [c.sb(f"a_ptm{n}", [P, VCH, G]) for n in range(2)], [c.sb(f"a_ptn{n}", [S, G]) for n in range(2)]
        kh, kl = ([c.sb(f"a_k{x}{n}", [P, NPP, PSIZE], F32R) for n in range(2)] for x in ("h", "l"))
        qh, ql = ([c.sb(f"a_q{x}{n}", [P, G], F32R) for n in range(2)] for x in ("h", "l"))
        mx, den, rc = (c.sb(f"a_{x}", [P, 2]) for x in ("mx", "den", "rc"))
        sc = [c.ps(f"a_sc{n}", [P, 1024]) for n in range(2)]
        tpm = [c.ps(f"a_tpm{n}", [P, VCH, G]) for n in range(2)]
        tpn = c.ps("a_tpn", [S, 2, G])
        oo = c.ps("a_oo", [P, 2, G])
        length_taken = c.sem("att_length_taken")
        qk_in, vn_in, stored = ([c.sem(f"att_{x}{n}") for n in range(2)] for x in ("qk_in", "vn_in", "stored"))
        o_moved, gate_dve = c.sem("att_o_moved"), c.sem("att_gate_dve")
        masked, scored, shifted, exped, inverse, normed, turned, moved_m, moved_n, mixed = (
            c.sem(f"att_{n}") for n in ("masked", "scored", "shifted", "exped", "inverse", "normed", "turned", "moved_m", "moved_n", "mixed"))
        high, low, low_g = (c.sem(f"att_{n}") for n in ("high", "low", "low_gpsimd"))
        NU = B * HK
        TURN = 2 * HK
        TOP = NPP // 4

        def unit_steps(eng, step):
            for u in range(TURN):
                step(u, u, 0, True)
            with eng.Fori(1, B // 2 - 1) as i:
                for u in range(TURN):
                    step(i * TURN + u, u, i, True)
            last = B // 2 - 1
            for u in range(TURN):
                step(last * TURN + u, u, last, u < TURN - 2)

        def final(n):
            return isinstance(n, int) and n == NU - 1

        def ahead(n, u, i, by):
            return (n + by, u + by, i) if u + by < TURN else (n + by, u + by - TURN, i + 1)

        with nc.Block() as block:
            @block.sync
            def _(sp):
                def load(b, s):
                    if not early(b, 1):
                        cache.load_keys(sp, b, s, None if early(b, 2) else lambda: sp.wait_ge(mixed, (b - 1) * HK))
                    sp.dma_start(qk[s][:], g["qk_scr"][at(b)].rearrange("o p g r -> (o p) g r")).then_inc(qk_in[s], 16)
                    sp.dma_start(vn[s][:], g["v_scr"][bass.ds(b * S, S), :]).then_inc(vn_in[s], 16)

                def store(b, s):
                    sp.wait_ge(o_moved, (b + 1) * HK)
                    sp.dma_start(g["o_scr"][at(b)].rearrange("o p r -> (o p) r"), ob[s][:].rearrange("p h r -> p (h r)")).then_inc(stored[s], 16)

                load(0, 0)
                load(1, 1)
                with sp.Fori(1, B // 2) as i:
                    for s in range(2):
                        load(i * 2 + s, s)
                        store(i * 2 + (s - 2), s)
                for s in range(2):
                    store(B - 2 + s, s)
                    sp.wait_ge(stored[s], 16 * (B // 2))

            @block.gpsimd
            def _(pool):
                def low_keys(n, u, i):
                    v, slot, h = u % 2, u // HK, u % HK
                    pool.wait_ge(high, n + 1)
                    nc.gpsimd.tensor_tensor(kl[v][:, 0:TOP], kb[slot][:, 0:TOP, h, :], f32(kh[v][:, 0:TOP]), ALU.subtract).then_inc(low_g, 1)

                def step(n, u, i, more):
                    v, h, s = u % 2, u % HK, u // HK
                    if h == 2 and not early(n, HK) and not (isinstance(n, int) and n >= NU - HK):
                        if u < HK:
                            pool.wait_ge(mixed, i * TURN)
                            cache.take_rows(pool, i * 2 + 1, 1)
                        else:
                            pool.wait_ge(mixed, i * TURN + HK)
                            cache.take_rows(pool, i * 2 + 2, 0)
                    if not final(n):
                        low_keys(*ahead(n, u, i, 1))
                    pool.wait_ge(inverse, n + 1)
                    if not early(n, 2):
                        pool.wait_ge(turned, n - 1)
                    pool.sem_inc(cache.gate, 1)
                    nc.gpsimd.tensor_scalar(pn[v][:], pr[v][:], rc[:, v:v + 1], 1.0, ALU.mult, ALU.mult).then_inc(normed, 1)
                    if 2 <= h < 2 + VCH and not early(n, HK) and not (isinstance(n, int) and n >= NU - HK):
                        cache.load_values(1 - s, h - 2)

                low_keys(0, 0, 0)
                cache.take_rows(pool, 1, 1)
                for j in range(VCH):
                    cache.load_values(1, j)
                unit_steps(pool, step)

            @block.scalar
            def _(act):
                def move_main(n, u):
                    act.wait_ge(turned, n + 1)
                    if not early(n, 2):
                        act.wait_ge(mixed, n - 1)
                    nc.scalar.activation(ptm[u][:], tpm[u][:], ACT.Copy).then_inc(moved_m, 1)

                def high_parts(n, u, i):
                    v, slot, h = u % 2, u // HK, u % HK
                    if h == 0:
                        act.wait_ge(k_in[slot], (i + 1) * (16 * NPP))
                        act.wait_ge(qk_in[slot], (i + 1) * 16)
                    if not early(n, 2):
                        act.wait_ge(scored, n - 1)
                    nc.scalar.activation(qh[v][:], qk[slot][:, h, :], ACT.Copy)
                    nc.scalar.activation(kh[v][:], kb[slot][:, :, h, :], ACT.Copy).then_inc(high, 1)

                def step(n, u, i, more):
                    act.wait_ge(shifted, n + 1)
                    if not early(n, 2):
                        act.wait_ge(normed, n - 1)
                    v = u % 2
                    nc.scalar.activation(pr[v][:], sm[v][:], ACT.Exp, bias=mx[:, v:v + 1], scale=-1.0,
                                         accum_out=den[:, v:v + 1]).then_inc(exped, 1)
                    if not early(n, 1):
                        move_main(n - 1, 1 - v)
                    if more:
                        high_parts(*ahead(n, u, i, 2))

                for n in range(2):
                    high_parts(n, n, 0)
                unit_steps(act, step)
                move_main(NU - 1, 1)

            @block.vector
            def _(dve):
                def move_out(n, v, s, h):
                    dve.wait_ge(mixed, n + 1)
                    if h == 0 and not early(n, 2 * HK):
                        dve.wait_ge(stored[s], (n - s * HK))
                    nc.vector.tensor_copy(ob[s][:, h, :], oo[:, v, :]).then_inc(o_moved, 1)

                def move_new(n, v):
                    dve.wait_ge(turned, n + 1)
                    if not early(n, 2):
                        dve.wait_ge(mixed, n - 1)
                    nc.vector.tensor_copy(ptn[v][:], tpn[:, v, :]).then_inc(moved_n, 1)

                def take_length(b, s):
                    nc.vector.tensor_copy(length[s][:], g["lens"][:, 1, at(b)]).then_inc(length_taken, 1)

                def make_mask(b, s):
                    dve.wait_ge(length_taken, b + 1)
                    if not early(b, 2):
                        dve.wait_ge(shifted, (b - 1) * HK)
                    dve.sem_inc(gate_dve, 1)
                    nc.vector.tensor_scalar(mask[s][:], g["keyidx"][:], length[s][:], NEG, ALU.is_ge, ALU.mult).then_inc(masked, 1)

                def low_parts(n, u, i):
                    v, slot, h = u % 2, u // HK, u % HK
                    dve.wait_ge(high, n + 1)
                    nc.vector.tensor_tensor(ql[v][:], qk[slot][:, h, :], f32(qh[v][:]), ALU.subtract)
                    nc.vector.tensor_tensor(kl[v][:, TOP:], kb[slot][:, TOP:, h, :], f32(kh[v][:, TOP:]), ALU.subtract).then_inc(low, 1)

                def step(n, u, i, more):
                    v, s, h = u % 2, u // HK, u % HK
                    next_batch = not (isinstance(n, int) and n >= NU - HK)
                    if h == 0:
                        dve.wait_ge(masked, i * 2 + s + 1)
                    dve.wait_ge(scored, n + 1)
                    if not early(n, 2):
                        dve.wait_ge(exped, n - 1)
                    dve.sem_inc(gate_dve, 1)
                    nc.vector.tensor_tensor_reduce(out=sm[v][:], in0=sc[v][:, 0:KEYS], in1=mask[s][:], scale=-ATT_SCALE, scalar=3e38,
                                                   op0=ALU.add, op1=ALU.min, accum_out=mx[:, v:v + 1]).then_inc(shifted, 1)
                    if not final(n):
                        low_parts(*ahead(n, u, i, 1))
                    dve.wait_ge(exped, n + 1)
                    if not early(n, 2):
                        dve.wait_ge(normed, n - 1)
                    nc.vector.reciprocal(rc[:, v:v + 1], den[:, v:v + 1]).then_inc(inverse, 1)
                    if not early(n, 2):
                        w = u - 2 if u >= 2 else u + 2 * HK - 2
                        move_out(n - 2, v, w // HK, w % HK)
                    if not early(n, 1):
                        move_new(n - 1, 1 - v)
                    if next_batch and h == 4:
                        take_length(i * 2 + (s + 1), 1 - s)
                    if next_batch and h == 5:
                        make_mask(i * 2 + (s + 1), 1 - s)

                take_length(0, 0)
                make_mask(0, 0)
                low_parts(0, 0, 0)
                unit_steps(dve, step)
                move_out(NU - 2, 0, 1, HK - 2)
                move_new(NU - 1, 1)
                move_out(NU - 1, 1, 1, HK - 1)

            @block.tensor
            def _(pe):
                def score(n, u, s, h, i):
                    v = u % 2
                    pe.wait_ge(low, n + 1)
                    pe.wait_ge(low_g, n + 1)
                    if not early(n, 2):
                        pe.wait_ge(shifted, n - 1)
                    new = qk[s][:, HK + h // REP, (h % REP) * S:(h % REP + 1) * S]
                    three_passes(nc, sc[v][:, 0:CACHE].rearrange("p (j k) -> p j k", k=PSIZE), qh[v][:], ql[v][:], kh[v][:], kl[v][:], True, True)
                    nc.tensor.matmul(sc[v][:, CACHE:KEYS], qk[s][:, h, :], new, start=True, stop=True).then_inc(scored, 1)

                def turn(n, u):
                    v = u % 2
                    pe.wait_ge(normed, n + 1)
                    if not early(n, 2):
                        pe.wait_ge(moved_m, n - 1)
                        pe.wait_ge(moved_n, n - 1)
                    for j in range(VCH):
                        nc.tensor.transpose(tpm[v][:, j, :], pn[v][:, j * P:(j + 1) * P], g["ident"][:])
                    nc.tensor.transpose(tpn[:, v, :], pn[v][:, CACHE:KEYS], g["ident"][:]).then_inc(turned, 1)

                def mix(n, u, s, h, i):
                    v = u % 2
                    if h == 0:
                        pe.wait_ge(v_in[s], (i + 1) * (16 * VCH))
                        pe.wait_ge(vn_in[s], (i + 1) * 16)
                    pe.wait_ge(moved_m, n + 1)
                    pe.wait_ge(moved_n, n + 1)
                    if not early(n, 2):
                        pe.wait_ge(o_moved, n - 1)
                    for j in range(VCH):
                        nc.tensor.matmul(oo[:, v, :], vb[s][:, j, h * D:(h + 1) * D], ptm[v][:, j, :], start=j == 0, stop=False)
                    nc.tensor.matmul(oo[:, v, :], vn[s][:, h * D:(h + 1) * D], ptn[v][:], start=False, stop=True).then_inc(mixed, 1)

                def step(u, n, i):
                    score(n, u, u // HK, u % HK, i)
                    if not early(n, 2):
                        w = u - 2 if u >= 2 else u + 2 * HK - 2
                        mix(n - 2, w, w // HK, w % HK, i if u >= 2 else i - 1)
                    if not early(n, 1):
                        turn(n - 1, u + 1)

                for u in range(2 * HK):
                    step(u, u, 0)
                with pe.Fori(1, B // 2) as i:
                    for u in range(2 * HK):
                        step(u, i * (2 * HK) + u, i)
                last = B // 2 - 1
                mix(NU - 2, 2 * HK - 2, 1, HK - 2, last)
                turn(NU - 1, 1)
                mix(NU - 1, 2 * HK - 1, 1, HK - 1, last)


def output_projection(nc, d, g, w, xt):
    assert H == HALF
    with ExitStack() as ctx:
        c = Core(nc, ctx)
        ring = [c.sb(f"wo_o{n}", [P, B, P]) for n in range(2)]
        mh, ml = ([c.sb(f"wo_{x}{n}", [P, TOK], F32R) for n in range(2)] for x in ("mh", "ml"))
        o_in = [c.sem(f"wo_o_in{n}") for n in range(2)]

        def load_extra(sp, t, u, i, made):
            if u % REP:
                return
            s = u // REP
            if not early(t, 2 * REP):
                sp.wait_ge(made, (t - REP) * 2)
            sp.dma_start(ring[s][:], g["o_scr"][:, :, bass.ds(t * S, P)].rearrange("b p r -> p b r")).then_inc(o_in[s], 16)

        def produce(dve, t, u, i, made):
            s, r = u // REP, u % REP
            if r == 0:
                dve.wait_ge(o_in[s], (i + 1) * 16)
            src = ring[s][:, :, r * S:(r + 1) * S]
            hi, lo = (m[u % 2][:].rearrange("p (b s) -> p b s", b=B) for m in (mh, ml))
            nc.vector.tensor_copy(hi, src).then_inc(made, 1)
            dve.wait_ge(made, t * 2 + 1)
            nc.vector.tensor_tensor(lo, src, f32(hi), ALU.subtract).then_inc(made, 1)

        def moving(t, u, i, tile):
            cols = slice(tile * P, (tile + 1) * P)
            return mh[u % 2][:, cols], ml[u % 2][:, cols]

        copied = Finish(high=lambda m, acc: nc.scalar.activation(xt[:, 2 * m:2 * m + 2, :].rearrange("p t f -> p (t f)"), acc, ACT.Copy))
        accumulate_phase(nc, d, g, "wo", w, moving, copied, produce=produce, load_extra=load_extra, token_major=True)


class LowRankWeights:
    PARTS = (("w2_b", KT * P), ("w3_la", KT * 2 * P), ("w3_wb", (KT + 2) * H))

    def __init__(self, nc, kept):
        self.hi = [kept.sb(f"lr_hi_{n}", [P, w], F32R) for n, w in self.PARTS]
        self.lo = [kept.sb(f"lr_lo_{n}", [P, w], F32R) for n, w in self.PARTS]
        self.fold_hi, self.fold_lo = kept.sb("lr_fold_hi", [P, H], F32R), kept.sb("lr_fold_lo", [P, H], F32R)

    def stage(self, c):
        self.a = c.sb("lr_a", [P, KT, P])
        self.fa = c.sb("lr_fa", [P, KT, 2 * P])
        self.wb = c.sb("lr_wb", [P, KT + 2, H])
        self.mixed = c.sb("lr_mixed", [P, 2, P])
        self.raw = [c.sb(f"lr_raw_{n}", [P, w]) for n, w in self.PARTS]
        self.fold_in = c.sem("lr_fold_in")
        self.part_in = [c.sem(f"lr_in_{n}") for n, w in self.PARTS]

    def load(self, sp, d):
        for dst, name in ((self.a, "w2_a"), (self.fa, "w2_fa"), (self.wb, "w2_wb")):
            sp.dma_start(dst[:], d[name]).then_inc(self.fold_in, 16)
        for n, (name, w) in enumerate(self.PARTS):
            sp.dma_start(self.raw[n][:], d[name].rearrange("p k c -> p (k c)")).then_inc(self.part_in[n], 16)

    def parts(self, n):
        k_tiles = KT + 2 if n == 2 else KT
        return tuple(x[n][:].rearrange("p (k c) -> p k c", k=k_tiles) for x in (self.hi, self.lo))


def route_phase(nc, d, g, xt, slot_of, tile_expert, x_slots, lr, probs, old_semaphores):
    E = EXPERTS
    with ExitStack() as ctx:
        c = Core(nc, ctx)
        lr.stage(c)
        gw, gb = c.sb("r_gw", [P, KT, E]), c.sb("r_gb", [P, E])
        before, ones = c.sb("r_before", [P, P]), c.sb("r_ones", [P, P])
        tile_no, tile_e = c.sb("r_tile_no", [P, SLOT_TILES]), c.sb("r_tile_e", [P, SLOT_TILES])
        zero = c.sb("r_zero", [P, H])
        x_t = c.sb("r_x_t", [P, KT, TOK])
        z_t = c.sb("r_z_t", [E, TOK])
        z, eq, sel, place = (c.sb(f"r_{x}", [P, TT, E]) for x in ("z", "eq", "sel", "place"))
        mx, taken, slot = (c.sb(f"r_{x}", [P, TT]) for x in ("mx", "taken", "slot"))
        count, tiles, start = c.sb("r_count", [P, E]), c.sb("r_tiles", [P, E]), c.sb("r_start", [P, E + 1])
        px = [c.ps(f"r_px{n}", [P, KT, P]) for n in range(2)]
        pz_t = c.ps("r_pz_t", [E, TOK])
        pz = c.ps("r_pz", [P, TT, E])
        p_rank = c.ps("r_rank", [P, 2, TT, E])
        p_fold = c.ps("r_fold", [P, H])
        w_in, link, logits, chosen, ranked, placed, scattered, zero_set, x_zeroed = (
            c.sem(f"route_{n}") for n in ("w_in", "chain", "logits", "chosen", "ranked", "placed", "scattered", "zero_set", "x_zeroed"))
        turned, x_even, x_odd, products, moved = (c.sem(f"route_{n}") for n in ("turned", "x_even", "x_odd", "products", "moved"))
        part_hi, part_lo, mixing, weighted, folding, fold_hi, fold_lo = (
            c.sem(f"route_{n}") for n in ("part_hi", "part_lo", "mixing", "weighted", "folding", "fold_hi", "fold_lo"))
        with nc.Block() as block:
            @block.sync
            def _(sp):
                sp.dma_start(gw[:], d["w1_gate"]).then_inc(w_in, 16)
                sp.dma_start(gb[:], d["L1_ffn_gate_b"].rearrange("(a s) -> a s", a=1).to_broadcast([P, E])).then_inc(w_in, 16)
                sp.dma_start(before[:], d["before"]).then_inc(w_in, 16)
                sp.dma_start(tile_no[:], d["tile_no"]).then_inc(w_in, 16)
                sp.wait_ge(zero_set, 1)
                sp.dma_start(x_slots.rearrange("(j p) f -> p j f", p=P),
                             zero[:].rearrange("p (o f) -> p o f", o=1).to_broadcast([P, SLOT_TILES, H])).then_inc(x_zeroed, 16)
                lr.load(sp, d)
                sp.sem_clear(old_semaphores)
                sp.wait_ge(scattered, 16 * TT)

            @block.tensor
            def _(pe):
                for t in range(TT):
                    if t >= 2:
                        pe.wait_ge(x_odd if t % 2 else x_even, t // 2)
                    for k in range(KT):
                        last = nc.tensor.transpose(px[t % 2][:, k, :], xt[:, t, k * P:(k + 1) * P], g["ident"][:])
                    last.then_inc(turned, 1)
                pe.wait_ge(w_in, 64)
                for half in range(2):
                    pe.wait_ge(x_even, 2 * half + 2)
                    pe.wait_ge(x_odd, 2 * half + 2)
                    cols = slice(half * HALF, (half + 1) * HALF)
                    for k in range(KT):
                        last = nc.tensor.matmul(pz_t[:, cols], gw[:, k, :], x_t[:, k, cols], start=k == 0, stop=k == KT - 1)
                    last.then_inc(products, 1)
                pe.wait_ge(moved, 2)
                for t in range(TT):
                    last = nc.tensor.transpose(pz[:, t, :], z_t[:, t * P:(t + 1) * P], g["ident"][0:E, 0:E])
                last.then_inc(logits, 1)
                pe.wait_ge(chosen, 1)
                nc.tensor.matmul(p_rank[:, 0].rearrange("p t e -> p (t e)"), before[:], sel[:].rearrange("p t e -> p (t e)"), start=True, stop=True)
                nc.tensor.matmul(p_rank[:, 1].rearrange("p t e -> p (t e)"), ones[:], sel[:].rearrange("p t e -> p (t e)"),
                                 start=True, stop=True).then_inc(ranked, 1)
                pe.wait_ge(lr.fold_in, 48)
                for j in range(2):
                    for k in range(KT):
                        last = nc.tensor.matmul(p_fold[:, j * P:(j + 1) * P], lr.fa[:, k, j * P:(j + 1) * P], lr.a[:, k, :], start=k == 0, stop=k == KT - 1)
                last.then_inc(mixing, 1)
                pe.wait_ge(weighted, 1)
                for k in range(KT):
                    nc.tensor.matmul(p_fold[:], lr.a[:, k, :], lr.wb[:, k, :], start=k == 0, stop=False)
                for j in range(2):
                    last = nc.tensor.matmul(p_fold[:], lr.mixed[:, j, :], lr.wb[:, KT + j, :], start=False, stop=j == 1)
                last.then_inc(folding, 1)

            @block.vector
            def _(dve):
                steps = [0]

                def chain(ins):
                    steps[0] += 1
                    ins.then_inc(link, 1)
                    dve.wait_ge(link, steps[0])

                tt, tsc, _, _ = arithmetic(nc, chain)
                chain(nc.vector.memset(ones[:], 1.0))
                for t in range(1, TT, 2):
                    dve.wait_ge(turned, t + 1)
                    nc.vector.tensor_copy(x_t[:, :, t * P:(t + 1) * P], px[1][:]).then_inc(x_odd, 1)
                dve.wait_ge(logits, 1)
                dve.wait_ge(w_in, 64)
                tt(z[:], pz[:], gb[:].rearrange("p (o e) -> p o e", o=1).to_broadcast([P, TT, E]), ALU.add)
                chain(nc.vector.reduce_max(mx[:], z[:], AX_X))
                tt(eq[:], z[:], mx[:].rearrange("p (t o) -> p t o", o=1).to_broadcast([P, TT, E]), ALU.is_equal)
                chain(nc.vector.memset(taken[:], 0.0))
                for j in range(E):
                    tt(sel[:, :, j], eq[:, :, j], taken[:], ALU.is_gt)
                    tt(taken[:], taken[:], eq[:, :, j], ALU.max)
                dve.sem_inc(chosen, 1)
                chain(nc.vector.memset(place[:, 0, :], 0.0))
                chain(nc.vector.memset(start[:, 0:1], 0.0))
                chain(nc.vector.memset(tile_e[:], 0.0))
                dve.wait_ge(ranked, 1)
                for t in range(1, TT):
                    tt(place[:, t, :], place[:, t - 1, :], p_rank[:, 1, t - 1, :], ALU.add)
                tt(count[:], place[:, TT - 1, :], p_rank[:, 1, TT - 1, :], ALU.add)
                tsc(tiles[:], count[:], (P - 1) / 2, 1.0 / P, ALU.add, ALU.mult)
                tsc(tiles[:], tiles[:], MAGIC, 0.0, ALU.add, ALU.add)
                tsc(tiles[:], tiles[:], -MAGIC, 0.0, ALU.add, ALU.add)
                for e in range(E):
                    tt(start[:, e + 1:e + 2], start[:, e:e + 1], tiles[:, e:e + 1], ALU.add)
                tt(place[:], place[:], p_rank[:, 0], ALU.add)
                first = start[:, 0:E].rearrange("p (o e) -> p o e", o=1).to_broadcast([P, TT, E])
                chain(nc.vector.scalar_tensor_tensor(place[:], first, float(P), place[:], ALU.mult, ALU.add))
                tt(place[:], place[:], sel[:], ALU.mult)
                chain(nc.vector.reduce_sum(slot[:], place[:], AX_X))
                nc.vector.tensor_copy(slot_of[:], slot[:]).then_inc(placed, 1)
                for e in range(E):
                    chain(nc.vector.scalar_tensor_tensor(tile_e[:], tile_no[:], start[:, e + 1:e + 2], tile_e[:], ALU.is_ge, ALU.add))
                tsc(tile_e[:], tile_e[:], float(E - 1), 0.0, ALU.min, ALU.max)
                chain(nc.vector.tensor_copy(tile_expert[:], tile_e[0:1, :]))
                dve.wait_ge(mixing, 1)
                for j in range(2):
                    tsc(lr.mixed[:, j, :], p_fold[:, j * P:(j + 1) * P], probs[:, j:j + 1], None, ALU.mult, ALU.bypass)
                dve.sem_inc(weighted, 1)
                dve.wait_ge(fold_hi, 1)
                nc.vector.tensor_tensor(lr.fold_lo[:], p_fold[:], f32(lr.fold_hi[:]), ALU.subtract).then_inc(fold_lo, 1)

            @block.scalar
            def _(act):
                for t in range(0, TT, 2):
                    act.wait_ge(turned, t + 1)
                    nc.scalar.activation(x_t[:, :, t * P:(t + 1) * P], px[0][:], ACT.Copy).then_inc(x_even, 1)
                for half in range(2):
                    cols = slice(half * HALF, (half + 1) * HALF)
                    act.wait_ge(products, half + 1)
                    nc.scalar.activation(z_t[:, cols], pz_t[:, cols], ACT.Copy).then_inc(moved, 1)
                for n in range(len(lr.PARTS)):
                    act.wait_ge(lr.part_in[n], 16)
                    nc.scalar.activation(lr.hi[n][:], lr.raw[n][:], ACT.Copy).then_inc(part_hi, 1)
                act.wait_ge(folding, 1)
                nc.scalar.activation(lr.fold_hi[:], p_fold[:], ACT.Copy).then_inc(fold_hi, 1)

            @block.gpsimd
            def _(pool):
                nc.gpsimd.memset(zero[:], 0.0).then_inc(zero_set, 1)
                pool.wait_ge(placed, 1)
                pool.wait_ge(x_zeroed, 16)
                for t in range(TT):
                    nc.gpsimd.indirect_dma_start(x_slots, bass.IndirectOffsetOnAxis(ap=slot_of[:, t:t + 1], axis=0), xt[:, t, :], None).then_inc(scattered, 16)
                for n in range(len(lr.PARTS)):
                    pool.wait_ge(part_hi, n + 1)
                    nc.gpsimd.tensor_tensor(lr.lo[n][:], lr.raw[n][:], f32(lr.hi[n][:]), ALU.subtract).then_inc(part_lo, 1)


def expert_phase(nc, d, g, slots, tile_expert, x_slots, y_slots):
    W = KT * H
    PIECES = [slice(h * W // 2, (h + 1) * W // 2) for h in range(2)]
    CUT = W // 8
    with ExitStack() as ctx:
        c = Core(nc, ctx)
        raw = [c.sb(f"e_raw{n}", [P, W]) for n in range(2)]
        wh, wl = ([c.sb(f"e_w{x}{n}", [P, W], F32R) for n in range(2)] for x in ("h", "l"))
        bias = c.sb("e_bias", [P, EXPERTS * H])
        y = [c.sb(f"e_y{n}", [P, H]) for n in range(2)]
        x = slots.raw
        xh, xl = ([part[n].rearrange("p (k s) -> p k s", k=KT) for n in range(2)] for part in (slots.hi, slots.lo))
        px = [c.ps(f"e_px{n}", [P, KT, P]) for n in range(2)]
        py = [c.ps(f"e_py{n}", [P, H]) for n in range(2)]
        w_in = [[c.sem(f"expert_w_in{n}_{h}") for h in range(2)] for n in range(2)]
        x_in, stored = ([c.sem(f"expert_{x}{n}") for n in range(2)] for x in ("x_in", "stored"))
        bias_in, gate, w_hi, w_lo, w_lo_g, turned, x_hi, x_lo, done, y_done = (
            c.sem(f"expert_{n}") for n in ("bias_in", "gate", "w_hi", "w_lo", "w_lo_gpsimd", "turned", "x_hi", "x_lo", "done", "y_done"))

        def expert_of(engine, t):
            return nc.values_load_multi_w_load_instructions(
                tile_expert[0:1, at(t)], engines=[engine], min_val=0, max_val=EXPERTS - 1,
                skip_runtime_bounds_check_because="a tile's expert is clamped to the last one")[1][0]

        with nc.Block() as block:
            @block.sync
            def _(sp):
                def load(t, u, i):
                    expert = expert_of(mybir.EngineType.SP, t)
                    for h, piece in enumerate(PIECES):
                        if not early(t, 2):
                            sp.wait_ge(w_lo, t * 2 + (h - 3))
                            sp.wait_ge(w_lo_g, t * 2 + (h - 3))
                        sp.dma_start(raw[u][:, piece], d["w1_e"][at(expert)].rearrange("o p m -> (o p) m")[:, piece]).then_inc(w_in[u][h], 16)
                    if not early(t, 2):
                        sp.wait_ge(turned, t - 1)
                    sp.dma_start(x[u], x_slots[bass.ds(t * P, P), :]).then_inc(x_in[u], 16)
                    if early(t, 1):
                        sp.dma_start(bias[:], d["L1_ffn_expert_b"].rearrange("(o e) f -> o (e f)", o=1).to_broadcast([P, EXPERTS * H])).then_inc(bias_in, 16)

                run_steps(sp, SLOT_TILES, 2, load)
                for u in range(2):
                    sp.wait_ge(stored[u], 16 * ((SLOT_TILES + 1 - u) // 2))

            @block.scalar
            def _(act):
                def high_parts(t, u, i):
                    for h, piece in enumerate(PIECES):
                        act.wait_ge(w_in[u][h], 16 * (i + 1))
                        if not early(t, 2):
                            act.wait_ge(done, t * 2 + (h - 3))
                        nc.scalar.activation(wh[u][:, piece], raw[u][:, piece], ACT.Copy).then_inc(w_hi, 1)
                    act.wait_ge(turned, t + 1)
                    nc.scalar.activation(xh[u], px[u][:], ACT.Copy).then_inc(x_hi, 1)

                run_steps(act, SLOT_TILES, 2, high_parts)

            @block.gpsimd
            def _(pool):
                def low_part(t, u, i):
                    for h, piece in enumerate(PIECES):
                        cols = slice(piece.start, piece.start + CUT)
                        pool.wait_ge(w_hi, t * 2 + (h + 1))
                        nc.gpsimd.tensor_tensor(wl[u][:, cols], raw[u][:, cols], f32(wh[u][:, cols]), ALU.subtract).then_inc(w_lo_g, 1)
                    if not early(t, 2):
                        store(t - 2, u)

                def store(t, u):
                    pool.wait_ge(y_done, t + 1)
                    nc.gpsimd.dma_start(y_slots[bass.ds(t * P, P), :], y[u][:]).then_inc(stored[u], 16)

                run_steps(pool, SLOT_TILES, 2, low_part)
                for t in (SLOT_TILES - 2, SLOT_TILES - 1):
                    store(t, t % 2)

            @block.vector
            def _(dve):
                def add_bias(t, u):
                    expert = expert_of(mybir.EngineType.DVE, t)
                    dve.wait_ge(done, t * 2 + 2)
                    if early(t, 1):
                        dve.wait_ge(bias_in, 16)
                    if not early(t, 2):
                        dve.wait_ge(stored[u], (t - u) * 8)
                    dve.sem_inc(gate, 1)
                    nc.vector.tensor_tensor(y[u][:], py[u][:], bias[:, bass.ds(expert * H, H)], ALU.add).then_inc(y_done, 1)

                def step(t, u, i):
                    for h, piece in enumerate(PIECES):
                        cols = slice(piece.start + CUT, piece.stop)
                        dve.wait_ge(w_hi, t * 2 + (h + 1))
                        nc.vector.tensor_tensor(wl[u][:, cols], raw[u][:, cols], f32(wh[u][:, cols]), ALU.subtract).then_inc(w_lo, 1)
                    dve.wait_ge(x_hi, t + 1)
                    nc.vector.tensor_tensor(xl[u], px[u][:], f32(xh[u]), ALU.subtract).then_inc(x_lo, 1)
                    if not early(t, 1):
                        add_bias(t - 1, 1 - u)

                run_steps(dve, SLOT_TILES, 2, step)
                add_bias(SLOT_TILES - 1, (SLOT_TILES - 1) % 2)

            @block.tensor
            def _(pe):
                def product(t, u):
                    pe.wait_ge(x_lo, t + 1)
                    if not early(t, 2):
                        pe.wait_ge(y_done, t - 1)
                    for k in range(KT):
                        cols = slice(k * H, (k + 1) * H)
                        if k % 2 == 0:
                            pe.wait_ge(w_lo, t * 2 + (k // 2 + 1))
                            pe.wait_ge(w_lo_g, t * 2 + (k // 2 + 1))
                        last = three_passes(nc, py[u][:], xh[u][:, k, :], xl[u][:, k, :], wh[u][:, cols], wl[u][:, cols], k == 0, k == KT - 1)
                        if k % 2:
                            last.then_inc(done, 1)

                def step(t, u, i):
                    pe.wait_ge(x_in[u], 16 * (i + 1))
                    if not early(t, 2):
                        pe.wait_ge(x_lo, t - 1)
                    for k in range(KT):
                        last = nc.tensor.transpose(px[u][:, k, :], x[u][:, k * P:(k + 1) * P], g["ident"][:])
                    last.then_inc(turned, 1)
                    if not early(t, 1):
                        product(t - 1, 1 - u)

                run_steps(pe, SLOT_TILES, 2, step)
                product(SLOT_TILES - 1, (SLOT_TILES - 1) % 2)


def collect_phase(nc, g, slot_of, y_slots):
    resid, xh, xl = g["resid"], g["xh"], g["xl"]
    with ExitStack() as ctx:
        c = Core(nc, ctx)
        y = c.sb("y_rows", [P, TT, H])
        px = [c.ps(f"y_px{n}", [P, KT, P]) for n in range(2)]
        y_in = [c.sem(f"collect_y_in{n}") for n in range(TT)]
        turned, added, x_hi, x_lo_even, x_lo_odd = (c.sem(f"collect_{n}") for n in ("turned", "added", "hi", "lo_even", "lo_odd"))

        def low_part(eng, t):
            cols = slice(t * P, (t + 1) * P)
            return eng.tensor_tensor(xl[:, :, cols], resid[:, :, cols], f32(xh[:, :, cols]), ALU.subtract)

        with nc.Block() as block:
            @block.gpsimd
            def _(pool):
                for t in range(TT):
                    nc.gpsimd.indirect_dma_start(y[:, t, :], None, y_slots, bass.IndirectOffsetOnAxis(ap=slot_of[:, t:t + 1], axis=0)).then_inc(y_in[t], 16)
                for t in range(1, TT, 2):
                    pool.wait_ge(x_hi, t + 1)
                    low_part(nc.gpsimd, t).then_inc(x_lo_odd, 1)

            @block.tensor
            def _(pe):
                for t in range(TT):
                    pe.wait_ge(y_in[t], 16)
                    if t >= 2:
                        pe.wait_ge(added, t - 1)
                    for k in range(KT):
                        last = nc.tensor.transpose(px[t % 2][:, k, :], y[:, t, k * P:(k + 1) * P], g["ident"][:])
                    last.then_inc(turned, 1)

            @block.vector
            def _(dve):
                for t in range(TT):
                    cols = slice(t * P, (t + 1) * P)
                    dve.wait_ge(turned, t + 1)
                    nc.vector.tensor_tensor(resid[:, :, cols], px[t % 2][:], resid[:, :, cols], ALU.add).then_inc(added, 1)
                    if t % 2:
                        dve.wait_ge(x_hi, t)
                        low_part(nc.vector, t - 1).then_inc(x_lo_even, 1)

            @block.scalar
            def _(act):
                for t in range(TT):
                    cols = slice(t * P, (t + 1) * P)
                    act.wait_ge(added, t + 1)
                    nc.scalar.activation(xh[:, :, cols], resid[:, :, cols], ACT.Copy).then_inc(x_hi, 1)


def low_rank_phase(nc, d, g, lr, bias, following):
    xh, xl, resid = g["xh"], g["xl"], g["resid"]
    (b_hi, b_lo), (a_hi, a_lo), (w_hi, w_lo) = (lr.parts(n) for n in range(3))
    halves = [slice(n * HALF, (n + 1) * HALF) for n in range(2)]
    LAST = (2, 3, 0, 1)
    with ExitStack() as ctx:
        c = Core(nc, ctx)
        hf = c.sb("l_hf", [P, 2, TOK])
        lh, ll = c.sb("l_h", [P, 2, TOK], F32R), c.sb("l_l", [P, 2, TOK], F32R)
        acc = c.ps("l_acc", [P, KT, TOK])
        down_sums, down_masked, down_hi, down_lo = (c.sem(f"adapter_{n}") for n in ("sums", "masked", "hi", "lo"))
        up_sums, added, x_hi, x_lo_even, x_lo_odd = (c.sem(f"layer2_{n}") for n in ("sums", "added", "hi", "lo_even", "lo_odd"))
        low_sums, low_masked, low_hi, low_lo = (c.sem(f"label_{n}") for n in ("sums", "masked", "hi", "lo"))
        out_sums, out_hi, out_lo = (c.sem(f"cond3_{n}") for n in ("sums", "hi", "lo"))

        with nc.Block() as block:
            @block.sync
            def _(sp):
                following.ahead_load(sp)

            @block.tensor
            def _(pe):
                for cols in halves:
                    for k in range(KT):
                        last = three_passes(nc, acc[:, 0, cols], b_hi[:, k, :], b_lo[:, k, :], xh[:, k, cols], xl[:, k, cols], k == 0, k == KT - 1)
                    last.then_inc(down_sums, 1)
                for n, cols in enumerate(halves):
                    pe.wait_ge(down_lo, n + 1)
                    for m in range(KT):
                        rows = slice(m * P, (m + 1) * P)
                        three_passes(nc, acc[:, m, cols], lr.fold_hi[:, rows], lr.fold_lo[:, rows], lh[:, 0, cols], ll[:, 0, cols],
                                     True, True).then_inc(up_sums, 1)
                for n, cols in enumerate(halves):
                    for j in range(2):
                        for k in range(KT):
                            pe.wait_ge(x_lo_odd if k % 2 else x_lo_even, n * 2 + k // 2 + 1)
                            last = three_passes(nc, acc[:, j, cols], a_hi[:, k, j * P:(j + 1) * P], a_lo[:, k, j * P:(j + 1) * P],
                                                xh[:, k, cols], xl[:, k, cols], k == 0, k == KT - 1)
                        last.then_inc(low_sums, 1)
                for m in LAST:
                    rows = slice(m * P, (m + 1) * P)
                    for n, cols in enumerate(halves):
                        if m < 2:
                            pe.wait_ge(low_masked, n * 2 + m + 1)
                        for k in range(KT):
                            three_passes(nc, acc[:, m, cols], w_hi[:, k, rows], w_lo[:, k, rows], xh[:, k, cols], xl[:, k, cols], k == 0, False)
                pe.wait_ge(low_lo, 4)
                for m in LAST:
                    rows = slice(m * P, (m + 1) * P)
                    for cols in halves:
                        for j in range(2):
                            last = three_passes(nc, acc[:, m, cols], w_hi[:, KT + j, rows], w_lo[:, KT + j, rows], lh[:, j, cols], ll[:, j, cols], False, j == 1)
                        last.then_inc(out_sums, 1)

            @block.vector
            def _(dve):
                def masked(j, cols, mask, n):
                    mk = mask[:, n * B // 2:(n + 1) * B // 2].rearrange("p (b o) -> p b o", o=1).to_broadcast([P, B // 2, S])
                    return nc.vector.tensor_tensor(hf[:, j, cols].rearrange("p (b s) -> p b s", s=S), acc[:, j, cols].rearrange("p (b s) -> p b s", s=S), mk, ALU.mult)

                for n, cols in enumerate(halves):
                    dve.wait_ge(down_sums, n + 1)
                    masked(0, cols, g["amask"][:], n).then_inc(down_masked, 1)
                    dve.wait_ge(down_hi, n + 1)
                    nc.vector.tensor_tensor(ll[:, 0, cols], hf[:, 0, cols], f32(lh[:, 0, cols]), ALU.subtract).then_inc(down_lo, 1)
                for n, cols in enumerate(halves):
                    def x_low(m):
                        dve.wait_ge(x_hi, n * KT + m + 1)
                        nc.vector.tensor_tensor(xl[:, m, cols], resid[:, m, cols], f32(xh[:, m, cols]), ALU.subtract).then_inc(x_lo_even, 1)

                    for m in range(KT):
                        dve.wait_ge(up_sums, n * KT + m + 1)
                        nc.vector.scalar_tensor_tensor(resid[:, m, cols], acc[:, m, cols], bias[:, m:m + 1], resid[:, m, cols], ALU.add, ALU.add).then_inc(added, 1)
                        if m % 2:
                            x_low(m - 1)
                for n, cols in enumerate(halves):
                    for j in range(2):
                        dve.wait_ge(low_sums, n * 2 + j + 1)
                        masked(j, cols, g["bmask"][:, j, :], n).then_inc(low_masked, 1)
                        dve.wait_ge(low_hi, n * 2 + j + 1)
                        nc.vector.tensor_tensor(ll[:, j, cols], hf[:, j, cols], f32(lh[:, j, cols]), ALU.subtract).then_inc(low_lo, 1)
                following.ahead_ternary(dve)
                for n in range(2 * KT):
                    m, cols = LAST[n // 2], halves[n % 2]
                    dve.wait_ge(out_hi, n + 1)
                    nc.vector.tensor_tensor(xl[:, m, cols], acc[:, m, cols], f32(xh[:, m, cols]), ALU.subtract).then_inc(out_lo, 1)

            @block.scalar
            def _(act):
                for n, cols in enumerate(halves):
                    act.wait_ge(down_masked, n + 1)
                    nc.scalar.activation(lh[:, 0, cols], hf[:, 0, cols], ACT.Copy).then_inc(down_hi, 1)
                for n, cols in enumerate(halves):
                    for m in range(KT):
                        act.wait_ge(added, n * KT + m + 1)
                        nc.scalar.activation(xh[:, m, cols], resid[:, m, cols], ACT.Copy).then_inc(x_hi, 1)
                for n, cols in enumerate(halves):
                    for j in range(2):
                        act.wait_ge(low_masked, n * 2 + j + 1)
                        nc.scalar.activation(lh[:, j, cols], hf[:, j, cols], ACT.Copy).then_inc(low_hi, 1)
                for n in range(2 * KT):
                    m, cols = LAST[n // 2], halves[n % 2]
                    act.wait_ge(out_sums, n + 1)
                    nc.scalar.activation(xh[:, m, cols], acc[:, m, cols], ACT.Copy).then_inc(out_hi, 1)

            @block.gpsimd
            def _(pool):
                for n, cols in enumerate(halves):
                    for m in (1, 3):
                        pool.wait_ge(x_hi, n * KT + m + 1)
                        nc.gpsimd.tensor_tensor(xl[:, m, cols], resid[:, m, cols], f32(xh[:, m, cols]), ALU.subtract).then_inc(x_lo_odd, 1)


def program(nc, d, out, upto=99):
    Core.used.clear()
    with ExitStack() as ctx:
        c = Core(nc, ctx)
        g = {
            "resid": c.sb("resid", [P, KT, TOK]), "xh": c.sb("xh", [P, KT, TOK], F32R), "xl": c.sb("xl", [P, KT, TOK], F32R),
            "ident": c.sb("ident_sb", [P, P]), "cols": c.sb("cols_sb", [P, 8]),
            "lens": c.sb("lens", [P, 4, B]), "vec": c.sb("vectors", [P, 2 * IT + 4 * KT]), "rows": c.sb("w3_rows", [P, IT, 3]),
            "bt": c.sb("bt_sb", [1, B * NPP], I32), "vrow": c.sb("vrow", [P, B * VCH], I32), "lmask": c.sb("lmask", [P, KT, B]), "amask": c.sb("amask", [P, B]),
            "bmask": c.sb("bmask", [P, 2, B]), 
            "scale3": c.sb("scale3", [P, 3]), "thr3": c.sb("thr3", [P, 6]),
            "kpad": nc.dram_tensor("kpad", [S, KPAD], F32).ap(),
            "qk_scr": nc.dram_tensor("qk_scr", [B, P, GROUPS, REP * S], F32).ap(),
            "v_scr": nc.dram_tensor("v_scr", [TOK, HK * D], F32).ap(),
            "o_scr": nc.dram_tensor("o_scr", [B, P, HQ * S], F32).ap(),
        }
        vec = g["vec"]
        AG, AU, AD, BIAS2, PROBS = 0, IT, 2 * IT, 2 * IT + KT, 2 * IT + 2 * KT
        xh, xl = g["xh"], g["xl"]

        def column(base):
            return lambda t: vec[:, base + t:base + t + 1] if isinstance(t, int) else vec[:, bass.ds(t + base, 1)]

        attn = ctx.enter_context(ExitStack())
        ca = Core(nc, attn)
        g["keyidx"] = ca.sb("keyidx_sb", [P, KEYS])
        rope = ca.sb("rope", [P, 2, 2, TT, D])
        g["rope_c"], g["rope_s"] = rope[:, 0], rope[:, 1]
        front = ctx.enter_context(ExitStack())
        cf_ = Core(nc, front)
        for name, shape, dt in (("ints", [P, 4, B], I32), ("posi", [P, TT], I32), ("spos", [P, TT], F32), ("posf", [P, TT], F32),
                                ("invf", [P, D // 2], F32), ("nw", [P, 2, D], F32), ("vpage", [P, B * VCH], I32), ("vpf", [P, B * VCH], F32),
                                ("fr", [P, 2, TT, D // 2], F32), ("fk", [P, 2, TT, D // 2], F32)):
            g[name] = cf_.sb("b_" + name, shape, dt)
        gu_slots = WeightSlots(cf_, "gu0", 2 * H)
        conv_input = front.enter_context(ExitStack())
        cx = Core(nc, conv_input)
        g["xr"], g["xr_in"], g["xr_zeroed"] = cx.sb("xr", [P, S, KT - 1 + KT, B]), cx.sem("xr_in"), cx.sem("xr_zeroed")
        setup_phase(nc, d, g)
        if upto > 0:
            with ExitStack() as inner:
                ci = Core(nc, inner)
                w_gu = WeightStream(nc, cf_, "gu0", gu_slots, d["w0_gu"], 2 * H, IT, 2)
                conv_phase(nc, d, g, w_gu)
                conv_input.close()
                hh, hl = ci.sb("hh", [P, IT, TOK], F32R), ci.sb("hl", [P, IT, TOK], F32R)
                w_down = WeightStream(nc, ci, "d0", WeightSlots(ci, "d0", H), d["w0_d"], H, IT, 2)
                gate_up_phase(nc, d, g, hh, hl, "f0", w_gu, ACT.Silu, column(AG), column(AU), w_down,
                              gate_room=rope[:].rearrange("p c a t d -> p (c a t d)"),
                              vector_first=lambda chain: rotary_angles(nc, d, g, chain),
                              scalar_last=lambda: nc.scalar.activation(g["fk"][:], g["fr"][:], ACT.Sin))

                W = KT * P
                w3_gu = [gu_slots.all_raw[:, n * 2 * W:(n + 1) * 2 * W] for n in range(2)]
                w3_d = ci.sb("w3_down", [P, W])
                w3_in, w3_d_in, w3_sums = [ci.sem(f"w3_in{n}") for n in range(2)], ci.sem("w3_d_in"), ci.sem("w3_sums")
                w3_gate = ci.sem("w3_gate")

                def load_w3(sp, t, u, i, made):
                    sp.dma_start(w3_gu[u], d["w3_gu"][at(t)].rearrange("o p m -> (o p) m")).then_inc(w3_in[u], 16)
                    if not early(t, 1):
                        sp.wait_ge(w3_sums, t)
                    sp.dma_start(w3_d[:], d["w3_d"][at(t)].rearrange("o p m -> (o p) m")).then_inc(w3_d_in, 16)

                def sum_w3(dve, t, u, i):
                    dve.wait_ge(w3_in[u], (i + 1) * 16)
                    dve.wait_ge(w3_d_in, t * 16 + 16)
                    dve.sem_inc(w3_gate, 1)
                    rows = g["rows"][:, at(t), :].rearrange("p o n -> p (o n)")
                    nc.vector.tensor_reduce(rows[:, 0:2], w3_gu[u].rearrange("p (n w) -> p n w", n=2),
                                            axis=AX_X, op=ALU.add, apply_absolute_value=True)
                    nc.vector.tensor_reduce(rows[:, 2:3], w3_d[:].rearrange("p (n w) -> p n w", n=1),
                                            axis=AX_X, op=ALU.add, apply_absolute_value=True).then_inc(w3_sums, 1)

                accumulate_phase(nc, d, g, "d0", w_down, resident(hh, hl), onto_residual(nc, g, lambda m: vec[:, AD + m:AD + m + 1], batch_major=False),
                                 vector_first=lambda chain: rotary_tables(nc, d, g, chain), load_extra=load_w3, side=sum_w3)
            front.close()
        if upto > 1:
            cache = CacheLoads(nc, ca, d, g)
            project_phase(nc, d, g, cache)
            attention_phase(nc, d, g, cache)
        attn.close()
        old = range(min(Core.used), max(Core.used) + 1)
        thr, sc3 = g["thr3"], g["scale3"]
        slots = WeightSlots(c, "slots", H)
        w_gu3 = WeightStream(nc, c, "gu3", WeightSlots(c, "gu3", 2 * H, ternary_only=True), d["w3_gu"], 2 * H, IT, 2,
                             thresholds=[(thr[:, n:n + 1], thr[:, 3 + n:4 + n]) for n in range(2)])
        x_slots = nc.dram_tensor("x_slots", [SLOT_TILES * P, H], F32).ap()
        y_slots = nc.dram_tensor("y_slots", [SLOT_TILES * P, H], F32).ap()
        with ExitStack() as low:
            ck = Core(nc, low)
            lr = LowRankWeights(nc, ck)
            slot_of, tile_expert = ck.sb("slot_of", [P, TT], I32), ck.sb("tile_expert", [1, SLOT_TILES], I32)
            with ExitStack() as tokens:
                xt = Core(nc, tokens).sb("x_tokens", [P, TT, H])
                output_projection(nc, d, g, WeightStream(nc, ck, "wo", slots, d["w1_o"], H, HQ, 2 * REP), xt)
                route_phase(nc, d, g, xt, slot_of, tile_expert, x_slots, lr, vec[:, PROBS:PROBS + 2], old)
            expert_phase(nc, d, g, slots, tile_expert, x_slots, y_slots)
            collect_phase(nc, g, slot_of, y_slots)
            low_rank_phase(nc, d, g, lr, vec[:, BIAS2:BIAS2 + KT], w_gu3)
        with ExitStack() as inner:
            ci = Core(nc, inner)
            hh, hl = ci.sb("hh3", [P, IT, TOK], F32R), ci.sb("hl3", [P, IT, TOK], F32R)
            gate_room = ci.sb("gate_room", [P, 3 * TOK])
            w_down3 = WeightStream(nc, ci, "d3", slots, d["w3_d"], H, IT, 2, thresholds=[(thr[:, 2:3], thr[:, 5:6])])
            gate_up_phase(nc, d, g, hh, hl, "f3", w_gu3, ACT.Copy, lambda t: sc3[:, 0:1], lambda t: sc3[:, 1:2], w_down3, gate_room[:])
            accumulate_phase(nc, d, g, "d3", w_down3, resident(hh, hl), onto_residual(nc, g, lambda m: sc3[:, 2:3], split=False),
                             store=lambda sp, m: sp.dma_start(out[:, m, :], g["resid"][:, m, :]))


def tiles_of(w, k_tiles, cols):
    full = np.zeros((k_tiles * P, cols), np.float32)
    full[:w.shape[0], :w.shape[1]] = w
    return full.reshape(k_tiles, P, cols)


def on_partitions(w, k_tiles):
    return w.reshape(k_tiles, P, -1).transpose(1, 0, 2)


def gate_up_tiles(wg, wu):
    both = np.stack([tiles_of(w.T, KT, IT * P) for w in (wg, wu)])
    return np.ascontiguousarray(both.reshape(2, KT, P, IT, P).transpose(3, 2, 0, 1, 4)).reshape(IT, P, 2 * KT * P)


def vector_columns(v, tiles):
    full = np.zeros(tiles * P, np.float32)
    full[:v.shape[0]] = v
    return full.reshape(tiles, P).T


def layouts(i):
    i = {k: np.asarray(v) for k, v in i.items()}
    a = {k: i[k] for k in ("itok_B_78_3631", "itok_B_207_1644", "itok_B_3_7", "itok_B_0_4", "itok_Bx16_0_63", "L0_cond_log_dt", "L0_cond_D",
                           "L1_cond_q_norm_w", "L1_cond_k_norm_w", "L1_ffn_gate_b", "L1_ffn_expert_b")}
    x = i["x"]
    a["xT"] = x.transpose(2, 0, 1).reshape(KT, P, TOK).transpose(1, 0, 2)
    a["x_rev"] = x.transpose(2, 1, 0).reshape(KT, P, S, B)[:, ::-1].transpose(1, 2, 0, 3)
    for name, w in (("logA2", i["L0_cond_log_A_real"]), ("Aim2", i["L0_cond_A_imag"]), ("Cre2", i["L0_cond_C"][..., 0]), ("Cim2", i["L0_cond_C"][..., 1])):
        a[name] = np.concatenate([w.T, w.T])
    W = REP * D
    wq = i["L1_cond_Wq"].T.reshape(KT, P, HQ * D // W, W).transpose(2, 1, 0, 3)
    wk = i["L1_cond_Wk"].T.reshape(KT, P, HK * D // W, W).transpose(2, 1, 0, 3)
    wv = i["L1_cond_Wv"].T.reshape(KT, P, HK * D // W, W).transpose(2, 1, 0, 3)
    a["w1_qkv"] = np.concatenate([wq, wk, wv]).reshape(-1, P, KT * W)
    a["kT_pages"] = i["L1_cond_k_cache"].transpose(0, 3, 2, 1).reshape(PAGES, P, HK * PSIZE)
    a["v_rows"] = i["L1_cond_v_cache"].reshape(PAGES * PSIZE, HK * D)
    a["vpages"] = i["itok_Bx16_0_63"].reshape(B, VCH, NPP // VCH).transpose(2, 0, 1).reshape(NPP // VCH, B * VCH)
    a["w1_o"] = i["L1_cond_Wo"].T.reshape(HQ, P, H)
    a["w1_gate"] = i["L1_ffn_gate_w"].T.reshape(KT, P, EXPERTS).transpose(1, 0, 2)
    a["w1_e"] = i["L1_ffn_expert_w"].transpose(0, 2, 1).reshape(EXPERTS, KT, P, H).transpose(0, 2, 1, 3).reshape(EXPERTS, P, KT * H)
    a["w0_gu"] = gate_up_tiles(i["L0_ffn_Wg"], i["L0_ffn_Wu"])
    a["w0_d"] = tiles_of(i["L0_ffn_Wd"].T, IT, H)
    a["w3_gu"] = gate_up_tiles(i["L3_ffn_w_gate"], i["L3_ffn_w_up"])
    a["w3_d"] = tiles_of(i["L3_ffn_w_down"].T, IT, H)
    a["vectors"] = np.concatenate([vector_columns(i["L0_ffn_ag"], IT), vector_columns(i["L0_ffn_au"], IT), vector_columns(i["L0_ffn_ad"], KT),
                                   vector_columns(i["L2_ffn_b"], KT), vector_columns(np.repeat(i["L2_ffn_probs"], 16), 2)], axis=1)
    a["w2_b"] = on_partitions(i["L2_cond_B"].reshape(ADAPTERS * RANK2, H).T, KT)
    a["w2_a"] = on_partitions(i["L2_cond_A"].transpose(1, 0, 2).reshape(H, ADAPTERS * RANK2), KT)
    a["w2_fa"] = on_partitions(i["L2_ffn_A"].reshape(-1, H).T, KT)
    a["w2_wb"] = on_partitions(np.concatenate([i["L2_ffn_W"].T, i["L2_ffn_B"].transpose(0, 2, 1).reshape(-1, H)]), KT + 2)
    a["w3_la"] = tiles_of(i["L3_cond_lora_A"].transpose(1, 0, 2).reshape(H, LABELS * RANK3), KT, 2 * P).transpose(1, 0, 2)
    low = np.concatenate([i["L3_cond_lora_B_w"].T] * LABELS)
    a["w3_wb"] = on_partitions(np.concatenate([i["L3_cond_weight"].T, low, np.zeros((2 * P - LABELS * RANK3, H), np.float32)]), KT + 2)

    row = np.arange(P)
    a["posbase"] = np.repeat(i["itok_B_207_1644"], S).reshape(TT, P).T
    a["seqpos"] = np.tile((row % S).astype(np.float32)[:, None], (1, TT))
    a["inv_freq"] = np.tile((1.0 / THETA ** (np.arange(0, D, 2, dtype=np.float32) / D)).astype(np.float32), (P, 1))
    upper = row < P // 2
    a["signs"] = np.stack([np.where(upper, 2.0, 0.0), np.where(upper, 0.0, -2.0), np.where(upper, -2.0, 0.0), np.where(upper, 0.0, -2.0)], 1).astype(np.float32)
    a["positions"] = np.tile(np.concatenate([np.arange(LO_N), LO_N * np.arange(HI_N)]).astype(np.float32), (P, 1))
    a["ident"] = np.eye(P, dtype=np.float32)
    a["keyidx"] = np.tile(np.concatenate([np.arange(CACHE), -np.ones(S)]).astype(np.float32), (P, 1))
    cols = np.zeros((P, 8), np.float32)
    for m in range(KT):
        cols[:, m] = m * P + row
    cols[:, 4] = row // RANK2
    cols[:, 5], cols[:, 6] = row // RANK3, (P + row) // RANK3
    cols[:, 7] = row % PSIZE
    a["cols"] = cols
    a["before"] = (row[:, None] < row[None, :]).astype(np.float32)
    a["tile_no"] = np.tile(np.arange(SLOT_TILES, dtype=np.float32), (P, 1))
    return {k: np.ascontiguousarray(v) for k, v in a.items()}


def kernel(**inputs):
    import concourse.bacc as bacc
    from concourse.bass_utils import run_bass_kernel_spmd

    nc = bacc.Bacc("TRN2", target_bir_lowering=False, num_devices=1)
    arrays, d = {}, {}
    for name, a in layouts(inputs).items():
        arrays[f"in_{name}"] = a
        d[name] = nc.dram_tensor(f"in_{name}", a.shape, mybir.dt.from_np(a.dtype), kind="ExternalInput").ap()
    out = nc.dram_tensor("out_x", [P, KT, TOK], F32, kind="ExternalOutput").ap()
    program(nc, d, out)
    r = run_bass_kernel_spmd(nc, [arrays], core_ids=[0])
    got = r.results[0]["out_x"]
    return np.ascontiguousarray(got.reshape(P, KT, B, S).transpose(2, 3, 1, 0).reshape(B, S, H))
```
